# Optimizing a Trainium2 kernel written in Bass

```python
import numpy as np
import jax
import jax.numpy as jnp

def _softmax(x, axis=-1):
    return jax.nn.softmax(x, axis=axis)

def _gelu(x):
    return jax.nn.gelu(x, approximate=True)

def _silu(x):
    return jax.nn.silu(x)

def _sigmoid(x):
    return jax.nn.sigmoid(x)

def _layernorm(x, axis=-1, eps=1e-05):
    m = jnp.mean(x, axis=axis, keepdims=True)
    v = jnp.var(x, axis=axis, keepdims=True)
    return (x - m) / jnp.sqrt(v + eps)

def _scatter_add(tgt, idx, src, axis=0):
    return tgt.at[idx].add(src)

def _segment_sum(src, seg, n):
    return jax.ops.segment_sum(src, seg, n)
kernel_name = 'mk_adaln_d2_jaxref_r8_3f74da'

def setup_inputs(seed: int=0):
    np.random.seed(seed)
    _w = jnp.asarray

    def _L0_attn_setup():
        import jax, jax.numpy as jnp
        import numpy as np
        D_MODEL = 128
        NHEAD = 16
        D_K = D_MODEL // NHEAD
        MAX_REL = 128
        key = jax.random.key(seed)
        ks = jax.random.split(key, 6)
        B, S = (4, 256)
        s = 1.0 / np.sqrt(D_MODEL)
        x = jax.random.normal(ks[0], (B, S, D_MODEL), dtype=jnp.float32)
        W_qkv = jax.random.normal(ks[1], (D_MODEL, 3 * D_MODEL), dtype=jnp.float32) * s
        b_qkv = jnp.zeros((3 * D_MODEL,), dtype=jnp.float32)
        W_out = jax.random.normal(ks[2], (D_MODEL, D_MODEL), dtype=jnp.float32) * s
        b_out = jnp.zeros((D_MODEL,), dtype=jnp.float32)
        rel_bias = jax.random.normal(ks[3], (2 * MAX_REL + 1, NHEAD), dtype=jnp.float32) * 0.02
        return {'x': x, 'W_qkv': W_qkv, 'b_qkv': b_qkv, 'W_out': W_out, 'b_out': b_out, 'rel_bias': rel_bias}
    _L0_attn_in = _L0_attn_setup()

    def _L0_ffn_setup():
        import jax, jax.numpy as jnp
        import numpy as np
        D_MODEL = 128
        HIDDEN = 512
        NUM_EXPERTS = 8
        TOP_K = 2
        NUM_SHARED = 2

        def _gelu(x):
            return jax.nn.gelu(x, approximate=False)
        key = jax.random.key(seed)
        ks = jax.random.split(key, 12)
        s = 0.02
        return {'x': jax.random.normal(ks[0], (2, 256, D_MODEL), dtype=jnp.float32), 'rW': jax.random.normal(ks[1], (D_MODEL, NUM_EXPERTS), dtype=jnp.float32) * s, 'rb': jnp.zeros((NUM_EXPERTS,), dtype=jnp.float32), 'W1': jax.random.normal(ks[2], (NUM_EXPERTS, D_MODEL, HIDDEN), dtype=jnp.float32) * s, 'b1': jnp.zeros((NUM_EXPERTS, HIDDEN), dtype=jnp.float32), 'W2': jax.random.normal(ks[3], (NUM_EXPERTS, HIDDEN, D_MODEL), dtype=jnp.float32) * s, 'b2': jnp.zeros((NUM_EXPERTS, D_MODEL), dtype=jnp.float32), 'sW1': jax.random.normal(ks[4], (NUM_SHARED, D_MODEL, HIDDEN), dtype=jnp.float32) * s, 'sb1': jnp.zeros((NUM_SHARED, HIDDEN), dtype=jnp.float32), 'sW2': jax.random.normal(ks[5], (NUM_SHARED, HIDDEN, D_MODEL), dtype=jnp.float32) * s, 'sb2': jnp.zeros((NUM_SHARED, D_MODEL), dtype=jnp.float32)}
    _L0_ffn_in = _L0_ffn_setup()
    _L0_c = _w((lambda *s: np.random.randn(*s).astype(np.float32) * 0.05)(1, 128))
    _L0_wmod = _w((lambda *s: np.random.randn(*s).astype(np.float32) * 0.05)(128, 6 * 128) * 128 ** (-0.5))

    def _L1_attn_setup():
        import jax, jax.numpy as jnp
        import numpy as np
        D_MODEL = 128
        N_HEADS = 16
        HEAD_DIM = D_MODEL // N_HEADS
        D_LATENT = 32
        LAMBDA_DECAY = 0.01
        TIME_STEP = 0.01
        CLAMP = 10000.0

        def _reference_tuple_inner(x, Wq, Wk, Wv, Wo, W_down_kv, W_up_k, W_up_v):
            B, S, _ = x.shape
            q = x @ Wq
            k = x @ Wk
            v = x @ Wv
            latent_kv = (k + v) @ W_down_kv
            k_rec = latent_kv @ W_up_k
            v_rec = latent_kv @ W_up_v

            def heads(t):
                return t.reshape(B, S, N_HEADS, HEAD_DIM).transpose(0, 2, 1, 3)
            qh, kh, vh = (heads(q), heads(k_rec), heads(v_rec))
            scale = 1.0 / (jnp.sqrt(jnp.float32(D_MODEL)) + 1e-08)
            scores = jnp.einsum('bhqd,bhkd->bhqk', qh, kh) * scale
            scores = jnp.clip(jnp.nan_to_num(scores, nan=-1000000000.0), -CLAMP, CLAMP)
            idx = jnp.arange(S, dtype=jnp.float32)
            decay = jnp.exp(-LAMBDA_DECAY * TIME_STEP * jnp.abs(idx[:, None] - idx[None, :]))
            scores = scores * decay[None, None, :, :]
            scores = jnp.clip(jnp.nan_to_num(scores, nan=-1000000000.0), -CLAMP, CLAMP)
            attn = jax.nn.softmax(scores, axis=-1)
            out = jnp.einsum('bhqk,bhkd->bhqd', attn, vh)
            out = out.transpose(0, 2, 1, 3).reshape(B, S, D_MODEL)
            return (out @ Wo, latent_kv)
        key = jax.random.key(seed)
        ks = jax.random.split(key, 8)
        B, S = (2, 256)

        def w(k, i, o):
            return jax.random.normal(k, (i, o), dtype=jnp.float32) * 0.02
        return {'x': jax.random.normal(ks[0], (B, S, D_MODEL), dtype=jnp.float32), 'Wq': w(ks[1], D_MODEL, D_MODEL), 'Wk': w(ks[2], D_MODEL, D_MODEL), 'Wv': w(ks[3], D_MODEL, D_MODEL), 'Wo': w(ks[4], D_MODEL, D_MODEL), 'W_down_kv': w(ks[5], D_MODEL, D_LATENT), 'W_up_k': w(ks[6], D_LATENT, D_MODEL), 'W_up_v': w(ks[7], D_LATENT, D_MODEL)}
    _L1_attn_in = _L1_attn_setup()

    def _L1_ffn_setup():
        import jax, jax.numpy as jnp
        import numpy as np
        B, S, D, H, M, E, K = (8, 256, 128, 256, 64, 8, 2)
        EH = H // 2

        def _layernorm(x, g, b, eps=1e-05):
            mu = jnp.mean(x, axis=-1, keepdims=True)
            var = jnp.var(x, axis=-1, keepdims=True)
            return (x - mu) * jax.lax.rsqrt(var + eps) * g + b
        key = jax.random.key(seed)
        ks = jax.random.split(key, 16)
        sc = lambda *shape: 1.0 / np.sqrt(shape[0])
        return {'inputs_embeds': jax.random.normal(ks[0], (B, S, D), jnp.float32), 'W_enc': jax.random.normal(ks[1], (D, H), jnp.float32) * sc(D), 'b_enc': jnp.zeros((H,), jnp.float32), 'W_s2c': jax.random.normal(ks[2], (H, M), jnp.float32) * sc(H), 'b_s2c': jnp.zeros((M,), jnp.float32), 'Wr': jax.random.normal(ks[3], (M, E), jnp.float32) * sc(M), 'br': jnp.zeros((E,), jnp.float32), 'W1': jax.random.normal(ks[4], (E, M, EH), jnp.float32) * sc(M), 'b1': jnp.zeros((E, EH), jnp.float32), 'W2': jax.random.normal(ks[5], (E, EH, M), jnp.float32) * sc(EH), 'b2': jnp.zeros((E, M), jnp.float32), 'W_c2s': jax.random.normal(ks[6], (M, H), jnp.float32) * sc(M), 'b_c2s': jnp.zeros((H,), jnp.float32), 'W_dec': jax.random.normal(ks[7], (H, D), jnp.float32) * sc(H), 'b_dec': jnp.zeros((D,), jnp.float32), 'ln_g': jnp.ones((D,), jnp.float32), 'ln_b': jnp.zeros((D,), jnp.float32)}
    _L1_ffn_in = _L1_ffn_setup()
    _L1_c = _w((lambda *s: np.random.randn(*s).astype(np.float32) * 0.05)(1, 128))
    _L1_wmod = _w((lambda *s: np.random.randn(*s).astype(np.float32) * 0.05)(128, 6 * 128) * 128 ** (-0.5))
    _d = {'L0_attn_x': _L0_attn_in['x'], 'L0_attn_W_qkv': _L0_attn_in['W_qkv'], 'L0_attn_b_qkv': _L0_attn_in['b_qkv'], 'L0_attn_W_out': _L0_attn_in['W_out'], 'L0_attn_b_out': _L0_attn_in['b_out'], 'L0_attn_rel_bias': _L0_attn_in['rel_bias'], 'L0_ffn_rW': _L0_ffn_in['rW'], 'L0_ffn_rb': _L0_ffn_in['rb'], 'L0_ffn_W1': _L0_ffn_in['W1'], 'L0_ffn_b1': _L0_ffn_in['b1'], 'L0_ffn_W2': _L0_ffn_in['W2'], 'L0_ffn_b2': _L0_ffn_in['b2'], 'L0_ffn_sW1': _L0_ffn_in['sW1'], 'L0_ffn_sb1': _L0_ffn_in['sb1'], 'L0_ffn_sW2': _L0_ffn_in['sW2'], 'L0_ffn_sb2': _L0_ffn_in['sb2'], 'L0_c': _L0_c, 'L0_wmod': _L0_wmod, 'L1_attn_Wq': _L1_attn_in['Wq'], 'L1_attn_Wk': _L1_attn_in['Wk'], 'L1_attn_Wv': _L1_attn_in['Wv'], 'L1_attn_Wo': _L1_attn_in['Wo'], 'L1_attn_W_down_kv': _L1_attn_in['W_down_kv'], 'L1_attn_W_up_k': _L1_attn_in['W_up_k'], 'L1_attn_W_up_v': _L1_attn_in['W_up_v'], 'L1_ffn_W_enc': _L1_ffn_in['W_enc'], 'L1_ffn_b_enc': _L1_ffn_in['b_enc'], 'L1_ffn_W_s2c': _L1_ffn_in['W_s2c'], 'L1_ffn_b_s2c': _L1_ffn_in['b_s2c'], 'L1_ffn_Wr': _L1_ffn_in['Wr'], 'L1_ffn_br': _L1_ffn_in['br'], 'L1_ffn_W1': _L1_ffn_in['W1'], 'L1_ffn_b1': _L1_ffn_in['b1'], 'L1_ffn_W2': _L1_ffn_in['W2'], 'L1_ffn_b2': _L1_ffn_in['b2'], 'L1_ffn_W_c2s': _L1_ffn_in['W_c2s'], 'L1_ffn_b_c2s': _L1_ffn_in['b_c2s'], 'L1_ffn_W_dec': _L1_ffn_in['W_dec'], 'L1_ffn_b_dec': _L1_ffn_in['b_dec'], 'L1_ffn_ln_g': _L1_ffn_in['ln_g'], 'L1_ffn_ln_b': _L1_ffn_in['ln_b'], 'L1_c': _L1_c, 'L1_wmod': _L1_wmod}
    _x0 = _d['L0_attn_x']
    _d['L0_attn_x'] = jax.random.normal(jax.random.fold_in(jax.random.key(seed), 1), (1, 2048, 128), dtype=_x0.dtype)
    del _x0
    return _d

def reference(L0_attn_x, L0_attn_W_qkv, L0_attn_b_qkv, L0_attn_W_out, L0_attn_b_out, L0_attn_rel_bias, L0_ffn_rW, L0_ffn_rb, L0_ffn_W1, L0_ffn_b1, L0_ffn_W2, L0_ffn_b2, L0_ffn_sW1, L0_ffn_sb1, L0_ffn_sW2, L0_ffn_sb2, L0_c, L0_wmod, L1_attn_Wq, L1_attn_Wk, L1_attn_Wv, L1_attn_Wo, L1_attn_W_down_kv, L1_attn_W_up_k, L1_attn_W_up_v, L1_ffn_W_enc, L1_ffn_b_enc, L1_ffn_W_s2c, L1_ffn_b_s2c, L1_ffn_Wr, L1_ffn_br, L1_ffn_W1, L1_ffn_b1, L1_ffn_W2, L1_ffn_b2, L1_ffn_W_c2s, L1_ffn_b_c2s, L1_ffn_W_dec, L1_ffn_b_dec, L1_ffn_ln_g, L1_ffn_ln_b, L1_c, L1_wmod):

    def _L0_attn_ref(x, W_qkv, b_qkv, W_out, b_out, rel_bias):
        import jax, jax.numpy as jnp
        import numpy as np
        D_MODEL = 128
        NHEAD = 16
        D_K = D_MODEL // NHEAD
        MAX_REL = 128
        B, S, D = x.shape
        qkv = x @ W_qkv + b_qkv
        qkv = qkv.reshape(B, S, 3, NHEAD, D_K)
        q, k, v = (qkv[:, :, 0], qkv[:, :, 1], qkv[:, :, 2])
        scores = jnp.einsum('bihd,bjhd->bhij', q, k) / jnp.sqrt(jnp.float32(D_K))
        idxs = jnp.arange(S)
        rel = jnp.clip(idxs[:, None] - idxs[None, :] + MAX_REL, 0, 2 * MAX_REL)
        bias = rel_bias[rel]
        scores = scores + jnp.transpose(bias, (2, 0, 1))[None]
        attn = jax.nn.softmax(scores, axis=-1)
        out = jnp.einsum('bhij,bjhd->bihd', attn, v).reshape(B, S, D)
        return out @ W_out + b_out

    def _L0_ffn_ref(x, rW, rb, W1, b1, W2, b2, sW1, sb1, sW2, sb2):
        import jax, jax.numpy as jnp
        import numpy as np
        D_MODEL = 128
        HIDDEN = 512
        NUM_EXPERTS = 8
        TOP_K = 2
        NUM_SHARED = 2

        def _gelu(x):
            return jax.nn.gelu(x, approximate=False)
        B, L, D = x.shape
        xf = x.reshape(-1, D)
        sh = _gelu(jnp.einsum('td,sdh->sth', xf, sW1) + sb1[:, None, :])
        shared = jnp.einsum('sth,shd->std', sh, sW2) + sb2[:, None, :]
        shared = shared.mean(axis=0)
        gates = xf @ rW + rb
        topk_vals, topk_idx = jax.lax.top_k(gates, TOP_K)
        topk_probs = jax.nn.softmax(topk_vals, axis=-1)
        onehot = topk_idx[:, :, None] == jnp.arange(NUM_EXPERTS)[None, None, :]
        w = jnp.sum(topk_probs[:, :, None] * onehot, axis=1)
        h = _gelu(jnp.einsum('td,edh->eth', xf, W1) + b1[:, None, :])
        y = jnp.einsum('eth,ehd->etd', h, W2) + b2[:, None, :]
        moe = jnp.einsum('te,etd->td', w, y)
        return (shared + moe).reshape(B, L, D)

    def _L1_attn_ref(x, Wq, Wk, Wv, Wo, W_down_kv, W_up_k, W_up_v):
        import jax, jax.numpy as jnp
        import numpy as np
        D_MODEL = 128
        N_HEADS = 16
        HEAD_DIM = D_MODEL // N_HEADS
        D_LATENT = 32
        LAMBDA_DECAY = 0.01
        TIME_STEP = 0.01
        CLAMP = 10000.0

        def _reference_tuple_inner(x, Wq, Wk, Wv, Wo, W_down_kv, W_up_k, W_up_v):
            B, S, _ = x.shape
            q = x @ Wq
            k = x @ Wk
            v = x @ Wv
            latent_kv = (k + v) @ W_down_kv
            k_rec = latent_kv @ W_up_k
            v_rec = latent_kv @ W_up_v

            def heads(t):
                return t.reshape(B, S, N_HEADS, HEAD_DIM).transpose(0, 2, 1, 3)
            qh, kh, vh = (heads(q), heads(k_rec), heads(v_rec))
            scale = 1.0 / (jnp.sqrt(jnp.float32(D_MODEL)) + 1e-08)
            scores = jnp.einsum('bhqd,bhkd->bhqk', qh, kh) * scale
            scores = jnp.clip(jnp.nan_to_num(scores, nan=-1000000000.0), -CLAMP, CLAMP)
            idx = jnp.arange(S, dtype=jnp.float32)
            decay = jnp.exp(-LAMBDA_DECAY * TIME_STEP * jnp.abs(idx[:, None] - idx[None, :]))
            scores = scores * decay[None, None, :, :]
            scores = jnp.clip(jnp.nan_to_num(scores, nan=-1000000000.0), -CLAMP, CLAMP)
            attn = jax.nn.softmax(scores, axis=-1)
            out = jnp.einsum('bhqk,bhkd->bhqd', attn, vh)
            out = out.transpose(0, 2, 1, 3).reshape(B, S, D_MODEL)
            return (out @ Wo, latent_kv)
        return _reference_tuple_inner(x, Wq, Wk, Wv, Wo, W_down_kv, W_up_k, W_up_v)[0]

    def _L1_ffn_ref(inputs_embeds, W_enc, b_enc, W_s2c, b_s2c, Wr, br, W1, b1, W2, b2, W_c2s, b_c2s, W_dec, b_dec, ln_g, ln_b):
        import jax, jax.numpy as jnp
        import numpy as np
        B, S, D, H, M, E, K = (8, 256, 128, 256, 64, 8, 2)
        EH = H // 2

        def _layernorm(x, g, b, eps=1e-05):
            mu = jnp.mean(x, axis=-1, keepdims=True)
            var = jnp.var(x, axis=-1, keepdims=True)
            return (x - mu) * jax.lax.rsqrt(var + eps) * g + b
        b, s, d = inputs_embeds.shape
        spikes_enc = jax.nn.sigmoid(inputs_embeds @ W_enc + b_enc)
        flat = spikes_enc.reshape(b * s, -1)
        cont = flat @ W_s2c + b_s2c
        probs = jax.nn.softmax(cont @ Wr + br, axis=-1)
        topk_w, topk_idx = jax.lax.top_k(probs, K)
        topk_w = topk_w / jnp.sum(topk_w, axis=-1, keepdims=True)
        gate = jnp.sum(jax.nn.one_hot(topk_idx, E, dtype=cont.dtype) * topk_w[..., None], axis=1)
        h = jax.nn.relu(jnp.einsum('tm,emh->eth', cont, W1) + b1[:, None, :])
        y = jnp.einsum('eth,ehm->etm', h, W2) + b2[:, None, :]
        expert_out = jnp.einsum('etm,te->tm', y, gate)
        spikes_moe = jax.nn.sigmoid(expert_out @ W_c2s + b_c2s)
        spikes_moe = spikes_moe.reshape(b, s, -1)
        decoded = spikes_moe @ W_dec + b_dec
        return _layernorm(decoded, ln_g, ln_b)
    x = L0_attn_x
    mod = (_silu(L0_c) @ L0_wmod).reshape(L0_c.shape[0], 6, 1, -1)
    sa, ca, ga, sb, cb, gb = (mod[:, 0], mod[:, 1], mod[:, 2], mod[:, 3], mod[:, 4], mod[:, 5])
    ga = (2 * (ga >= 0) - 1) * jnp.maximum(jnp.abs(ga), 0.25)
    gb = (2 * (gb >= 0) - 1) * jnp.maximum(jnp.abs(gb), 0.25)
    h = _layernorm(x, axis=-1) * (1 + ca) + sa
    x = x + ga * _L0_attn_ref(h, L0_attn_W_qkv, L0_attn_b_qkv, L0_attn_W_out, L0_attn_b_out, L0_attn_rel_bias)
    h = _layernorm(x, axis=-1) * (1 + cb) + sb
    x = x + gb * _L0_ffn_ref(h, L0_ffn_rW, L0_ffn_rb, L0_ffn_W1, L0_ffn_b1, L0_ffn_W2, L0_ffn_b2, L0_ffn_sW1, L0_ffn_sb1, L0_ffn_sW2, L0_ffn_sb2)
    mod = (_silu(L1_c) @ L1_wmod).reshape(L1_c.shape[0], 6, 1, -1)
    sa, ca, ga, sb, cb, gb = (mod[:, 0], mod[:, 1], mod[:, 2], mod[:, 3], mod[:, 4], mod[:, 5])
    ga = (2 * (ga >= 0) - 1) * jnp.maximum(jnp.abs(ga), 0.25)
    gb = (2 * (gb >= 0) - 1) * jnp.maximum(jnp.abs(gb), 0.25)
    h = _layernorm(x, axis=-1) * (1 + ca) + sa
    x = x + ga * _L1_attn_ref(h, L1_attn_Wq, L1_attn_Wk, L1_attn_Wv, L1_attn_Wo, L1_attn_W_down_kv, L1_attn_W_up_k, L1_attn_W_up_v)
    h = _layernorm(x, axis=-1) * (1 + cb) + sb
    x = x + gb * _L1_ffn_ref(h, L1_ffn_W_enc, L1_ffn_b_enc, L1_ffn_W_s2c, L1_ffn_b_s2c, L1_ffn_Wr, L1_ffn_br, L1_ffn_W1, L1_ffn_b1, L1_ffn_W2, L1_ffn_b2, L1_ffn_W_c2s, L1_ffn_b_c2s, L1_ffn_W_dec, L1_ffn_b_dec, L1_ffn_ln_g, L1_ffn_ln_b)
    return x

_drawn_inputs = setup_inputs


def setup_inputs(seed=0):
    import zlib

    import numpy as np

    out = dict(_drawn_inputs(seed))
    spreads = {'L0_attn_b_qkv': (0.0, 0.311),
     'L0_attn_b_out': (0.0, 0.338),
     'L0_ffn_rb': (0.0, 0.693),
     'L0_ffn_b1': (0.0, 0.8),
     'L0_ffn_b2': (0.0, 0.47),
     'L0_ffn_sb1': (0.0, 0.8),
     'L0_ffn_sb2': (0.0, 0.45),
     'L1_ffn_b_enc': (0.0, 2.0),
     'L1_ffn_b_s2c': (0.0, 0.502),
     'L1_ffn_br': (0.0, 0.572),
     'L1_ffn_b1': (0.0, 2.0),
     'L1_ffn_b2': (0.0, 2.0),
     'L1_ffn_b_c2s': (0.0, 0.736),
     'L1_ffn_b_dec': (0.0, 0.273),
     'L1_ffn_ln_g': (1.0, 0.2),
     'L1_ffn_ln_b': (0.0, 0.317)}
    factors = {'L0_attn_rel_bias': 64.0,
     'L0_ffn_rW': 3.342,
     'L0_ffn_W1': 5.985,
     'L0_ffn_W2': 5.466,
     'L0_ffn_sW1': 5.998,
     'L0_ffn_sW2': 5.449,
     'L1_attn_Wq': 8.0,
     'L1_attn_Wk': 8.0,
     'L1_attn_Wv': 8.0,
     'L1_attn_Wo': 8.0,
     'L1_attn_W_down_kv': 8.0,
     'L1_attn_W_up_k': 8.0,
     'L1_attn_W_up_v': 8.0,
     'L1_ffn_W1': 2.998}
    for name, (base, spread) in spreads.items():
        noise = np.random.default_rng([zlib.crc32(name.encode()), seed]).standard_normal(out[name].shape)
        drawn = base * np.exp(spread * noise) if base else spread * noise
        out[name] = jnp.asarray(drawn.astype(out[name].dtype))
    for name, factor in factors.items():
        out[name] = (out[name] * factor).astype(out[name].dtype)
    return out
```

```python
from contextlib import ExitStack

import numpy as np

import concourse.bass as bass
from concourse import mybir

P = 128
S = 2048
D = 128
H = 16
DK = D // H
NT = S // P
CW = 512
NC = S // CW
TC = CW // P
GH = 4
NG = H // GH
VW = 32
REL = 128
E0, HID0, SH0 = 8, 512, 2
E1, HID1, M1, ENC1 = 8, 128, 64, 256
KT0 = HID0 // P
BIAS_ROWS = 3 * NT
PARTS = 3
QK_ROWS = PARTS * PARTS * DK
EPS = 1e-5
DECAY = 0.01 * 0.01
CLAMP = 10000.0
SCALE = (1.0 / float(np.sqrt(np.float32(DK))), 1.0 / (float(np.sqrt(np.float32(D))) + 1e-8))
SCORE_LIMIT = 40.0
BIAS_LIMIT = 20.0
MAGIC = 1597463007.0
BAND = 3 * P
STRIP = (2 * NT - 1) * P
TROW = 512

F32 = mybir.dt.float32
BF16 = mybir.dt.bfloat16
I32 = mybir.dt.int32
U32 = mybir.dt.uint32
ALU = mybir.AluOpType
ACT = mybir.ActivationFunctionType
AX = mybir.AxisListType.X

NSTEP = 2 * NT * NC
NGRP = NT * NC
SCORE_BUFS = 3
PROB_BUFS = 3
EXP0 = SCORE_BUFS + 1
AV0 = 2 * NGRP
ACC0 = 2
GEN0 = 1
LAG = 2
TURN_AT, COPY_AT, NORM_AT = 5, 3, 7
HB = 3


def last_use(k, bufs, n):
    return k - bufs if k >= bufs else max(j for j in range(n) if j % bufs == k) - n


def adaln_two_layers(nc, t, out):
    with ExitStack() as ctx:
        names = set()

        def sb(name, shape, dt=F32, scope=ctx):
            return scope.enter_context(nc.sbuf_tensor("sb_" + name, shape, dt))

        def sem(name):
            assert name not in names
            names.add(name)
            return ctx.enter_context(nc.semaphore(name))

        ctx.enter_context(nc.allow_non_contiguous_dma(reason="small vectors, one element a partition"))
        ps = ctx.enter_context(nc.psum_tensor("ps", [P, 8, CW], F32))

        x = sb("x", [P, NT, D])
        hT = sb("hT", [P, S])
        ao = sb("ao", [P, NT, D])
        vall = sb("vall", [P, NT, D])
        ident = sb("ident", [P, P])
        headones = sb("headones", [P, P], BF16)
        ccol = sb("ccol", [P, 2])
        cexp = sb("cexp", [P, 2])
        silu = sb("silu", [P, 2])
        silub = sb("silub", [P, 2, P])
        mod = sb("mod", [P, 2, 6])
        gatesgn = sb("gatesgn", [P, 2])
        gateabs = sb("gateabs", [P, 2])
        gbrow = sb("gbrow", [P, 2, P])
        gbsgn = sb("gbsgn", [P, 2, P])
        stats = sb("stats", [P, NT, 6])
        meanvar = sb("meanvar", [P, NT, 2])
        rs_v = sb("rs_v", [P, TC])
        rs_i = sb("rs_i", [P, TC], I32)
        rs_y = sb("rs_y", [P, TC])
        rs_t = sb("rs_t", [P, TC])
        xn = sb("xn", [P, 2, TC, P])
        onorm = sb("onorm", [P, 2, TC, GH])
        nmx = sb("nmx", [P, 2, 2, NC])
        pm = sb("pm", [P, 4])
        flagf = sb("flagf", [1, 4])
        flagr = sb("flagr", [H, 1])
        flag = sb("flag", [1, 2], I32)
        iota_e = sb("iota_e", [P, 8])
        dup = sb("dup", [P, 2, CW])
        dtri = sb("dtri", [P, P])
        marks = sb("marks", [1, 16])
        wqkv = sb("wqkv", [P, 3 * D])
        wout0 = sb("wout0", [P, D])
        bqk = sb("bqk", [P, 3])
        bqs = sb("bqs", [P, 1])
        bvrow = sb("bvrow", [P, D])
        wq1 = sb("wq1", [P, D])
        wk1 = sb("wk1", [P, D])
        wv1 = sb("wv1", [P, D])
        wo1 = sb("wo1", [P, D])
        wdn1 = sb("wdn1", [P, 32])
        wup1 = sb("wup1", [32, 2, D])
        crow = sb("crow", [P, 2, H])
        mx8 = sb("mx8", [P, NT, 8])
        ix8 = sb("ix8", [P, NT, 8], U32)
        ixf = sb("ixf", [P, NT, 2])
        gts = sb("gts", [P, NT, 8])
        gsm = sb("gsm", [P, NT, 4])
        eq1 = sb("eq1", [P, NT, 8])
        eq2 = sb("eq2", [P, NT, 8])
        wgt = sb("wgt", [P, NT, 10])
        with ExitStack() as a0:
            w10 = sb("w10", [P, E0 + SH0, HID0], scope=a0)
            w20 = sb("w20", [P, E0 + SH0, KT0, D], scope=a0)
            b10 = sb("b10", [P, E0 + SH0, KT0], scope=a0)
            b20 = sb("b20", [E0 + SH0, D], scope=a0)
            rw0 = sb("rw0", [P, E0], scope=a0)
            rb0 = sb("rb0", [P, E0], scope=a0)
            rp = sb("rp", [BIAS_ROWS, 8], scope=a0)
            cpa = sb("cpa", [BIAS_ROWS, 2, H], BF16, scope=a0)
            cpb = sb("cpb", [BIAS_ROWS, 2, H], scope=a0)
            cpc = sb("cpc", [BIAS_ROWS, 2, H], BF16, scope=a0)
            cpd = sb("cpd", [BIAS_ROWS, 2, H], BF16, scope=a0)
            kbi = sb("kbi", [BIAS_ROWS, NT], scope=a0)
            mhi = sb("mhi", [BIAS_ROWS, NT], scope=a0)
            mlo = sb("mlo", [BIAS_ROWS, NT], scope=a0)
            oneh = sb("oneh", [BIAS_ROWS, NT], scope=a0)
            onehw = sb("onehw", [BIAS_ROWS, S], BF16, scope=a0)
            ktab = sb("ktab", [BIAS_ROWS, H, NT], scope=a0)
            ktab2 = sb("ktab2", [BIAS_ROWS, H, NT], scope=a0)
            with ExitStack() as s0:
                relt = sb("relt", [P, 3, H], scope=s0)
                relf = sb("relf", [H, 2 * REL + 1], scope=s0)
                relsq = sb("relsq", [H, 2 * REL + 1], scope=s0)
                relv = sb("relv", [H, TROW], scope=s0)
                wmod_sb = [sb(f"wmod{L}", [P, 6 * D], scope=s0) for L in range(2)]
                q32_0 = sb("q32_0", [P, 2, 2, CW], scope=s0)
                sq_0 = sb("sq_0", [P, 2, 2, CW], BF16, scope=s0)
                r1_0 = sb("r1_0", [P, 4, CW], scope=s0)
                pp_0 = sb("pp_0", [P, 4, PARTS, CW], BF16, scope=s0)
            with ExitStack() as s0:
                pr0 = sb("pr0", [P, PROB_BUFS, 2, 2, CW], scope=s0)
                tb0 = sb("tb0", [P, 2, GH, BAND], scope=s0)
                ot0 = sb("ot0", [P, CW], scope=s0)
                qst0 = sb("qst0", [P, 2, 1, GH, CW], BF16, scope=s0)
                kst0 = sb("kst0", [P, 2, 1, GH, S], BF16, scope=s0)
                vh0 = sb("vh0", [P, 2, NT, GH, VW], scope=s0)
            with ExitStack() as s0:
                oT_0 = sb("oT_0", [P, 2, CW], scope=s0)
                yT_0 = sb("yT_0", [P, 2, CW], scope=s0)
                hbuf0 = sb("hbuf0", [P, HB, KT0, CW], scope=s0)
                wT0 = sb("wT0", [E0 + SH0, S], scope=s0)
                q32_1 = sb("q32_1", [P, 2, 2, CW], scope=s0)
                sq_1 = sb("sq_1", [P, 2, 2, CW], BF16, scope=s0)
                lat = sb("lat", [32, 2, CW], scope=s0)
                w32 = sb("w32", [P, 4, CW], scope=s0)
                r1_1 = sb("r1_1", [P, 4, CW], scope=s0)
                pp_1 = sb("pp_1", [P, 4, PARTS, CW], BF16, scope=s0)
                kv32 = sb("kv32", [P, 2, CW], scope=s0)
            with ExitStack() as s0:
                g_k = sb("g_k", [DK, S], scope=s0)
                g_q = sb("g_q", [DK, S], scope=s0)
                g_qt = sb("g_qt", [DK, P], scope=s0)
                g_s = sb("g_s", [P, S], scope=s0)
                g_pt = sb("g_pt", [P, S], scope=s0)
                g_strip = sb("g_strip", [P, STRIP], scope=s0)
                g_tb = sb("g_tb", [P, BAND], scope=s0)
                g_m = sb("g_m", [P, 4], scope=s0)
        with ExitStack() as a1:
            wenc = sb("wenc", [P, ENC1], scope=a1)
            benc = sb("benc", [P, 2], scope=a1)
            ws2c = sb("ws2c", [P, 2, M1], scope=a1)
            bs2c = sb("bs2c", [M1, 1], scope=a1)
            wr1 = sb("wr1", [M1 + 1, E1], scope=a1)
            w11 = sb("w11", [M1 + 1, E1 * HID1], scope=a1)
            w21 = sb("w21", [P, E1, M1], scope=a1)
            b21 = sb("b21", [E1, M1], scope=a1)
            wc2s = sb("wc2s", [M1 + 1, ENC1], scope=a1)
            wdec = sb("wdec", [P, 2, D], scope=a1)
            bdec = sb("bdec", [P, D], scope=a1)
            lngr = sb("lngr", [P, D], scope=a1)
            lnbr = sb("lnbr", [P, D], scope=a1)
            with ExitStack() as s1:
                vh1 = sb("vh1", [P, 2, NT, GH, VW], scope=s1)
                kst1 = sb("kst1", [P, 2, 2, GH, S], BF16, scope=s1)
                qst1 = sb("qst1", [P, 2, 2, GH, CW], BF16, scope=s1)
                pr1 = sb("pr1", [P, PROB_BUFS, 2, 2, CW], scope=s1)
                ot1 = sb("ot1", [P, CW], scope=s1)
            with ExitStack() as s1:
                oT_1 = sb("oT_1", [P, 2, CW], scope=s1)
                yT_1 = sb("yT_1", [P, 2, CW], scope=s1)
                sp_e = sb("sp_e", [P, 2, 2, CW], scope=s1)
                contT = sb("contT", [M1 + 1, S], scope=s1)
                wT1 = sb("wT1", [E1, S], scope=s1)
                hbuf1 = sb("hbuf1", [P, E1, CW], scope=s1)
                ymul = sb("ymul", [P, 2, E1, M1], scope=s1)
                eo = sb("eo", [P, 2, TC, M1], scope=s1)
                eoT = sb("eoT", [M1 + 1, 2, CW], scope=s1)
                dec = sb("dec", [P, 2, TC, D], scope=s1)
                fo = sb("fo", [P, NC, TC, D], scope=s1)
            with ExitStack() as s1:
                h_k = sb("h_k", [DK, S], scope=s1)
                h_q = sb("h_q", [DK, S], scope=s1)
                h_qt = sb("h_qt", [DK, P], scope=s1)
                h_s = sb("h_s", [P, S], scope=s1)
                h_m = sb("h_m", [P, S], scope=s1)
                h_r = sb("h_r", [P, S], scope=s1)
                h_pt = sb("h_pt", [P, S], scope=s1)
                h_strip = sb("h_strip", [P, STRIP], scope=s1)
                h_st = sb("h_st", [P, 4], scope=s1)
        q32, sq, oT, yT = (q32_0, q32_1), (sq_0, sq_1), (oT_0, oT_1), (yT_0, yT_1)
        r1, pp = (r1_0, r1_1), (pp_0, pp_1)

        qparts = [nc.dram_tensor(f"qparts{L}", (L + 1, PARTS, PARTS, D, S), BF16, kind="Internal").ap() for L in range(2)]
        kparts = [nc.dram_tensor(f"kparts{L}", (L + 1, H, PARTS, DK, S), BF16, kind="Internal").ap() for L in range(2)]
        qkf = [nc.dram_tensor(f"qkf{L}", (2, D, S), F32, kind="Internal").ap() for L in range(2)]
        relrows = nc.dram_tensor("relrows", (H, P, TROW), F32, kind="Internal").ap()

        ld_x = [sem(f"ld_x{c}") for c in range(NC)]
        ld_mod, ld_att0, ld_rel, ld_att1, ld_ffn0, ld_ffn1 = (sem(n) for n in (
            "ld_mod", "ld_att0", "ld_rel", "ld_att1", "ld_ffn0", "ld_ffn1"))
        consts = sem("consts")
        decays = sem("decays")
        silu_exp, silu_done, mod_psum, mod_done = sem("silu_exp"), sem("silu_done"), sem("mod_psum"), sem("mod_done")
        dve_self = sem("dve_self")
        act_self = sem("act_self")
        pool_self = sem("pool_self")
        xn_ready, ln_psum, hT_ready = sem("xn_ready"), sem("ln_psum"), sem("hT_ready")
        relT_psum, relv_ready, relrows_stored = sem("relT_psum"), sem("relv_ready"), sem("relrows_stored")
        onehw_ready, _, ktab_ready = sem("onehw_ready"), None, sem("ktab_ready")
        gb_folded = sem("gb_folded")
        Ls = range(2)
        qk_psum = sem("qk_psum")
        q32_ready = sem("q32_ready")
        kv_psum, kv_read, lat_psum, lat_ready = sem("kv_psum"), sem("kv_read"), sem("lat_psum"), sem("lat_ready")
        v_psum = [sem(f"v_psum{L}") for L in Ls]
        v_ready = [sem(f"v_ready{L}") for L in Ls]
        w32_ready = sem("w32_ready")
        p1_ready = [sem(f"p1_ready{L}") for L in Ls]
        r1_ready = [sem(f"r1_ready{L}") for L in Ls]
        p2_ready = [sem(f"p2_ready{L}") for L in Ls]
        split_done = [sem(f"split_done{L}") for L in Ls]
        sq_ready = sem("sq_ready")
        nrm_psum = sem("nrm_psum")
        nrm_read = sem("nrm_read")
        parts_st = [[sem(f"parts_st{L}_{s}") for s in range(4)] for L in Ls]
        qkf_st = [[sem(f"qkf_st{L}_{s}") for s in range(4)] for L in Ls]
        pm_ready = sem("pm_ready")
        pmT_psum = sem("pmT_psum")
        flag_ready = sem("flag_ready")
        k_loaded = [[sem(f"k_loaded{L}_{p}") for p in range(2)] for L in Ls]
        q_loaded = [[sem(f"q_loaded{L}_{p}") for p in range(2)] for L in Ls]
        group_ready = [sem(f"group_ready{L}") for L in Ls]
        vh_filled = [sem(f"vh_filled{L}") for L in Ls]
        scores_psum = [sem(f"scores_psum{L}") for L in Ls]
        fixed = [sem(f"fixed{L}") for L in Ls]
        exp_done = [sem(f"exp_done{L}") for L in Ls]
        av_done = [sem(f"av_done{L}") for L in Ls]
        acc_copied = [sem(f"acc_copied{L}") for L in Ls]
        accT_psum = [sem(f"accT_psum{L}") for L in Ls]
        den_ready = [sem(f"den_ready{L}") for L in Ls]
        acc_free = [sem(f"acc_free{L}") for L in Ls]
        g_load, g_strip_ready, g_q_ready, g_sc, g_max, g_exp, g_tp, g_tc, g_av, g_fin, g_dv = (
            [sem(f"{n}{L}") for L in Ls] for n in (
                "g_load", "g_strip_ready", "g_q_ready", "g_sc", "g_max", "g_exp", "g_tp", "g_tc", "g_av", "g_fin", "g_dv"))
        g_tbT = sem("g_tbT")
        ao_ready = sem("ao_ready")
        aoT_psum = sem("aoT_psum")
        oT_ready = sem("oT_ready")
        y_psum = sem("y_psum")
        yT_ready = sem("yT_ready")
        yback_psum = sem("yback_psum")
        x_added = sem("x_added")
        gate_psum = sem("gate_psum")
        gate_d = sem("gate_d")
        gate_e = sem("gate_e")
        w_ready = sem("w_ready")
        wT_psum = sem("wT_psum")
        wT_ready = sem("wT_ready")
        h_psum, h_act, y0_psum, y0_read = sem("h_psum"), sem("h_act"), sem("y0_psum"), sem("y0_read")
        enc_psum, enc_act, cont_psum, cont_ready = sem("enc_psum"), sem("enc_act"), sem("cont_psum"), sem("cont_ready")
        hh_psum, hh_act, yy_psum, yy_read, yb_psum = sem("hh_psum"), sem("hh_act"), sem("yy_psum"), sem("yy_read"), sem("yb_psum")
        eo_ready, eoT_psum, eoT_ready = sem("eo_ready"), sem("eoT_psum"), sem("eoT_ready")
        exp1_psum, exp1_act, dec_psum, dec_ready, fo_ready = (
            sem("exp1_psum"), sem("exp1_act"), sem("dec_psum"), sem("dec_ready"), sem("fo_ready"))
        stored = sem("stored")

        def keys_of(qc):
            return list(range(NT))

        def fix_of(L, qc, kb):
            first, last = 4 * qc, 4 * qc + TC - 1
            lo, hi = (max(first, kb - 1), min(last, kb + 1)) if L == 0 else (kb, kb)
            if lo > hi or lo > last or hi < first:
                return None
            return lo - first, hi - first + 1

        groups = [(qc, kb) for qc in range(NC) for kb in keys_of(qc)]

        def fixes_before(L, gi):
            return 2 * sum(fix_of(L, *groups[j]) is not None for j in range(gi))

        NFIX = [fixes_before(L, NGRP) for L in Ls]
        KLOADS = [16 * (GH + 1), 16 * 2 * GH]
        QLOADS = [16 * (GH + 1), 16 * 2 * GH]
        qst, kst, vh, pr, ot = (qst0, qst1), (kst0, kst1), (vh0, vh1), (pr0, pr1), (ot0, ot1)
        ROW0 = (0, 0)
        ROWS = (BIAS_ROWS + QK_ROWS, QK_ROWS)
        QROW = (BIAS_ROWS, 0)
        NSPLIT = (2, 4)

        def bank(b):
            return ps[:, b, :]

        def tile4(b):
            return ps[:, b, :].rearrange("p (t d) -> p t d", t=TC)

        block = ctx.enter_context(nc.Block())

        @block.sync
        def _(sp):
            def load(dst, src, done):
                sp.dma_start(dst, src).then_inc(done, 16)

            def row(name, n, parts_=P, off=0):
                a = t[name]
                return bass.AP(a.tensor, a.offset + off, [[0, parts_], [1, n]])

            xin = t["L0_attn_x"].rearrange("b (t p) d -> p (b t) d", p=P)
            load(x[:, 0:TC, :], xin[:, 0:TC, :], ld_x[0])
            for L in Ls:
                load(ccol[:, L:L + 1], t[f"L{L}_c"].rearrange("a d -> d a"), ld_mod)
            for L in Ls:
                load(wmod_sb[L][:], t[f"L{L}_wmod"], ld_mod)
            load(wqkv[:], t["L0_attn_W_qkv"], ld_att0)
            load(bqk[:, 0:2], t["L0_attn_b_qkv"][0:2 * D].rearrange("(a p) -> p a", p=P), ld_att0)
            load(bqk[:, 2:3], t["L0_attn_b_out"].rearrange("(p a) -> p a", a=1), ld_att0)
            load(bvrow[:], row("L0_attn_b_qkv", D, off=2 * D), ld_att0)
            for c in range(1, NC):
                load(x[:, TC * c:TC * (c + 1), :], xin[:, TC * c:TC * (c + 1), :], ld_x[c])
            load(wout0[:], t["L0_attn_W_out"], ld_att0)
            rel = t["L0_attn_rel_bias"]
            load(relt[:, 0, :], rel[0:P, :], ld_rel)
            load(relt[:, 1, :], rel[P:2 * P, :], ld_rel)
            load(relt[0:1, 2, :], rel[2 * P:2 * P + 1, :], ld_rel)
            load(relf[:], bass.AP(rel.tensor, rel.offset, [[2 * REL + 1, H], [1, 2 * REL + 1]]), ld_rel)
            load(crow[:, 0, :], row("L0_attn_rel_bias", H), ld_rel)
            load(crow[:, 1, :], row("L0_attn_rel_bias", H, off=2 * REL * H), ld_rel)

            for e in range(E0):
                load(w10[:, e, :], t["L0_ffn_W1"][e], ld_ffn0)
                load(w20[:, e, :, :], t["L0_ffn_W2"][e].rearrange("(k p) d -> p k d", p=P), ld_ffn0)
            for e in range(SH0):
                load(w10[:, E0 + e, :], t["L0_ffn_sW1"][e], ld_ffn0)
                load(w20[:, E0 + e, :, :], t["L0_ffn_sW2"][e].rearrange("(k p) d -> p k d", p=P), ld_ffn0)
            load(b10[:, 0:E0, :], t["L0_ffn_b1"].rearrange("e (k p) -> p e k", p=P), ld_ffn0)
            load(b10[:, E0:, :], t["L0_ffn_sb1"].rearrange("e (k p) -> p e k", p=P), ld_ffn0)
            load(b20[0:E0, :], t["L0_ffn_b2"], ld_ffn0)
            load(b20[E0:, :], t["L0_ffn_sb2"], ld_ffn0)
            load(rw0[:], t["L0_ffn_rW"], ld_ffn0)
            load(rb0[:], row("L0_ffn_rb", E0), ld_ffn0)
            for dst, name in ((wq1, "Wq"), (wk1, "Wk"), (wv1, "Wv"), (wo1, "Wo"), (wdn1, "W_down_kv")):
                load(dst[:], t[f"L1_attn_{name}"], ld_att1)
            load(wup1[:, 0, :], t["L1_attn_W_up_k"], ld_att1)
            load(wup1[:, 1, :], t["L1_attn_W_up_v"], ld_att1)

            sp.wait_ge(relv_ready, 1)
            for h4 in range(NG):
                v = relv[GH * h4:GH * (h4 + 1), :].unsqueeze(1).to_broadcast([GH, P, TROW])
                sp.dma_start(relrows[GH * h4:GH * (h4 + 1)], v).then_inc(relrows_stored, 16)

            def stores(L, c):
                for u in range(2):
                    n = 2 * c + u
                    sp.wait_ge(q32_ready, 2 * NC * L + n + 1)
                    sp.dma_start(qkf[L][u, :, CW * c:CW * (c + 1)], q32[L][:, c % 2, u, :]).then_inc(qkf_st[L][n % 4], 16)
                for u in range(NSPLIT[L]):
                    n = NSPLIT[L] * c + u
                    sp.wait_ge(split_done[L], n + 1)
                    for a in range(PARTS):
                        src = pp[L][:, n % 4, a, :]
                        if u % 2 == 0:
                            dst = qparts[L][u // 2, a, :, :, CW * c:CW * (c + 1)].rearrange("r p n -> p r n")
                            src = src.unsqueeze(1).to_broadcast([P, PARTS, CW])
                        else:
                            dst = kparts[L][u // 2, :, a, :, CW * c:CW * (c + 1)]
                        sp.dma_start(dst, src).then_inc(parts_st[L][n % 4], 16)

            def stack_loads(L, v, u, dst, col0, n, head0, done):
                for hh in range(GH):
                    head = head0 + hh
                    if u == 0:
                        a = qparts[L]
                        src = bass.AP(a.tensor, a.offset + v * PARTS * PARTS * D * S + head * DK * S + col0,
                                      [[D * S, PARTS * PARTS], [S, DK], [1, n]])
                    else:
                        a = kparts[L]
                        src = bass.AP(a.tensor, a.offset + (v * H + head) * PARTS * DK * S + col0,
                                      [[0, PARTS], [S, PARTS * DK], [1, n]])
                    sp.dma_start(dst(hh)[QROW[L]:ROWS[L], :], src).then_inc(done, 16)

            def parts_complete(L):
                for s in range(4):
                    sp.wait_ge(parts_st[L][s], 16 * PARTS * NSPLIT[L] * NC // 4)
                    sp.wait_ge(qkf_st[L][s], 16 * 2 * NC // 4)

            def fast(L):
                def keys(g):
                    if g >= 2:
                        sp.wait_ge(av_done[L], AV0 + NGRP * (g - 1))
                    for v in range(L + 1):
                        stack_loads(L, v, 1, lambda hh: kst[L][:, g % 2, v, hh, :], 0, S, GH * g, k_loaded[L][g % 2])
                    if L == 0:
                        a = bass.AP(relrows.tensor, relrows.offset + GH * g * P * TROW + P - 1,
                                    [[TROW - 1, P], [P * TROW, GH], [1, BAND]])
                        sp.dma_start(tb0[:, g % 2, :, :], a).then_inc(k_loaded[0][g % 2], 16)

                def queries(m):
                    if m >= 2:
                        sp.wait_ge(scores_psum[L], 2 * NT * (m - 1))
                    c0 = CW * (m % NC)
                    for v in range(L + 1):
                        stack_loads(L, v, 0, lambda hh: qst[L][:, m % 2, v, hh, :], c0, CW,
                                    GH * (m // NC), q_loaded[L][m % 2])
                    if L == 0:
                        src = onehw[:, c0:c0 + CW].unsqueeze(1).to_broadcast([BIAS_ROWS, GH, CW])
                        sp.dma_start(qst0[0:BIAS_ROWS, m % 2, 0, :, :], src).then_inc(q_loaded[0][m % 2], 16)

                keys(0)
                queries(0)
                queries(1)
                keys(1)
                for m in range(2, NC * NG):
                    queries(m)
                    if m % NC == 0 and m // NC + 1 < NG:
                        keys(m // NC + 1)

            def general(L, k_, q_):
                with sp.Fori(0, H) as h:
                    for u, dst in ((1, k_), (0, q_)):
                        if u == 1:
                            sp.wait_ge(g_fin[L], h * NT + 1)
                        a = bass.AP(qkf[L].tensor, qkf[L].offset + u * D * S + h * (DK * S), [[S, DK], [1, S]])
                        sp.dma_start(dst[:], a).then_inc(g_load[L], 16)
                    if L == 0:
                        a = bass.AP(relrows.tensor, relrows.offset + P - 1 + h * (P * TROW), [[TROW - 1, P], [1, BAND]])
                        sp.dma_start(g_tb[:], a).then_inc(g_load[L], 16)

            for c in range(NC):
                stores(0, c)
            parts_complete(0)
            sp.wait_ge(onehw_ready, 1)
            sp.wait_ge(relrows_stored, 16 * NG)
            sp.wait_ge(flag_ready, 1)
            fv = sp.value_load(flag[0:1, 0:1])
            with sp.If(fv > 0):
                fast(0)
            with sp.Else():
                general(0, g_k, g_q)
            for c in range(NC - 1):
                stores(1, c)
            sp.wait_ge(y0_read, NC * (E0 + 1))
            load(wenc[:], t["L1_ffn_W_enc"], ld_ffn1)
            load(benc[:], t["L1_ffn_b_enc"].rearrange("(a p) -> p a", p=P), ld_ffn1)
            load(ws2c[:], t["L1_ffn_W_s2c"].rearrange("(a p) m -> p a m", p=P), ld_ffn1)
            load(bs2c[:], t["L1_ffn_b_s2c"].rearrange("(p a) -> p a", a=1), ld_ffn1)
            load(wr1[0:M1, :], t["L1_ffn_Wr"], ld_ffn1)
            load(wr1[M1:, :], row("L1_ffn_br", E1, 1), ld_ffn1)
            load(w11[0:M1, :].rearrange("m (e h) -> m e h", e=E1), t["L1_ffn_W1"].rearrange("e m h -> m e h"), ld_ffn1)
            load(w11[M1:, :], row("L1_ffn_b1", E1 * HID1, 1), ld_ffn1)
            load(w21[:], t["L1_ffn_W2"].rearrange("e h m -> h e m"), ld_ffn1)
            load(b21[:], t["L1_ffn_b2"], ld_ffn1)
            load(wc2s[0:M1, :], t["L1_ffn_W_c2s"], ld_ffn1)
            load(wc2s[M1:, :], row("L1_ffn_b_c2s", ENC1, 1), ld_ffn1)
            load(wdec[:], t["L1_ffn_W_dec"].rearrange("(a p) d -> p a d", p=P), ld_ffn1)
            load(bdec[:], row("L1_ffn_b_dec", D), ld_ffn1)
            load(lngr[:], row("L1_ffn_ln_g", D), ld_ffn1)
            load(lnbr[:], row("L1_ffn_ln_b", D), ld_ffn1)
            stores(1, NC - 1)
            parts_complete(1)
            sp.wait_ge(flag_ready, 1 + 1)
            fv = sp.value_load(flag[0:1, 1:2])
            with sp.If(fv > 0):
                fast(1)
            with sp.Else():
                general(1, h_k, h_q)
            xout = out.rearrange("b (t p) d -> p (b t) d", p=P)
            for c in range(NC):
                sp.wait_ge(fo_ready, c + 1)
                sp.dma_start(xout[:, TC * c:TC * (c + 1), :], fo[:, c, :, :]).then_inc(stored, 16)
            sp.wait_ge(stored, 16 * NC)

        order0 = [E0, E0 + 1] + list(range(E0))

        def y_index(n):
            c, j = divmod(n, len(order0))
            return (E0 + 1) * c + max(j - 1, 0)

        def ln_pass(L, second):
            return 2 * L + second

        @block.gpsimd
        def _(pool):
            self_n = [0]

            def link(ins):
                self_n[0] += 1
                ins.then_inc(pool_self, 1)
                pool.wait_ge(pool_self, self_n[0])

            def iota(dst, pattern, base, mult):
                return nc.gpsimd.iota(dst, pattern, base, mult, allow_small_or_imprecise_dtypes=True)

            link(nc.gpsimd.memset(ident[:], 0.0))
            link(nc.gpsimd.affine_select(out=ident[:], in_=ident[:], compare_op=ALU.not_equal, fill=1.0, base=0,
                                         pattern=[[-1, P]], channel_multiplier=1))
            link(nc.gpsimd.memset(headones[:], 1.0))
            hv = headones[:].rearrange("p (a b) -> p a b", b=DK)
            link(nc.gpsimd.affine_select(out=hv, in_=hv, compare_op=ALU.is_ge, fill=0.0, base=0,
                                         pattern=[[-DK, H], [0, DK]], channel_multiplier=1))
            link(nc.gpsimd.affine_select(out=hv, in_=hv, compare_op=ALU.is_ge, fill=0.0, base=DK - 1,
                                         pattern=[[DK, H], [0, DK]], channel_multiplier=-1))
            iota(iota_e[:], [[1, 8]], 0, 0)
            iota(rp[:, 0:1], [[0, 1]], 0, 1)
            iota(kbi[:], [[1, NT]], 0, 0)
            iota(dup[:, 0, :], [[1, CW]], 0, 0)
            iota(dup[:, 1, :], [[1, CW]], 0, 0)
            iota(dtri[:], [[1, P]], 0, -1).then_inc(consts, 1)
            for L in Ls:
                nc.gpsimd.memset(marks[0:1, 0 + L:1 + L], 0.0).then_inc(exp_done[L], EXP0)
                nc.gpsimd.memset(marks[0:1, 2 + L:3 + L], 0.0).then_inc(av_done[L], AV0)
                nc.gpsimd.memset(marks[0:1, 4 + L:5 + L], 0.0).then_inc(acc_free[L], ACC0)
                nc.gpsimd.memset(marks[0:1, 6 + L:7 + L], 0.0).then_inc(g_fin[L], GEN0)
            pool.wait_ge(mod_done, 1)
            pool.wait_ge(ld_ffn0, 16 * (2 * (E0 + SH0) + 6))
            w20v = w20[:].rearrange("p e k d -> p (e k) d")
            nk = (E0 + SH0) * KT0
            link(nc.gpsimd.tensor_tensor(w20v, w20v, gbrow[:, 0, :].unsqueeze(1).to_broadcast([P, nk, D]), ALU.mult))
            nc.gpsimd.tensor_tensor(b20[:], b20[:], gbrow[0:E0 + SH0, 0, :], ALU.mult)
            link(nc.gpsimd.tensor_scalar(w20[:, E0:, :, :].rearrange("p e k d -> p (e k d)"),
                                         w20[:, E0:, :, :].rearrange("p e k d -> p (e k d)"),
                                         1.0 / SH0, None, ALU.mult))
            nc.gpsimd.memset(marks[0:1, 8:9], 0.0).then_inc(gb_folded, 1)

            def fill(L):
                nc.gpsimd.memset(vh[L][:].rearrange("p a k h w -> p (a k h w)"), 0.0).then_inc(vh_filled[L], 1)
                pool.wait_ge(vh_filled[L], 1)
                nc.gpsimd.memset(vh[L][:, :, :, :, DK:DK + 1].rearrange("p a k h w -> p (a k) h w"), 1.0)\
                  .then_inc(vh_filled[L], 1)

            def group(L, g):
                p_ = g % 2
                if L == 0:
                    for hh in range(GH):
                        nc.gpsimd.tensor_copy(
                            kst0[0:BIAS_ROWS, p_, 0, hh, :].rearrange("p (k n) -> p k n", n=P),
                            ktab[:, g * GH + hh, :].unsqueeze(2).to_broadcast([BIAS_ROWS, NT, P]))
                if g == 0:
                    pool.wait_ge(vh_filled[L], 2)
                    pool.wait_ge(v_ready[L], NC)
                nc.gpsimd.tensor_copy(
                    vh[L][:, p_, :, :, 0:DK],
                    vall[:, :, g * (GH * DK):(g + 1) * (GH * DK)].rearrange("p k (h d) -> p k h d", h=GH))\
                  .then_inc(group_ready[L], 1)

            def fast(L):
                for g in range(1, NG):
                    pool.wait_ge(av_done[L], g * NGRP + (AV0 - NGRP))
                    group(L, g)

            def general1():
                iota(h_strip[:], [[-1, STRIP]], (NT - 1) * P, 1).then_inc(g_strip_ready[1], 1)

            fill(0)
            pool.wait_ge(ktab_ready, 1)
            group(0, 0)
            pool.wait_ge(flag_ready, 1)
            fv = pool.value_load(flag[0:1, 0:1])
            with pool.If(fv > 0):
                fast(0)
            pool.wait_ge(y0_read, NC * (E0 + 1))
            fill(1)
            group(1, 0)
            pool.wait_ge(flag_ready, 1 + 1)
            fv = pool.value_load(flag[0:1, 1:2])
            with pool.If(fv > 0):
                fast(1)
            with pool.Else():
                general1()

        @block.scalar
        def _(act):
            def modcol(L, j):
                return mod[:, L, j:j + 1]

            def ln_out(L, second, c):
                m = NC * ln_pass(L, second) + c
                act.wait_ge(ln_psum, m + 1)
                nc.scalar.activation(hT[:, CW * c:CW * (c + 1)], bank(6), ACT.Identity,
                                     bias=modcol(L, 3 * second), scale=modcol(L, 3 * second + 1)).then_inc(hT_ready, 1)

            def q32_slot(L, c, u):
                n = 2 * c + u
                if n >= 4:
                    act.wait_ge(qkf_st[L][n % 4], 16 * (n // 4))
                    act.wait_ge(split_done[L], NSPLIT[L] * (c - 1))
                    act.wait_ge(nrm_psum, 2 * NC * L + 2 * (c - 1))
                return q32[L][:, c % 2, u, :]

            def square(L, c, u):
                nc.scalar.activation(sq[L][:, c % 2, u, :], q32[L][:, c % 2, u, :], ACT.Square).then_inc(sq_ready, 1)

            def first_part(L, n, src):
                if n >= 4:
                    act.wait_ge(parts_st[L][n % 4], 16 * PARTS * (n // 4))
                nc.scalar.copy(pp[L][:, n % 4, 0, :], src).then_inc(p1_ready[L], 1)

            def second_part(L, n):
                act.wait_ge(r1_ready[L], n + 1)
                nc.scalar.copy(pp[L][:, n % 4, 1, :], r1[L][:, n % 4, :]).then_inc(p2_ready[L], 1)

            def project0(c):
                for u in range(2):
                    act.wait_ge(qk_psum, 2 * c + u + 1)
                    dst = q32_slot(0, c, u)
                    bias, scale = (bqs[:, 0:1], SCALE[0]) if u == 0 else (bqk[:, 1:2], 1.0)
                    nc.scalar.activation(dst, bank(3 * (c % 2) + u), ACT.Identity, bias=bias, scale=scale)\
                      .then_inc(q32_ready, 1)
                    act.wait_ge(q32_ready, 2 * c + u + 1)
                    first_part(0, 2 * c + u, dst)
                    square(0, c, u)
                for u in range(2):
                    second_part(0, 2 * c + u)

            def layer1_step(j, c):
                if j == 2:
                    ln_out(1, 0, c)
                elif j == 3:
                    act.wait_ge(qk_psum, 2 * NC + 2 * c + 1)
                    dst = q32_slot(1, c, 0)
                    nc.scalar.activation(dst, bank(5), ACT.Copy, scale=SCALE[1]).then_inc(q32_ready, 1)
                    act.wait_ge(kv_psum, c + 1)
                    nc.scalar.copy(kv32[:, c % 2, :], bank(6)).then_inc(kv_read, 1)
                elif j == 4:
                    act.wait_ge(lat_psum, c + 1)
                    nc.scalar.copy(lat[:, c % 2, :], ps[0:32, 5, :]).then_inc(lat_ready, 1)
                elif j == 5:
                    act.wait_ge(qk_psum, 2 * NC + 2 * c + 2)
                    dst = q32_slot(1, c, 1)
                    nc.scalar.copy(dst, bank(6)).then_inc(q32_ready, 1)
                    act.wait_ge(q32_ready, 2 * NC + 2 * c + 2)
                    for u in range(2):
                        square(1, c, u)
                elif j == 7:
                    for n in range(4 * c, 4 * c + 4):
                        act.wait_ge(w32_ready, n + 1)
                        first_part(1, n, w32[:, n % 4, :])
                elif j == 9:
                    for n in range(4 * c, 4 * c + 4):
                        second_part(1, n)

            def fast(L):
                with act.Fori(0, NG // 2) as i:
                    for p_ in range(2):
                        g = 2 * i + p_
                        nfix = 0
                        for gi, (qc, kb) in enumerate(groups):
                            k = NGRP * p_ + gi
                            for pair in range(2):
                                step = 2 * gi + pair
                                b = 2 * ((NSTEP * p_ + step) % SCORE_BUFS)
                                if fix_of(L, qc, kb):
                                    nfix += 1
                                    act.wait_ge(fixed[L], g * NFIX[L] + nfix)
                                else:
                                    act.wait_ge(scores_psum[L], g * NSTEP + (step + 1))
                                if pair == 0:
                                    act.wait_ge(av_done[L], i * (2 * NGRP) + (AV0 + last_use(k, PROB_BUFS, 2 * NGRP) + 1))
                                nc.scalar.activation(pr[L][:, k % PROB_BUFS, pair, :, :], ps[:, b:b + 2, :], ACT.Exp)\
                                  .then_inc(exp_done[L], 1)

            def general(L):
                g_row = (g_s, h_s)[L]
                st = (g_m, h_st)[L]
                if L == 1:
                    act.wait_ge(g_strip_ready[1], 1)
                    nc.scalar.activation(h_strip[:], h_strip[:], ACT.Abs).then_inc(g_strip_ready[1], 1)
                    act.wait_ge(g_strip_ready[1], 2)
                    nc.scalar.activation(h_strip[:], h_strip[:], ACT.Exp, scale=-DECAY).then_inc(g_strip_ready[1], 1)
                with act.Fori(0, H * NT) as n:
                    act.wait_ge(g_max[L], n + 1)
                    nc.scalar.activation(g_row[:], g_row[:], ACT.Exp, bias=st[:, 1:2], accum_out=st[:, 2:3])\
                      .then_inc(g_exp[L], 1)

            def attend(L):
                act.wait_ge(flag_ready, L + 1)
                fv = act.value_load(flag[0:1, L:L + 1])
                with act.If(fv > 0):
                    fast(L)
                with act.Else():
                    general(L)

            def projected(L):
                for c in range(NC):
                    act.wait_ge(aoT_psum, NC * L + c + 1)
                    if c >= 2:
                        act.wait_ge(y_psum, NC * L + c - 1)
                    nc.scalar.copy(oT[L][:, c % 2, :], bank(c)).then_inc(oT_ready, 1)
                for c in range(NC):
                    ln_out(L, 1, c)

            act.wait_ge(ld_mod, 16 * 4)
            nc.scalar.activation(cexp[:], ccol[:], ACT.Exp, scale=-1.0).then_inc(silu_exp, 1)
            act.wait_ge(consts, 1)
            nc.scalar.activation(dup[:, 0, :], dup[:, 0, :], ACT.Exp, scale=-DECAY).then_inc(decays, 1)
            nc.scalar.activation(dup[:, 1, :], dup[:, 1, :], ACT.Exp, scale=DECAY).then_inc(decays, 1)
            act.wait_ge(decays, 3)
            nc.scalar.activation(dtri[:], dtri[:], ACT.Exp, scale=2 * DECAY).then_inc(decays, 1)
            act.wait_ge(mod_done, 1)
            act.wait_ge(ld_att0, 16 * 5)
            ln_out(0, 0, 0)
            for c in range(NC):
                if c + 1 < NC:
                    ln_out(0, 0, c + 1)
                project0(c)
            attend(0)
            projected(0)
            act.wait_ge(gate_d, 1)
            nc.scalar.activation(gsm[:, :, 1], gsm[:, :, 0], ACT.Exp).then_inc(gate_e, 1)
            act.wait_ge(ld_ffn0, 16 * (2 * (E0 + SH0) + 6))
            for n in range(NC * len(order0)):
                e = order0[n % len(order0)]
                if n >= HB:
                    act.wait_ge(y0_psum, y_index(n - HB) + 1)
                for k in range(KT0):
                    act.wait_ge(h_psum, KT0 * n + k + 1)
                    nc.scalar.activation(hbuf0[:, n % HB, k, :], bank((KT0 * n + k) % 3), ACT.Gelu,
                                         bias=b10[:, e, k:k + 1]).then_inc(h_act, 1)
                c, j = divmod(n, len(order0))
                if c:
                    layer1_step(j, c - 1)
            for j in range(len(order0)):
                layer1_step(j, NC - 1)
            attend(1)
            projected(1)
            act.wait_ge(ld_ffn1, 16 * 16)
            for c in range(NC):
                for a in range(2):
                    act.wait_ge(enc_psum, 2 * c + a + 1)
                    if c >= 2:
                        act.wait_ge(cont_psum, c - 1)
                    nc.scalar.activation(sp_e[:, c % 2, a, :], bank(2 * (c % 2) + a), ACT.Sigmoid,
                                         bias=benc[:, a:a + 1]).then_inc(enc_act, 1)
            act.wait_ge(gate_d, 1 + 1)
            nc.scalar.activation(gts[:], gts[:], ACT.Exp).then_inc(gate_e, 1)

            def expand1(c):
                act.wait_ge(eoT_psum, c + 1)
                if c >= 2:
                    act.wait_ge(exp1_psum, 2 * (c - 1))
                nc.scalar.copy(eoT[0:M1, c % 2, :], ps[0:M1, 5, :]).then_inc(eoT_ready, 1)
                for a in range(2):
                    act.wait_ge(exp1_psum, 2 * c + a + 1)
                    if c >= 2:
                        act.wait_ge(dec_psum, c - 1)
                    nc.scalar.activation(sp_e[:, c % 2, a, :], bank(6 + a), ACT.Sigmoid).then_inc(exp1_act, 1)

            for c in range(NC):
                if c:
                    act.wait_ge(yy_psum, TC * c)
                for e in range(E1):
                    act.wait_ge(hh_psum, E1 * c + e + 1)
                    nc.scalar.activation(hbuf1[:, e, :], bank((E1 * c + e) % 2), ACT.Relu).then_inc(hh_act, 1)
                if c:
                    expand1(c - 1)
            expand1(NC - 1)

        @block.tensor
        def _(pe):
            mm, tr = nc.tensor.matmul, nc.tensor.transpose

            def ln_transpose(L, second, c):
                m = NC * ln_pass(L, second) + c
                pe.wait_ge(xn_ready, m + 1)
                if m:
                    pe.wait_ge(hT_ready, m)
                for k in range(TC):
                    last = tr(ps[:, 6, P * k:P * (k + 1)], xn[:, m % 2, k, :], ident[:])
                last.then_inc(ln_psum, 1)

            def norms(L, c, us=range(2)):
                for u in us:
                    i = 2 * c + u
                    pe.wait_ge(sq_ready, 2 * NC * L + i + 1)
                    if i:
                        pe.wait_ge(nrm_read, 2 * NC * L + i)
                    mm(bank(7), headones[:], sq[L][:, c % 2, u, :], start=True, stop=True).then_inc(nrm_psum, 1)

            def project0(c):
                b = 3 * (c % 2)
                cols = slice(CW * c, CW * (c + 1))
                pe.wait_ge(hT_ready, c + 1)
                if c >= 2:
                    pe.wait_ge(q32_ready, 2 * (c - 1))
                    pe.wait_ge(v_ready[0], c - 1)
                for u in range(2):
                    mm(bank(b + u), wqkv[:, D * u:D * (u + 1)], hT[:, cols], start=True, stop=True)\
                      .then_inc(qk_psum, 1)
                for k in range(TC):
                    last = mm(ps[:, b + 2, P * k:P * (k + 1)], hT[:, CW * c + P * k:CW * c + P * (k + 1)],
                              wqkv[:, 2 * D:3 * D], start=True, stop=True)
                last.then_inc(v_psum[0], 1)

            def layer1_step(j, c):
                if j == 2:
                    if c:
                        pe.wait_ge(q32_ready, 2 * NC + 2 * c)
                    ln_transpose(1, 0, c)
                elif j == 3:
                    cols = slice(CW * c, CW * (c + 1))
                    pe.wait_ge(hT_ready, 2 * NC + c + 1)
                    if c:
                        pe.wait_ge(v_ready[1], c)
                    mm(bank(5), wq1[:], hT[:, cols], start=True, stop=True).then_inc(qk_psum, 1)
                    mm(bank(6), wk1[:], hT[:, cols], start=True, stop=False)
                    mm(bank(6), wv1[:], hT[:, cols], start=False, stop=True).then_inc(kv_psum, 1)
                elif j == 4:
                    pe.wait_ge(kv_read, c + 1)
                    pe.wait_ge(q32_ready, 2 * NC + 2 * c + 1)
                    mm(ps[0:32, 5, :], wdn1[:], kv32[:, c % 2, :], start=True, stop=True).then_inc(lat_psum, 1)
                elif j == 5:
                    pe.wait_ge(lat_ready, c + 1)
                    mm(bank(6), wup1[:, 0, :], lat[:, c % 2, :], start=True, stop=True).then_inc(qk_psum, 1)
                    for k in range(TC):
                        last = mm(ps[:, 5, P * k:P * (k + 1)], lat[:, c % 2, P * k:P * (k + 1)],
                                  wup1[:, 1, :], start=True, stop=True)
                    last.then_inc(v_psum[1], 1)
                elif j in (7, 9):
                    norms(1, c, [(j - 7) // 2])

            def decide(L):
                pe.wait_ge(pm_ready, L + 1)
                tr(ps[0:1, 7, 0:P], pm[:, 0:1], ident[:]).then_inc(pmT_psum, 1)

            def fast(L):
                def scores(g, p_, i, gi):
                    qc, kb = groups[gi]
                    if gi == 0:
                        pe.wait_ge(k_loaded[L][p_], i * KLOADS[L] + KLOADS[L])
                        pe.wait_ge(group_ready[L], g + 1)
                    if gi % NT == 0:
                        pe.wait_ge(q_loaded[L][qc % 2], g * (2 * QLOADS[L]) + QLOADS[L] * (qc // 2 + 1))
                    for pair in range(2):
                        step = 2 * gi + pair
                        b = 2 * ((NSTEP * p_ + step) % SCORE_BUFS)
                        last_exp = last_use(NSTEP * p_ + step, SCORE_BUFS, 2 * NSTEP)
                        pe.wait_ge(exp_done[L], i * (2 * NSTEP) + (EXP0 + last_exp + 1))
                        nlo = min(max(kb - TC * qc, 0), TC) * P if L == 1 else 0
                        for hh in range(2):
                            head = 2 * pair + hh
                            for v, lo, hi in ((1, 0, nlo), (0, nlo, CW)):
                                if lo < hi:
                                    last = mm(ps[:, b + hh, lo:hi],
                                              kst[L][0:ROWS[L], p_, v, head, P * kb:P * (kb + 1)],
                                              qst[L][0:ROWS[L], qc % 2, v, head, lo:hi], start=True, stop=True)
                        last.then_inc(scores_psum[L], 1)

                def values(g, p_, gi):
                    qc, kb = groups[gi]
                    pe.wait_ge(exp_done[L], g * NSTEP + (EXP0 + 2 * gi + 2))
                    if gi % NT == 0:
                        pe.wait_ge(acc_free[L], g * NC + (qc + ACC0 - 1))
                    for h in range(GH):
                        last = mm(ps[VW * h:VW * (h + 1), 6 + qc % 2, :], vh[L][:, p_, kb, h, :],
                                  pr[L][:, (NGRP * p_ + gi) % PROB_BUFS, h // 2, h % 2, :],
                                  start=(gi % NT == 0), stop=(gi % NT == NT - 1))
                    last.then_inc(av_done[L], 1)

                def turn(g, qc):
                    pe.wait_ge(acc_copied[L], g * NC + (qc + 1))
                    for k in range(TC):
                        last = tr(ps[:, 6 + qc % 2, P * k:P * (k + 1)], ot[L][:, P * k:P * (k + 1)], ident[:])
                    last.then_inc(accT_psum[L], 1)

                with pe.Fori(0, NG // 2) as i:
                    for k in range(2 * NGRP):
                        scores(2 * i + k // NGRP, k // NGRP, i, k % NGRP)
                        if k >= LAG:
                            p_, gi = divmod(k - LAG, NGRP)
                            values(2 * i + p_, p_, gi)
                        if k > NT and k % NT == TURN_AT:
                            p_, qc = divmod(k // NT - 1, NC)
                            turn(2 * i + p_, qc)
                    for gi in range(NGRP - LAG, NGRP):
                        values(2 * i + 1, 1, gi)
                    turn(2 * i + 1, NC - 1)

            def general(L):
                k_, qt_, row_, pt_ = ((g_k, g_qt, g_s, g_pt), (h_k, h_qt, h_s, h_pt))[L]
                nload = 48 if L == 0 else 32
                with pe.Fori(0, H) as h:
                    if L == 0:
                        pe.wait_ge(g_load[L], h * nload + nload)
                        for b in range(3):
                            last = tr(ps[:, 4, P * b:P * (b + 1)], g_tb[:, P * (2 - b):P * (3 - b)], ident[:])
                        last.then_inc(g_tbT, 1)
                    with pe.Fori(0, NT) as q:
                        n = h * NT + q
                        pe.wait_ge(g_load[L], h * nload + nload)
                        pe.wait_ge(g_q_ready[L], n + 1)
                        pe.wait_ge(g_fin[L], n + GEN0)
                        for c in range(NC):
                            last = mm(bank(c), qt_[:], k_[:, CW * c:CW * (c + 1)], start=True, stop=True)
                        last.then_inc(g_sc[L], 1)
                        pe.wait_ge(g_exp[L], n + 1)
                        for kb in range(NT):
                            last = tr(ps[:, 4 + kb // TC, P * (kb % TC):P * (kb % TC + 1)],
                                      row_[:, P * kb:P * (kb + 1)], ident[:])
                        last.then_inc(g_tp[L], 1)
                        pe.wait_ge(g_tc[L], n + 1)
                        for kb in range(NT):
                            last = mm(ps[:, 0, 0:DK], pt_[:, P * kb:P * (kb + 1)],
                                      vall[:, kb, bass.ds(h * DK, DK)], start=(kb == 0), stop=(kb == NT - 1))
                        last.then_inc(g_av[L], 1)

            def attend(L):
                pe.wait_ge(flag_ready, L + 1)
                fv = pe.value_load(flag[0:1, L:L + 1])
                with pe.If(fv > 0):
                    fast(L)
                with pe.Else():
                    general(L)

            def projected(L):
                wo = (wout0, wo1)[L]

                def turn(c):
                    for k in range(TC):
                        last = tr(ps[:, c, P * k:P * (k + 1)], ao[:, TC * c + k, :], ident[:])
                    last.then_inc(aoT_psum, 1)

                def product(c):
                    pe.wait_ge(oT_ready, NC * L + c + 1)
                    if c >= 2:
                        pe.wait_ge(yT_ready, NC * L + c - 1)
                    mm(bank(4 + c % 2), wo[:], oT[L][:, c % 2, :], start=True, stop=True).then_inc(y_psum, 1)

                def back(c):
                    pe.wait_ge(yT_ready, NC * L + c + 1)
                    for k in range(TC):
                        last = tr(ps[:, c, P * k:P * (k + 1)], yT[L][:, c % 2, P * k:P * (k + 1)], ident[:])
                    last.then_inc(yback_psum, 1)

                pe.wait_ge(ao_ready, L + 1)
                for c in range(NC):
                    turn(c)
                product(0)
                product(1)
                back(0)
                product(2)
                back(1)
                ln_transpose(L, 1, 0)
                product(3)
                back(2)
                ln_transpose(L, 1, 1)
                back(3)
                ln_transpose(L, 1, 2)
                ln_transpose(L, 1, 3)

            def turn_weights(L, n, dst_rows):
                pe.wait_ge(w_ready, L + 1)
                for c in range(NC):
                    if c >= 2:
                        pe.wait_ge(wT_ready, NC * L + c - 1)
                    for k in range(TC):
                        last = tr(ps[0:n, 6 + c % 2, P * k:P * (k + 1)], wgt[:, TC * c + k, 0:n], ident[:])
                    last.then_inc(wT_psum, 1)

            pe.wait_ge(consts, 1)
            pe.wait_ge(silu_done, 1)
            for L in Ls:
                for j in range(6):
                    mm(ps[:, 7, 6 * L + j:6 * L + j + 1], wmod_sb[L][:, D * j:D * (j + 1)], silu[:, L:L + 1],
                       start=True, stop=True)
            for L in Ls:
                last = mm(ps[:, 6, D * L:D * (L + 1)], silub[:, L, :], wmod_sb[L][:, 5 * D:6 * D], start=True, stop=True)
            last.then_inc(mod_psum, 1)
            pe.wait_ge(ld_rel, 16 * 6)
            tr(ps[0:H, 5, 0:P], relt[:, 0, :], ident[:])
            tr(ps[0:H, 5, P:2 * P], relt[:, 1, :], ident[:])
            tr(ps[0:H, 5, 2 * P:2 * P + 1], relt[0:1, 2, :], ident[0:1, 0:1]).then_inc(relT_psum, 1)
            pe.wait_ge(mod_done, 1)
            pe.wait_ge(relv_ready, 1)
            pe.wait_ge(ld_att0, 16 * 5)
            ln_transpose(0, 0, 0)
            for c in range(NC):
                if c + 1 < NC:
                    ln_transpose(0, 0, c + 1)
                project0(c)
                norms(0, c)
            decide(0)
            attend(0)
            projected(0)

            pe.wait_ge(ld_ffn0, 16 * (2 * (E0 + SH0) + 6))
            for c in range(NC):
                pe.wait_ge(hT_ready, NC + c + 1)
                for k in range(TC):
                    last = mm(ps[:, 7, E0 * (TC * c + k):E0 * (TC * c + k + 1)],
                              hT[:, CW * c + P * k:CW * c + P * (k + 1)], rw0[:], start=True, stop=True)
                last.then_inc(gate_psum, 1)

            def hidden0(n):
                c, j = divmod(n, len(order0))
                for k in range(KT0):
                    i = KT0 * n + k
                    if i >= 3:
                        pe.wait_ge(h_act, i - 2)
                    mm(bank(i % 3), w10[:, order0[j], P * k:P * (k + 1)], hT[:, CW * c:CW * (c + 1)],
                       start=True, stop=True).then_inc(h_psum, 1)

            def output0(n):
                c, j = divmod(n, len(order0))
                if j == 0:
                    return
                y = y_index(n)
                pe.wait_ge(h_act, KT0 * (n + 1))
                if y >= 2:
                    pe.wait_ge(y0_read, y - 1)
                for k in range(TC):
                    dst = ps[:, 3 + y % 2, P * k:P * (k + 1)]
                    toks = slice(P * k, P * (k + 1))
                    if j == 1:
                        mm(dst, wT0[:, CW * c + P * k:CW * c + P * (k + 1)], b20[:], start=True, stop=False)
                        terms = [(n - 1, order0[0]), (n, order0[1])]
                    else:
                        terms = [(n, order0[j])]
                    every = [(m, e, q) for m, e in terms for q in range(KT0)]
                    for a, (m, e, q) in enumerate(every):
                        last = mm(dst, hbuf0[:, m % HB, q, toks], w20[:, e, q, :],
                                  start=(j > 1 and a == 0), stop=(a == len(every) - 1))
                last.then_inc(y0_psum, 1)

            hidden0(0)
            hidden0(1)
            turn_weights(0, E0 + SH0, wT0)
            pe.wait_ge(wT_ready, NC)
            pe.wait_ge(gb_folded, 1)
            pe.wait_ge(ld_att1, 16 * 7)
            for n in range(2, NC * len(order0)):
                hidden0(n)
                output0(n - 1)
                c, j = divmod(n, len(order0))
                if c:
                    layer1_step(j, c - 1)
            output0(NC * len(order0) - 1)
            for j in range(len(order0)):
                layer1_step(j, NC - 1)
            decide(1)
            attend(1)
            projected(1)

            pe.wait_ge(ld_ffn1, 16 * 16)

            def encode(c):
                pe.wait_ge(hT_ready, 3 * NC + c + 1)
                for a in range(2):
                    if c >= 2:
                        pe.wait_ge(enc_act, 2 * (c - 2) + a + 1)
                    mm(bank(2 * (c % 2) + a), wenc[:, P * a:P * (a + 1)], hT[:, CW * c:CW * (c + 1)],
                       start=True, stop=True).then_inc(enc_psum, 1)

            def contract(c):
                pe.wait_ge(enc_act, 2 * (c + 1))
                if c >= 2:
                    pe.wait_ge(cont_ready, c - 1)
                for a in range(2):
                    last = mm(ps[0:M1, 4 + c % 2, :], ws2c[:, a, :], sp_e[:, c % 2, a, :], start=(a == 0), stop=(a == 1))
                last.then_inc(cont_psum, 1)

            def route(c):
                pe.wait_ge(cont_ready, c + 1)
                for k in range(TC):
                    last = mm(ps[:, 7, E1 * (TC * c + k):E1 * (TC * c + k + 1)],
                              contT[:, CW * c + P * k:CW * c + P * (k + 1)], wr1[:], start=True, stop=True)
                last.then_inc(gate_psum, 1)

            encode(0)
            for c in range(NC):
                if c + 1 < NC:
                    encode(c + 1)
                contract(c)
                if c:
                    route(c - 1)
            route(NC - 1)

            def hidden1(c):
                for e in range(E1):
                    i = E1 * c + e
                    if i >= 2:
                        pe.wait_ge(hh_act, i - 1)
                    mm(bank(i % 2), w11[:, HID1 * e:HID1 * (e + 1)], contT[:, CW * c:CW * (c + 1)],
                       start=True, stop=True).then_inc(hh_psum, 1)

            def output1(c):
                pe.wait_ge(hh_act, E1 * (c + 1))
                for k in range(TC):
                    y = TC * c + k
                    if y >= 2:
                        pe.wait_ge(yy_read, y - 1)
                    for e in range(E1):
                        last = mm(ps[:, 2 + y % 2, M1 * e:M1 * (e + 1)], hbuf1[:, e, P * k:P * (k + 1)], w21[:, e, :],
                                  start=True, stop=True)
                    last.then_inc(yy_psum, 1)
                if c:
                    pe.wait_ge(eo_ready, c)
                for k in range(TC):
                    last = mm(ps[:, 4, M1 * k:M1 * (k + 1)], wT1[:, CW * c + P * k:CW * c + P * (k + 1)], b21[:],
                              start=True, stop=True)
                last.then_inc(yb_psum, 1)

            def expand1(c):
                pe.wait_ge(eo_ready, c + 1)
                if c:
                    pe.wait_ge(dec_ready, c)
                for k in range(TC):
                    last = tr(ps[0:M1, 5, P * k:P * (k + 1)], eo[:, c % 2, k, :], ident[:])
                last.then_inc(eoT_psum, 1)
                pe.wait_ge(eoT_ready, c + 1)
                for a in range(2):
                    mm(bank(6 + a), wc2s[:, P * a:P * (a + 1)], eoT[:, c % 2, :], start=True, stop=True)\
                      .then_inc(exp1_psum, 1)
                pe.wait_ge(exp1_act, 2 * (c + 1))
                for k in range(TC):
                    for a in range(2):
                        last = mm(ps[:, 5, P * k:P * (k + 1)], sp_e[:, c % 2, a, P * k:P * (k + 1)], wdec[:, a, :],
                                  start=(a == 0), stop=(a == 1))
                last.then_inc(dec_psum, 1)

            hidden1(0)
            turn_weights(1, E1, wT1)
            pe.wait_ge(wT_ready, NC + NC)
            output1(0)
            for c in range(1, NC):
                hidden1(c)
                output1(c)
                expand1(c - 1)
            expand1(NC - 1)

        @block.vector
        def _(dve):
            v = nc.vector
            self_n = [0]

            def link(ins):
                self_n[0] += 1
                ins.then_inc(dve_self, 1)
                dve.wait_ge(dve_self, self_n[0])

            def rsqrt(var):
                link(v.tensor_scalar(rs_v[:], var, EPS, None, ALU.add))
                link(v.tensor_single_scalar(rs_i[:], rs_v[:].bitcast(I32), 1, op=ALU.logical_shift_right))
                link(v.tensor_scalar(rs_y[:].bitcast(I32), rs_i[:], -1.0, MAGIC, ALU.mult, ALU.add))
                for _ in range(3):
                    link(v.scalar_tensor_tensor(rs_t[:], rs_y[:], -0.5, rs_y[:], ALU.mult, ALU.mult))
                    link(v.tensor_tensor(rs_t[:], rs_t[:], rs_v[:], ALU.mult))
                    link(v.scalar_tensor_tensor(rs_y[:], rs_t[:], 1.5, rs_y[:], ALU.add, ALU.mult))

            def moments(src, c):
                for k in range(TC):
                    last = v.bn_stats(stats[:, TC * c + k, :], src(k))
                link(last)
                for k in range(TC):
                    last = v.bn_aggr(meanvar[:, TC * c + k, :], stats[:, TC * c + k, :])
                link(last)
                rsqrt(meanvar[:, TC * c:TC * (c + 1), 1])

            def ln(L, second, c):
                m = NC * ln_pass(L, second) + c
                moments(lambda k: x[:, TC * c + k, :], c)
                if m >= 2:
                    dve.wait_ge(ln_psum, m - 1)
                for k in range(TC):
                    last = v.tensor_scalar(xn[:, m % 2, k, :], x[:, TC * c + k, :], meanvar[:, TC * c + k, 0:1],
                                           rs_y[:, k:k + 1], ALU.subtract, ALU.mult)
                last.then_inc(xn_ready, 1)

            def remainder(L, n, src):
                dve.wait_ge(p1_ready[L], n + 1)
                v.tensor_tensor(r1[L][:, n % 4, :], src, pp[L][:, n % 4, 0, :], ALU.subtract).then_inc(r1_ready[L], 1)

            def third_part(L, n):
                dve.wait_ge(p2_ready[L], n + 1)
                v.tensor_tensor(pp[L][:, n % 4, 2, :], r1[L][:, n % 4, :], pp[L][:, n % 4, 1, :], ALU.subtract)\
                 .then_inc(split_done[L], 1)

            def norm_max(L, c, us=range(2)):
                for u in us:
                    dve.wait_ge(nrm_psum, 2 * NC * L + 2 * c + u + 1)
                    v.tensor_reduce(nmx[:, L, u, c:c + 1], bank(7), AX, ALU.max).then_inc(nrm_read, 1)

            def project0(c):
                for u in range(2):
                    remainder(0, 2 * c + u, q32[0][:, c % 2, u, :])
                dve.wait_ge(v_psum[0], c + 1)
                v.tensor_tensor(vall[:, TC * c:TC * (c + 1), :], tile4(3 * (c % 2) + 2),
                                bvrow[:].unsqueeze(1).to_broadcast([P, TC, D]), ALU.add).then_inc(v_ready[0], 1)
                for u in range(2):
                    third_part(0, 2 * c + u)
                norm_max(0, c)

            def layer1_step(j, c):
                four = range(4 * c, 4 * c + 4)
                if j == -1:
                    ln(1, 0, c)
                elif j == 4:
                    far = DECAY * (CW * c - S // 2)
                    for n in four:
                        u, d = n % 2, (n // 2) % 2
                        if d == 0:
                            dve.wait_ge(q32_ready, 2 * NC + 2 * c + u + 1)
                        sign = d ^ u
                        v.scalar_tensor_tensor(w32[:, n % 4, :], q32[1][:, c % 2, u, :],
                                               float(np.exp(far if sign else -far)), dup[:, sign, :],
                                               ALU.mult, ALU.mult).then_inc(w32_ready, 1)
                    dve.wait_ge(v_psum[1], c + 1)
                    v.tensor_copy(vall[:, TC * c:TC * (c + 1), :], tile4(5)).then_inc(v_ready[1], 1)
                elif j == 6:
                    dve.wait_ge(w32_ready, 4 * c + 4)
                    for n in four:
                        remainder(1, n, w32[:, n % 4, :])
                    norm_max(1, c, [0])
                elif j == 8:
                    for n in four:
                        third_part(1, n)
                    norm_max(1, c, [1])

            def decide(L):
                dve.wait_ge(nrm_read, 2 * NC * L + 2 * NC)
                link(v.tensor_reduce(pm[:, 2:4], nmx[:, L, :, :], AX, ALU.max))
                if L == 1:
                    link(v.memset(pm[:, 1:2], 0.0))
                link(v.scalar_tensor_tensor(pm[:, 0:1], pm[:, 2:3], 1.0 / SCORE_LIMIT ** 2, pm[:, 3:4], ALU.mult, ALU.mult))
                v.tensor_tensor(pm[:, 0:1], pm[:, 0:1], pm[:, 1:2], ALU.max).then_inc(pm_ready, 1)
                dve.wait_ge(pmT_psum, L + 1)
                link(v.tensor_reduce(flagf[0:1, L:L + 1], ps[0:1, 7, 0:P], AX, ALU.max))
                dve.wait_ge(group_ready[L], 1)
                v.tensor_single_scalar(flag[0:1, L:L + 1], flagf[0:1, L:L + 1], 1.0, op=ALU.is_le)\
                 .then_inc(flag_ready, 1)

            def fast(L):
                def fix(g, p_, gi):
                    qc, kb = groups[gi]
                    f = fix_of(L, qc, kb)
                    if not f:
                        return
                    for pair in range(2):
                        step = 2 * gi + pair
                        b = 2 * ((NSTEP * p_ + step) % SCORE_BUFS)
                        dve.wait_ge(scores_psum[L], g * NSTEP + (step + 1))
                        s_ = ps[:, b:b + 2, P * f[0]:P * f[1]]
                        if L == 0:
                            a = TC * qc + f[0] - kb + 1
                            other = tb0[:, p_, 2 * pair:2 * pair + 2, P * a:P * (a + f[1] - f[0])]
                        else:
                            other = dtri[:].unsqueeze(1).to_broadcast([P, 2, P])
                        v.tensor_tensor(s_, s_, other, (ALU.add, ALU.mult)[L]).then_inc(fixed[L], 1)

                def copy_out(g, qc):
                    dve.wait_ge(av_done[L], g * NGRP + (AV0 + NT * (qc + 1)))
                    v.tensor_copy(ot[L][:], bank(6 + qc % 2)).then_inc(acc_copied[L], 1)

                def normalise(g, qc):
                    acc = ps[:, 6 + qc % 2, :].rearrange("p (t h w) -> p t h w", t=TC, h=GH)
                    o_ = onorm[:, qc % 2, :, :]
                    dve.wait_ge(accT_psum[L], g * NC + (qc + 1))
                    v.reciprocal(o_, acc[:, :, :, DK]).then_inc(den_ready[L], 1)
                    dve.wait_ge(den_ready[L], g * NC + (qc + 1))
                    dst = ao[:, TC * qc:TC * (qc + 1), bass.ds(g * (GH * DK), GH * DK)]
                    v.tensor_tensor(dst.rearrange("p t (h d) -> p t h d", h=GH), acc[:, :, :, 0:DK],
                                    o_.unsqueeze(3).to_broadcast([P, TC, GH, DK]), ALU.mult).then_inc(acc_free[L], 1)

                with dve.Fori(0, NG // 2) as i:
                    for k in range(2 * NGRP):
                        p_, gi = divmod(k, NGRP)
                        if L == 0 and gi == 0:
                            dve.wait_ge(k_loaded[0][p_], i * KLOADS[0] + KLOADS[0])
                        fix(2 * i + p_, p_, gi)
                        if k > NT and k % NT in (COPY_AT, NORM_AT):
                            p_, qc = divmod(k // NT - 1, NC)
                            (copy_out if k % NT == COPY_AT else normalise)(2 * i + p_, qc)
                    copy_out(2 * i + 1, NC - 1)
                    normalise(2 * i + 1, NC - 1)
                dve.wait_ge(acc_free[L], ACC0 + NC * NG)

            def general(L):
                q_, qt_, row_, pt_, st = ((g_q, g_qt, g_s, g_pt, g_m), (h_q, h_qt, h_s, h_pt, h_st))[L]
                nload = 48 if L == 0 else 32
                ops = 2 if L == 0 else 8
                if L == 1:
                    dve.wait_ge(g_strip_ready[1], 3)
                with dve.Fori(0, H) as h:
                    if L == 0:
                        lo = P * (NT - 2)
                        dve.wait_ge(g_tbT, h + 1)
                        v.tensor_copy(g_strip[:, lo:lo + BAND], ps[:, 4, 0:BAND])
                        v.tensor_copy(g_strip[:, 0:lo], crow[:, 1, bass.ds(h, 1)].to_broadcast([P, lo]))
                        v.tensor_copy(g_strip[:, lo + BAND:], crow[:, 0, bass.ds(h, 1)].to_broadcast([P, lo]))\
                         .then_inc(g_strip_ready[0], 1)
                    with dve.Fori(0, NT) as q:
                        n = h * NT + q
                        done = [0]

                        def then(ins):
                            done[0] += 1
                            ins.then_inc(g_dv[L], 1)
                            dve.wait_ge(g_dv[L], n * ops + done[0])

                        strip = (g_strip, h_strip)[L][:, bass.ds(q * -P + (NT - 1) * P, S)]
                        dve.wait_ge(g_load[L], h * nload + nload)
                        v.tensor_copy(qt_[:], q_[:, bass.ds(q * P, P)]).then_inc(g_q_ready[L], 1)
                        dve.wait_ge(g_sc[L], n + 1)
                        scored = ps[:, 0:4, :].rearrange("p a b -> p (a b)")
                        if L == 0:
                            dve.wait_ge(g_strip_ready[0], h + 1)
                            then(v.tensor_tensor(row_[:], scored, strip, ALU.add))
                        else:
                            then(v.tensor_copy(row_[:], scored))
                            then(v.tensor_tensor(h_m[:], row_[:], row_[:], ALU.is_equal))
                            then(v.tensor_scalar(row_[:], row_[:], CLAMP, -CLAMP, ALU.min, ALU.max))
                            then(v.memset(h_r[:], -CLAMP))
                            v.memset(marks[0:1, 11:12], 0.0)
                            then(v.copy_predicated(h_r[:], h_m[:].bitcast(I32), row_[:]))
                            then(v.tensor_tensor(row_[:], h_r[:], strip, ALU.mult))
                            then(v.tensor_scalar(row_[:], row_[:], CLAMP, -CLAMP, ALU.min, ALU.max))
                        then(v.tensor_reduce(st[:, 0:1], row_[:], AX, ALU.max))
                        v.tensor_scalar(st[:, 1:2], st[:, 0:1], -1.0, None, ALU.mult).then_inc(g_max[L], 1)
                        dve.wait_ge(g_tp[L], n + 1)
                        v.tensor_copy(pt_[:], ps[:, 4:8, :].rearrange("p a b -> p (a b)")).then_inc(g_tc[L], 1)
                        dve.wait_ge(g_av[L], n + 1)
                        v.reciprocal(st[:, 3:4], st[:, 2:3]).then_inc(den_ready[L], 1)
                        dve.wait_ge(den_ready[L], n + 1)
                        v.tensor_scalar(ao[:, bass.ds(q, 1), bass.ds(h * DK, DK)].rearrange("p a d -> p (a d)"),
                                        ps[:, 0, 0:DK], st[:, 3:4], None, ALU.mult).then_inc(g_fin[L], 1)
                dve.wait_ge(g_fin[L], GEN0 + H * NT)

            def attend(L):
                fv = None
                dve.wait_ge(flag_ready, L + 1)
                fv = dve.value_load(flag[0:1, L:L + 1])
                with dve.If(fv > 0):
                    fast(L)
                with dve.Else():
                    general(L)
                v.memset(marks[0:1, 9 + L:10 + L], 0.0).then_inc(ao_ready, 1)

            def projected(L):
                def scaled(c):
                    dve.wait_ge(y_psum, NC * L + c + 1)
                    if c >= 2:
                        dve.wait_ge(yback_psum, NC * L + c - 1)
                    if L == 0:
                        ins = v.tensor_scalar(yT[0][:, c % 2, :], bank(4 + c % 2), bqk[:, 2:3], mod[:, 0, 2:3],
                                              ALU.add, ALU.mult)
                    else:
                        ins = v.tensor_scalar(yT[1][:, c % 2, :], bank(4 + c % 2), mod[:, 1, 2:3], None, ALU.mult)
                    ins.then_inc(yT_ready, 1)

                def add(c):
                    dve.wait_ge(yback_psum, NC * L + c + 1)
                    xc = x[:, TC * c:TC * (c + 1), :]
                    v.tensor_tensor(xc, xc, tile4(c), ALU.add).then_inc(x_added, 1)
                    dve.wait_ge(x_added, NC * L + c + 1)
                    ln(L, 1, c)

                scaled(0)
                scaled(1)
                add(0)
                scaled(2)
                add(1)
                scaled(3)
                add(2)
                add(3)

            def top2(c16, L):
                for k in range(NT):
                    v.max(mx8[:, k, :], gts[:, k, :])
                link(v.memset(wgt[:, :, 8:10], 1.0 if L else 1.0 / SH0))
                for k in range(NT):
                    last = v.max_index(ix8[:, k, :], mx8[:, k, :], gts[:, k, :])
                link(last)
                link(v.tensor_copy(ixf[:], ix8[:, :, 0:2]))

            def place(L):
                def wide(a):
                    return a.unsqueeze(2).to_broadcast([P, NT, 8])

                io = iota_e[:].unsqueeze(1).to_broadcast([P, NT, 8])
                v.tensor_tensor(eq1[:], io, wide(ixf[:, :, 0]), ALU.is_equal)
                link(v.tensor_tensor(eq2[:], io, wide(ixf[:, :, 1]), ALU.is_equal))
                v.tensor_tensor(eq1[:], eq1[:], wide(gsm[:, :, 2]), ALU.mult)
                link(v.tensor_tensor(eq2[:], eq2[:], wide(gsm[:, :, 3]), ALU.mult))
                v.tensor_tensor(wgt[:, :, 0:8], eq1[:], eq2[:], ALU.add).then_inc(w_ready, 1)

            def copy_weights(L, n, dst):
                for c in range(NC):
                    dve.wait_ge(wT_psum, NC * L + c + 1)
                    v.tensor_copy(dst[:, CW * c:CW * (c + 1)], ps[0:n, 6 + c % 2, :]).then_inc(wT_ready, 1)

            link(v.memset(pm[:], 0.0))
            dve.wait_ge(silu_exp, 1)
            link(v.tensor_scalar(silu[:], cexp[:], 1.0, None, ALU.add))
            link(v.reciprocal(cexp[:], silu[:]))
            link(v.tensor_tensor(silu[:], cexp[:], ccol[:], ALU.mult))
            v.tensor_copy(silub[:], silu[:].unsqueeze(2).to_broadcast([P, 2, P])).then_inc(silu_done, 1)
            dve.wait_ge(consts, 1)
            dve.wait_ge(decays, 2)
            v.tensor_scalar(dtri[:], dtri[:], 0.0, None, ALU.min).then_inc(decays, 1)
            dve.wait_ge(ld_x[0], 16)
            dve.wait_ge(mod_psum, 1)
            link(v.tensor_copy(mod[:], ps[:, 7, 0:12].rearrange("p (a b) -> p a b", a=2)))
            link(v.tensor_scalar(mod[:, :, 1:5:3], mod[:, :, 1:5:3], 1.0, None, ALU.add))
            v.tensor_scalar(gatesgn[:], mod[:, :, 2], 0.0, 2.0, ALU.is_ge, ALU.mult)
            link(v.scalar_tensor_tensor(gateabs[:], mod[:, :, 2], -1.0, mod[:, :, 2], ALU.mult, ALU.max))
            link(v.tensor_scalar(gateabs[:], gateabs[:], 0.25, None, ALU.max))
            link(v.scalar_tensor_tensor(mod[:, :, 2], gatesgn[:], -1.0, gateabs[:], ALU.add, ALU.mult))
            link(v.tensor_copy(gbrow[:], ps[:, 6, 0:2 * D].rearrange("p (a b) -> p a b", a=2)))
            link(v.tensor_scalar(gbsgn[:], gbrow[:], 0.0, 2.0, ALU.is_ge, ALU.mult))
            link(v.scalar_tensor_tensor(gbrow[:], gbrow[:], -1.0, gbrow[:], ALU.mult, ALU.max))
            link(v.tensor_scalar(gbrow[:], gbrow[:], 0.25, None, ALU.max))
            link(v.scalar_tensor_tensor(gbrow[:], gbsgn[:], -1.0, gbrow[:], ALU.add, ALU.mult))
            dve.wait_ge(ld_att0, 16 * 5)
            v.tensor_scalar(bqs[:], bqk[:, 0:1], SCALE[0], None, ALU.mult).then_inc(mod_done, 1)
            dve.wait_ge(relT_psum, 1)
            link(v.tensor_copy(relv[:, P - 1:P + 2 * REL], ps[0:H, 5, 0:2 * REL + 1]))
            v.tensor_copy(relv[:, 0:P - 1], relv[:, P - 1:P].to_broadcast([H, P - 1]))
            v.tensor_copy(relv[:, P + 2 * REL:], relv[:, P + 2 * REL - 1:P + 2 * REL].to_broadcast([H, TROW - P - 2 * REL]))\
             .then_inc(relv_ready, 1)
            link(v.tensor_tensor(relsq[:], relf[:], relf[:], ALU.mult))
            link(v.tensor_reduce(flagr[:], relsq[:], AX, ALU.max))
            link(v.tensor_scalar(pm[0:H, 1:2], flagr[:], 1.0 / BIAS_LIMIT ** 2, None, ALU.mult))
            ln(0, 0, 0)

            def bias_rows():
                link(v.tensor_scalar(rp[:, 1:2], rp[:, 0:1], float(NT), None, ALU.is_ge))
                link(v.tensor_scalar(rp[:, 2:3], rp[:, 0:1], 2.0 * NT, None, ALU.is_ge))
                link(v.scalar_tensor_tensor(rp[:, 3:4], rp[:, 1:2], -float(NT), rp[:, 0:1], ALU.mult, ALU.add))
                link(v.scalar_tensor_tensor(rp[:, 3:4], rp[:, 2:3], -float(NT), rp[:, 3:4], ALU.mult, ALU.add))
                link(v.tensor_scalar(rp[:, 4:6], rp[:, 1:3], -1.0, None, ALU.mult))
                v.tensor_scalar(mhi[:], kbi[:], rp[:, 3:4], -2.0, ALU.subtract, ALU.is_le)
                v.tensor_scalar(mlo[:], kbi[:], rp[:, 3:4], 2.0, ALU.subtract, ALU.is_ge)
                link(v.tensor_scalar(oneh[:], kbi[:], rp[:, 3:4], 0.0, ALU.subtract, ALU.is_equal))
                v.tensor_copy(onehw[:].rearrange("p (k n) -> p k n", n=P),
                              oneh[:].unsqueeze(2).to_broadcast([BIAS_ROWS, NT, P])).then_inc(onehw_ready, 1)
                cr = crow[0:BIAS_ROWS]
                link(v.tensor_copy(cpa[:], cr))
                link(v.scalar_tensor_tensor(cpb[:], cpa[:], rp[:, 4:5], cr, ALU.mult, ALU.add))
                link(v.tensor_copy(cpc[:], cpb[:]))
                link(v.scalar_tensor_tensor(cpd[:], cpc[:], rp[:, 5:6], cpb[:], ALU.mult, ALU.add))

                def over_heads(a):
                    return a.unsqueeze(1).to_broadcast([BIAS_ROWS, H, NT])

                def over_tiles(a):
                    return a.unsqueeze(2).to_broadcast([BIAS_ROWS, H, NT])

                v.tensor_tensor(ktab[:], over_heads(mhi[:]), over_tiles(cpd[:, 1, :]), ALU.mult)
                link(v.tensor_tensor(ktab2[:], over_heads(mlo[:]), over_tiles(cpd[:, 0, :]), ALU.mult))
                v.tensor_tensor(ktab[:], ktab[:], ktab2[:], ALU.add).then_inc(ktab_ready, 1)

            for c in range(NC):
                if c + 1 < NC:
                    dve.wait_ge(ld_x[c + 1], 16)
                    ln(0, 0, c + 1)
                project0(c)
                if c == 0:
                    bias_rows()
            decide(0)
            attend(0)
            projected(0)

            dve.wait_ge(gate_psum, NC)
            link(v.tensor_tensor(gts[:], ps[:, 7, 0:NT * E0].rearrange("p (a b) -> p a b", b=E0),
                                 rb0[:].unsqueeze(1).to_broadcast([P, NT, E0]), ALU.add))
            top2(0, 0)
            v.tensor_tensor(gsm[:, :, 0], mx8[:, :, 1], mx8[:, :, 0], ALU.subtract).then_inc(gate_d, 1)
            dve.wait_ge(gate_e, 1)
            link(v.tensor_scalar(gsm[:, :, 0], gsm[:, :, 1], 1.0, None, ALU.add))
            link(v.reciprocal(gsm[:, :, 2], gsm[:, :, 0]))
            link(v.tensor_tensor(gsm[:, :, 3], gsm[:, :, 1], gsm[:, :, 2], ALU.mult))
            place(0)
            copy_weights(0, E0 + SH0, wT0)
            for c in range(NC):
                for j in range(1, len(order0)):
                    n = len(order0) * c + j
                    y = y_index(n)
                    dve.wait_ge(y0_psum, y + 1)
                    if y:
                        dve.wait_ge(y0_read, y)
                    if j == 1:
                        xc = x[:, TC * c:TC * (c + 1), :]
                        last = v.tensor_tensor(xc, xc, tile4(3 + y % 2), ALU.add)
                    else:
                        e = order0[j]
                        for k in range(TC):
                            xt = x[:, TC * c + k, :]
                            last = v.scalar_tensor_tensor(xt, ps[:, 3 + y % 2, P * k:P * (k + 1)],
                                                          wgt[:, TC * c + k, e:e + 1], xt, ALU.mult, ALU.add)
                    last.then_inc(y0_read, 1)
                    if c:
                        layer1_step(j, c - 1)
                dve.wait_ge(y0_read, (E0 + 1) * (c + 1))
                layer1_step(-1, c)
            for j in range(len(order0)):
                layer1_step(j, NC - 1)
            decide(1)
            attend(1)
            projected(1)

            link(v.memset(contT[M1:, :], 1.0))
            link(v.memset(eoT[M1:, :, :], 1.0))
            dve.wait_ge(ld_ffn1, 16 * 16)
            for c in range(NC):
                dve.wait_ge(cont_psum, c + 1)
                v.tensor_scalar(contT[0:M1, CW * c:CW * (c + 1)], ps[0:M1, 4 + c % 2, :], bs2c[:, 0:1], None, ALU.add)\
                 .then_inc(cont_ready, 1)
            v.tensor_tensor(lngr[:], lngr[:], gbrow[:, 1, :], ALU.mult)
            link(v.tensor_tensor(lnbr[:], lnbr[:], gbrow[:, 1, :], ALU.mult))
            link(v.tensor_tensor(x[:], x[:], lnbr[:].unsqueeze(1).to_broadcast([P, NT, D]), ALU.add))
            dve.wait_ge(gate_psum, NC + NC)
            logits = ps[:, 7, 0:NT * E1].rearrange("p (a b) -> p a b", b=E1)

            def over(a):
                return a.unsqueeze(2).to_broadcast([P, NT, E1])

            link(v.tensor_reduce(gsm[:, :, 0], logits, AX, ALU.max))
            v.tensor_tensor(gts[:], logits, over(gsm[:, :, 0]), ALU.subtract).then_inc(gate_d, 1)
            dve.wait_ge(gate_e, 1 + 1)
            link(v.tensor_reduce(gsm[:, :, 1], gts[:], AX, ALU.add))
            link(v.reciprocal(gsm[:, :, 0], gsm[:, :, 1]))
            link(v.tensor_tensor(gts[:], gts[:], over(gsm[:, :, 0]), ALU.mult))
            top2(0, 1)
            link(v.tensor_tensor(gsm[:, :, 0], mx8[:, :, 0], mx8[:, :, 1], ALU.add))
            link(v.reciprocal(gsm[:, :, 1], gsm[:, :, 0]))
            v.tensor_tensor(gsm[:, :, 2], mx8[:, :, 0], gsm[:, :, 1], ALU.mult)
            link(v.tensor_tensor(gsm[:, :, 3], mx8[:, :, 1], gsm[:, :, 1], ALU.mult))
            place(1)
            copy_weights(1, E1, wT1)

            def gather1(c):
                for k in range(TC):
                    y = TC * c + k
                    dve.wait_ge(yy_psum, y + 1)
                    v.tensor_tensor(ymul[:, k % 2, :, :], ps[:, 2 + y % 2, :].rearrange("p (e m) -> p e m", e=E1),
                                    wgt[:, y, 0:E1].unsqueeze(2).to_broadcast([P, E1, M1]), ALU.mult).then_inc(yy_read, 1)
                    dve.wait_ge(yy_read, y + 1)
                    if c >= 2 and k == 0:
                        dve.wait_ge(eoT_psum, c - 1)
                    last = v.tensor_reduce(eo[:, c % 2, k, :], ymul[:, k % 2, :, :].rearrange("p e m -> p m e"), AX, ALU.add)
                link(last)
                dve.wait_ge(yb_psum, c + 1)
                v.tensor_tensor(eo[:, c % 2, :, :], eo[:, c % 2, :, :],
                                ps[:, 4, 0:TC * M1].rearrange("p (t m) -> p t m", t=TC), ALU.add).then_inc(eo_ready, 1)

            def finish1(c):
                dve.wait_ge(dec_psum, c + 1)
                d_ = dec[:, c % 2, :, :]
                v.tensor_tensor(d_, tile4(5), bdec[:].unsqueeze(1).to_broadcast([P, TC, D]), ALU.add)\
                 .then_inc(dec_ready, 1)
                dve.wait_ge(dec_ready, c + 1)
                moments(lambda k: dec[:, c % 2, k, :], c)
                for k in range(TC):
                    last = v.tensor_scalar(dec[:, c % 2, k, :], dec[:, c % 2, k, :], meanvar[:, TC * c + k, 0:1],
                                           rs_y[:, k:k + 1], ALU.subtract, ALU.mult)
                link(last)
                link(v.tensor_tensor(d_, d_, lngr[:].unsqueeze(1).to_broadcast([P, TC, D]), ALU.mult))
                v.tensor_tensor(fo[:, c, :, :], d_, x[:, TC * c:TC * (c + 1), :], ALU.add).then_inc(fo_ready, 1)

            for c in range(NC):
                gather1(c)
                if c:
                    finish1(c - 1)
            finish1(NC - 1)


def kernel(**inputs):
    import concourse.bacc as bacc
    from concourse.bass_utils import run_bass_kernel_spmd

    nc = bacc.Bacc("TRN2", target_bir_lowering=False, num_devices=1)
    arrays, args = {}, {}
    for name, a in inputs.items():
        a = np.ascontiguousarray(a)
        arrays[f"in_{name}_dram"] = a
        args[name] = nc.dram_tensor(f"in_{name}_dram", a.shape, mybir.dt.from_np(a.dtype), kind="ExternalInput").ap()
    out = nc.dram_tensor("out_0_dram", (1, S, D), F32, kind="ExternalOutput").ap()
    adaln_two_layers(nc, args, out)
    r = run_bass_kernel_spmd(nc, [arrays], core_ids=[0])
    return r.results[0]["out_0_dram"]
```

```python
from contextlib import ExitStack

import numpy as np

import concourse.bass as bass
from concourse import mybir

P = 128
S = 2048
D = 128
H = 16
DK = D // H
NT = S // P
CW = 512
NC = S // CW
TC = CW // P
GH = 4
NG = H // GH
VW = 32
REL = 128
E0, HID0, SH0 = 8, 512, 2
E1, HID1, M1, ENC1 = 8, 128, 64, 256
KT0 = HID0 // P
BIAS_ROWS = 3 * NT
PARTS = 3
QK_ROWS = PARTS * PARTS * DK
EPS = 1e-5
DECAY = 0.01 * 0.01
CLAMP = 10000.0
SCALE = (1.0 / float(np.sqrt(np.float32(DK))), 1.0 / (float(np.sqrt(np.float32(D))) + 1e-8))
SCORE_LIMIT = 40.0
BIAS_LIMIT = 20.0
MAGIC = 1597463007.0
BAND = 3 * P
STRIP = (2 * NT - 1) * P
TROW = 512

F32 = mybir.dt.float32
BF16 = mybir.dt.bfloat16
I32 = mybir.dt.int32
U32 = mybir.dt.uint32
ALU = mybir.AluOpType
ACT = mybir.ActivationFunctionType
AX = mybir.AxisListType.X

NSTEP = 2 * NT * NC
NGRP = NT * NC
SCORE_BUFS = 3
PROB_BUFS = 3
EXP0 = SCORE_BUFS + 1
AV0 = 2 * NGRP
ACC0 = 2
GEN0 = 1
LAG = 2
PROJ_AT = (9, 11, 13)
EARLY = NC - 1
TURN_AT, COPY_AT, NORM_AT = 5, 3, 7
HB = 3


def last_use(k, bufs, n):
    return k - bufs if k >= bufs else max(j for j in range(n) if j % bufs == k) - n


def adaln_two_layers(nc, t, out):
    with ExitStack() as ctx:
        names = set()

        def sb(name, shape, dt=F32, scope=ctx):
            return scope.enter_context(nc.sbuf_tensor("sb_" + name, shape, dt))

        def sem(name):
            assert name not in names
            names.add(name)
            return ctx.enter_context(nc.semaphore(name))

        ctx.enter_context(nc.allow_non_contiguous_dma(reason="small vectors, one element a partition"))
        ps = ctx.enter_context(nc.psum_tensor("ps", [P, 8, CW], F32))

        x = sb("x", [P, NT, D])
        hT = sb("hT", [P, S])
        ao = sb("ao", [P, NT, D])
        oT = sb("oT", [P, CW])
        yT = sb("yT", [P, CW])
        vall = sb("vall", [P, NT, D])
        ident = sb("ident", [P, P])
        headones = sb("headones", [P, P], BF16)
        ccol = sb("ccol", [P, 2])
        cexp = sb("cexp", [P, 2])
        silu = sb("silu", [P, 2])
        silub = sb("silub", [P, 2, P])
        mod = sb("mod", [P, 2, 6])
        gatesgn = sb("gatesgn", [P, 2])
        gateabs = sb("gateabs", [P, 2])
        gbrow = sb("gbrow", [P, 2, P])
        gbsgn = sb("gbsgn", [P, 2, P])
        stats = sb("stats", [P, NT, 6])
        meanvar = sb("meanvar", [P, NT, 2])
        rs_v = sb("rs_v", [P, TC])
        rs_i = sb("rs_i", [P, TC], I32)
        rs_y = sb("rs_y", [P, TC])
        rs_t = sb("rs_t", [P, TC])
        xn = sb("xn", [P, 2, TC, P])
        onorm = sb("onorm", [P, 2, TC, GH])
        nmx = sb("nmx", [P, 2, 2, NC])
        pm = sb("pm", [P, 4])
        flagf = sb("flagf", [1, 4])
        flagr = sb("flagr", [H, 1])
        flag = sb("flag", [1, 2], I32)
        iota_e = sb("iota_e", [P, 8])
        iota_p = sb("iota_p", [PARTS * E1, 4])
        sel8 = sb("sel8", [PARTS * E1, E1])
        sel1 = sb("sel1", [PARTS * E1, E1, P], BF16)
        dup = sb("dup", [P, 2, CW])
        dtri = sb("dtri", [P, P])
        marks = sb("marks", [1, 16])
        wqkv = sb("wqkv", [P, 3 * D])
        wout0 = sb("wout0", [P, D])
        bqk = sb("bqk", [P, 3])
        bqs = sb("bqs", [P, 1])
        bvrow = sb("bvrow", [P, D])
        wq1 = sb("wq1", [P, D])
        wk1 = sb("wk1", [P, D])
        wv1 = sb("wv1", [P, D])
        wo1 = sb("wo1", [P, D])
        wdn1 = sb("wdn1", [P, 32])
        wup1 = sb("wup1", [32, 2, D])
        crow = sb("crow", [P, 2, H])
        mx8 = sb("mx8", [P, NT, 8])
        ix8 = sb("ix8", [P, NT, 8], U32)
        ixf = sb("ixf", [P, NT, 2])
        gts = sb("gts", [P, NT, 8])
        gsm = sb("gsm", [P, NT, 4])
        eq1 = sb("eq1", [P, NT, 8])
        eq2 = sb("eq2", [P, NT, 8])
        wgt = sb("wgt", [P, NT, 10])
        with ExitStack() as a0:
            w10 = sb("w10", [P, E0 + SH0, HID0], scope=a0)
            w20 = sb("w20", [P, E0 + SH0, KT0, D], scope=a0)
            b10 = sb("b10", [P, E0 + SH0, KT0], scope=a0)
            b20 = sb("b20", [E0 + SH0, D], scope=a0)
            rw0 = sb("rw0", [P, E0], scope=a0)
            rb0 = sb("rb0", [P, E0], scope=a0)
            rp = sb("rp", [BIAS_ROWS, 8], scope=a0)
            cpa = sb("cpa", [BIAS_ROWS, 2, H], BF16, scope=a0)
            cpb = sb("cpb", [BIAS_ROWS, 2, H], scope=a0)
            cpc = sb("cpc", [BIAS_ROWS, 2, H], BF16, scope=a0)
            cpd = sb("cpd", [BIAS_ROWS, 2, H], BF16, scope=a0)
            kbi = sb("kbi", [BIAS_ROWS, NT], scope=a0)
            mhi = sb("mhi", [BIAS_ROWS, NT], scope=a0)
            mlo = sb("mlo", [BIAS_ROWS, NT], scope=a0)
            oneh = sb("oneh", [BIAS_ROWS, NT], scope=a0)
            onehw = sb("onehw", [BIAS_ROWS, S], BF16, scope=a0)
            ktab = sb("ktab", [BIAS_ROWS, H, NT], scope=a0)
            ktab2 = sb("ktab2", [BIAS_ROWS, H, NT], scope=a0)
            with ExitStack() as s0:
                relt = sb("relt", [P, 3, H], scope=s0)
                relf = sb("relf", [H, 2 * REL + 1], scope=s0)
                relsq = sb("relsq", [H, 2 * REL + 1], scope=s0)
                relv = sb("relv", [H, TROW], scope=s0)
                wmod_sb = [sb(f"wmod{L}", [P, 6 * D], scope=s0) for L in range(2)]
                q32_0 = sb("q32_0", [P, 2, 2, CW], scope=s0)
                sq_0 = sb("sq_0", [P, 2, 2, CW], BF16, scope=s0)
                r1_0 = sb("r1_0", [P, 4, CW], scope=s0)
                pp_0 = sb("pp_0", [P, 4, PARTS, CW], BF16, scope=s0)
            with ExitStack() as s0:
                pr0 = sb("pr0", [P, PROB_BUFS, 2, 2, CW], scope=s0)
                tb0 = sb("tb0", [P, 2, GH, BAND], scope=s0)
                ot0 = sb("ot0", [P, CW], scope=s0)
                qst0 = sb("qst0", [P, 2, 1, GH, CW], BF16, scope=s0)
                kst0 = sb("kst0", [P, 2, 1, GH, S], BF16, scope=s0)
                vh0 = sb("vh0", [P, 2, NT, GH, VW], scope=s0)
            with ExitStack() as s0:
                hbuf0 = sb("hbuf0", [P, HB, KT0, CW], scope=s0)
                wT0 = sb("wT0", [E0 + SH0, S], scope=s0)
                q32_1 = sb("q32_1", [P, 2, 2, CW], scope=s0)
                sq_1 = sb("sq_1", [P, 2, 2, CW], BF16, scope=s0)
                lat = sb("lat", [32, 2, CW], scope=s0)
                w32 = sb("w32", [P, 4, CW], scope=s0)
                r1_1 = sb("r1_1", [P, 4, CW], scope=s0)
                pp_1 = sb("pp_1", [P, 4, PARTS, CW], BF16, scope=s0)
                kv32 = sb("kv32", [P, 2, CW], scope=s0)
            with ExitStack() as s0:
                g_k = sb("g_k", [DK, S], scope=s0)
                g_q = sb("g_q", [DK, S], scope=s0)
                g_qt = sb("g_qt", [DK, P], scope=s0)
                g_s = sb("g_s", [P, S], scope=s0)
                g_pt = sb("g_pt", [P, S], scope=s0)
                g_strip = sb("g_strip", [P, STRIP], scope=s0)
                g_tb = sb("g_tb", [P, BAND], scope=s0)
                g_m = sb("g_m", [P, 4], scope=s0)
        with ExitStack() as a1:
            wenc = sb("wenc", [P, ENC1], scope=a1)
            benc = sb("benc", [P, 2], scope=a1)
            ws2c = sb("ws2c", [P, 2, M1], scope=a1)
            bs2c = sb("bs2c", [M1, 1], scope=a1)
            wr1 = sb("wr1", [M1 + 1, E1], scope=a1)
            w11 = sb("w11", [M1 + 1, E1 * HID1], scope=a1)
            w21 = sb("w21", [P, E1, M1], scope=a1)
            b21 = sb("b21", [PARTS * E1, M1], scope=a1)
            wc2s = sb("wc2s", [2 * M1, ENC1], scope=a1)
            bc2s = sb("bc2s", [P, 2], scope=a1)
            wdec = sb("wdec", [P, 2, D], scope=a1)
            bdec = sb("bdec", [P, D], scope=a1)
            lngr = sb("lngr", [P, D], scope=a1)
            lnbr = sb("lnbr", [P, D], scope=a1)
            with ExitStack() as s1:
                vh1 = sb("vh1", [P, 2, NT, GH, VW], scope=s1)
                kst1 = sb("kst1", [P, 2, 2, GH, S], BF16, scope=s1)
                qst1 = sb("qst1", [P, 2, 2, GH, CW], BF16, scope=s1)
                pr1 = sb("pr1", [P, PROB_BUFS, 2, 2, CW], scope=s1)
                ot1 = sb("ot1", [P, CW], scope=s1)
            with ExitStack() as s1:
                sp_e = sb("sp_e", [P, 2, 2, CW], scope=s1)
                contT = sb("contT", [M1 + 1, S], scope=s1)
                wpart = sb("wpart", [P, NT, PARTS * E1], scope=s1)
                wpb = sb("wpb", [P, NT, E1], BF16, scope=s1)
                wT1 = sb("wT1", [PARTS * E1, S], scope=s1)
                wTb = sb("wTb", [PARTS * E1, S], BF16, scope=s1)
                rbuf1 = sb("rbuf1", [P, E1, CW], scope=s1)
                hbuf1 = sb("hbuf1", [P, 4, CW], scope=s1)
                eoT = sb("eoT", [2 * M1, 2, CW], scope=s1)
                dec = sb("dec", [P, 2, TC, D], scope=s1)
                fo = sb("fo", [P, NC, TC, D], scope=s1)
            with ExitStack() as s1:
                h_k = sb("h_k", [DK, S], scope=s1)
                h_q = sb("h_q", [DK, S], scope=s1)
                h_qt = sb("h_qt", [DK, P], scope=s1)
                h_s = sb("h_s", [P, S], scope=s1)
                h_m = sb("h_m", [P, S], scope=s1)
                h_r = sb("h_r", [P, S], scope=s1)
                h_pt = sb("h_pt", [P, S], scope=s1)
                h_strip = sb("h_strip", [P, STRIP], scope=s1)
                h_st = sb("h_st", [P, 4], scope=s1)
        q32, sq = (q32_0, q32_1), (sq_0, sq_1)
        r1, pp = (r1_0, r1_1), (pp_0, pp_1)

        qparts = [nc.dram_tensor(f"qparts{L}", (L + 1, PARTS, PARTS, D, S), BF16, kind="Internal").ap() for L in range(2)]
        kparts = [nc.dram_tensor(f"kparts{L}", (L + 1, H, PARTS, DK, S), BF16, kind="Internal").ap() for L in range(2)]
        qkf = [nc.dram_tensor(f"qkf{L}", (2, D, S), F32, kind="Internal").ap() for L in range(2)]
        relrows = nc.dram_tensor("relrows", (H, P, TROW), F32, kind="Internal").ap()

        Ls = range(2)
        ld_x = [sem(f"ld_x{c}") for c in range(NC)]
        ld_mod, ld_att0, ld_rel, ld_att1, ld_ffn0, ld_ffn1 = (sem(n) for n in (
            "ld_mod", "ld_att0", "ld_rel", "ld_att1", "ld_ffn0", "ld_ffn1"))
        consts = sem("consts")
        decays = sem("decays")
        silu_exp = sem("silu_exp")
        silu_done = sem("silu_done")
        mod_psum = sem("mod_psum")
        mod_done = sem("mod_done")
        gates_ready = sem("gates_ready")
        dve_self = sem("dve_self")
        pool_self = sem("pool_self")
        xn_ready = sem("xn_ready")
        ln_psum = sem("ln_psum")
        hT_ready = sem("hT_ready")
        relT_psum = sem("relT_psum")
        relv_ready = sem("relv_ready")
        relrows_stored = sem("relrows_stored")
        onehw_ready = sem("onehw_ready")
        ktab_ready = sem("ktab_ready")
        gb_folded = sem("gb_folded")
        qk_psum = sem("qk_psum")
        q32_ready = sem("q32_ready")
        kv_psum, kv_read = sem("kv_psum"), sem("kv_read")
        lat_psum, lat_ready = sem("lat_psum"), sem("lat_ready")
        v_psum = [sem(f"v_psum{L}") for L in Ls]
        v_ready = [sem(f"v_ready{L}") for L in Ls]
        w32_ready = sem("w32_ready")
        p1_ready = [sem(f"p1_ready{L}") for L in Ls]
        r1_ready = [sem(f"r1_ready{L}") for L in Ls]
        p2_ready = [sem(f"p2_ready{L}") for L in Ls]
        split_done = [sem(f"split_done{L}") for L in Ls]
        sq_ready = sem("sq_ready")
        nrm_psum = sem("nrm_psum")
        nrm_read = sem("nrm_read")
        parts_st = [[sem(f"parts_st{L}_{s}") for s in range(4)] for L in Ls]
        qkf_st = [[sem(f"qkf_st{L}_{s}") for s in range(4)] for L in Ls]
        pm_ready = sem("pm_ready")
        pmT_psum = sem("pmT_psum")
        flag_ready = sem("flag_ready")
        k_loaded = [[sem(f"k_loaded{L}_{p}") for p in range(2)] for L in Ls]
        k_late = [[sem(f"k_late{L}_{p}") for p in range(2)] for L in Ls]
        q_loaded = [[sem(f"q_loaded{L}_{p}") for p in range(2)] for L in Ls]
        group_ready = [sem(f"group_ready{L}") for L in Ls]
        scores_psum = [sem(f"scores_psum{L}") for L in Ls]
        fixed = [sem(f"fixed{L}") for L in Ls]
        exp_done = [sem(f"exp_done{L}") for L in Ls]
        av_done = [sem(f"av_done{L}") for L in Ls]
        acc_copied = [sem(f"acc_copied{L}") for L in Ls]
        accT_psum = [sem(f"accT_psum{L}") for L in Ls]
        den_ready = [sem(f"den_ready{L}") for L in Ls]
        acc_free = [sem(f"acc_free{L}") for L in Ls]
        g_load, g_strip_ready, g_q_ready, g_sc, g_max, g_exp, g_tp, g_tc, g_av, g_fin, g_dv = (
            [sem(f"{n}{L}") for L in Ls] for n in (
                "g_load", "g_strip_ready", "g_q_ready", "g_sc", "g_max", "g_exp", "g_tp", "g_tc", "g_av", "g_fin", "g_dv"))
        g_tbT = sem("g_tbT")
        ao_ready = sem("ao_ready")
        aoT_psum = sem("aoT_psum")
        oT_ready = sem("oT_ready")
        y_psum = sem("y_psum")
        yT_ready = sem("yT_ready")
        yback_psum = sem("yback_psum")
        x_added = sem("x_added")
        gate_psum = sem("gate_psum")
        gate_d, gate_e = sem("gate_d"), sem("gate_e")
        w_ready = sem("w_ready")
        wT_psum = sem("wT_psum")
        wT_ready = sem("wT_ready")
        h_psum, h_act = sem("h_psum"), sem("h_act")
        y0_psum, y0_read = sem("y0_psum"), sem("y0_read")
        enc_psum, enc_act, cont_psum, cont_ready = sem("enc_psum"), sem("enc_act"), sem("cont_psum"), sem("cont_ready")
        sel_ready = sem("sel_ready")
        hh_psum, relu_done = sem("hh_psum"), sem("relu_done")
        wb_psum = sem("wb_psum")
        hh_act = sem("hh_act")
        yy_psum = sem("yy_psum")
        eoT_ready = sem("eoT_ready")
        exp1_psum, exp1_act, dec_psum, dec_ready, fo_ready = (
            sem("exp1_psum"), sem("exp1_act"), sem("dec_psum"), sem("dec_ready"), sem("fo_ready"))
        stored = sem("stored")

        def fix_of(L, qc, kb):
            first, last = 4 * qc, 4 * qc + TC - 1
            lo, hi = (max(first, kb - 1), min(last, kb + 1)) if L == 0 else (kb, kb)
            if lo > hi or lo > last or hi < first:
                return None
            return lo - first, hi - first + 1

        groups = [(qc, kb) for qc in range(NC) for kb in range(NT)]

        def fixes_before(L, gi):
            return 2 * sum(fix_of(L, *groups[j]) is not None for j in range(gi))

        NFIX = [fixes_before(L, NGRP) for L in Ls]
        KLOADS = [16 * (GH + 1), 16 * 2 * GH]
        KLATE = [16 * GH, 16 * 2 * GH]
        QLOADS = [16 * (GH + 1), 16 * 2 * GH]
        qst, kst, vh, pr, ot = (qst0, qst1), (kst0, kst1), (vh0, vh1), (pr0, pr1), (ot0, ot1)
        ROWS = (BIAS_ROWS + QK_ROWS, QK_ROWS)
        QROW = (BIAS_ROWS, 0)
        NSPLIT = (2, 4)

        def bank(b):
            return ps[:, b, :]

        def tile4(b):
            return ps[:, b, :].rearrange("p (t d) -> p t d", t=TC)

        block = ctx.enter_context(nc.Block())

        @block.sync
        def _(sp):
            def load(dst, src, done):
                sp.dma_start(dst, src).then_inc(done, 16)

            def row(name, n, parts_=P, off=0):
                a = t[name]
                return bass.AP(a.tensor, a.offset + off, [[0, parts_], [1, n]])

            xin = t["L0_attn_x"].rearrange("b (t p) d -> p (b t) d", p=P)
            load(x[:, 0:TC, :], xin[:, 0:TC, :], ld_x[0])
            for L in Ls:
                load(ccol[:, L:L + 1], t[f"L{L}_c"].rearrange("a d -> d a"), ld_mod)
            for L in Ls:
                load(wmod_sb[L][:], t[f"L{L}_wmod"], ld_mod)
            load(wqkv[:], t["L0_attn_W_qkv"], ld_att0)
            load(bqk[:, 0:2], t["L0_attn_b_qkv"][0:2 * D].rearrange("(a p) -> p a", p=P), ld_att0)
            load(bqk[:, 2:3], t["L0_attn_b_out"].rearrange("(p a) -> p a", a=1), ld_att0)
            load(bvrow[:], row("L0_attn_b_qkv", D, off=2 * D), ld_att0)
            for c in range(1, NC):
                load(x[:, TC * c:TC * (c + 1), :], xin[:, TC * c:TC * (c + 1), :], ld_x[c])
            load(wout0[:], t["L0_attn_W_out"], ld_att0)
            rel = t["L0_attn_rel_bias"]
            load(relt[:, 0, :], rel[0:P, :], ld_rel)
            load(relt[:, 1, :], rel[P:2 * P, :], ld_rel)
            load(relt[0:1, 2, :], rel[2 * P:2 * P + 1, :], ld_rel)
            load(relf[:], bass.AP(rel.tensor, rel.offset, [[2 * REL + 1, H], [1, 2 * REL + 1]]), ld_rel)
            load(crow[:, 0, :], row("L0_attn_rel_bias", H), ld_rel)
            load(crow[:, 1, :], row("L0_attn_rel_bias", H, off=2 * REL * H), ld_rel)

            for e in range(E0):
                load(w10[:, e, :], t["L0_ffn_W1"][e], ld_ffn0)
                load(w20[:, e, :, :], t["L0_ffn_W2"][e].rearrange("(k p) d -> p k d", p=P), ld_ffn0)
            for e in range(SH0):
                load(w10[:, E0 + e, :], t["L0_ffn_sW1"][e], ld_ffn0)
                load(w20[:, E0 + e, :, :], t["L0_ffn_sW2"][e].rearrange("(k p) d -> p k d", p=P), ld_ffn0)
            load(b10[:, 0:E0, :], t["L0_ffn_b1"].rearrange("e (k p) -> p e k", p=P), ld_ffn0)
            load(b10[:, E0:, :], t["L0_ffn_sb1"].rearrange("e (k p) -> p e k", p=P), ld_ffn0)
            load(b20[0:E0, :], t["L0_ffn_b2"], ld_ffn0)
            load(b20[E0:, :], t["L0_ffn_sb2"], ld_ffn0)
            load(rw0[:], t["L0_ffn_rW"], ld_ffn0)
            load(rb0[:], row("L0_ffn_rb", E0), ld_ffn0)
            for dst, name in ((wq1, "Wq"), (wk1, "Wk"), (wv1, "Wv"), (wo1, "Wo"), (wdn1, "W_down_kv")):
                load(dst[:], t[f"L1_attn_{name}"], ld_att1)
            load(wup1[:, 0, :], t["L1_attn_W_up_k"], ld_att1)
            load(wup1[:, 1, :], t["L1_attn_W_up_v"], ld_att1)

            sp.wait_ge(relv_ready, 1)
            for h4 in range(NG):
                v = relv[GH * h4:GH * (h4 + 1), :].unsqueeze(1).to_broadcast([GH, P, TROW])
                sp.dma_start(relrows[GH * h4:GH * (h4 + 1)], v).then_inc(relrows_stored, 16)

            def stores(L, c):
                for u in range(2):
                    n = 2 * c + u
                    sp.wait_ge(q32_ready, 2 * NC * L + n + 1)
                    sp.dma_start(qkf[L][u, :, CW * c:CW * (c + 1)], q32[L][:, c % 2, u, :]).then_inc(qkf_st[L][n % 4], 16)
                for a, made in enumerate((p1_ready, p2_ready, split_done)):
                    for u in range(NSPLIT[L]):
                        n = NSPLIT[L] * c + u
                        sp.wait_ge(made[L], n + 1)
                        src = pp[L][:, n % 4, a, :]
                        if u % 2 == 0:
                            dst = qparts[L][u // 2, a, :, :, CW * c:CW * (c + 1)].rearrange("r p n -> p r n")
                            src = src.unsqueeze(1).to_broadcast([P, PARTS, CW])
                        else:
                            dst = kparts[L][u // 2, :, a, :, CW * c:CW * (c + 1)]
                        sp.dma_start(dst, src).then_inc(parts_st[L][n % 4], 16)

            def stack_loads(L, v, u, dst, col0, n, head0, done):
                for hh in range(GH):
                    head = head0 + hh
                    if u == 0:
                        a = qparts[L]
                        src = bass.AP(a.tensor, a.offset + v * PARTS * PARTS * D * S + head * DK * S + col0,
                                      [[D * S, PARTS * PARTS], [S, DK], [1, n]])
                    else:
                        a = kparts[L]
                        src = bass.AP(a.tensor, a.offset + (v * H + head) * PARTS * DK * S + col0,
                                      [[0, PARTS], [S, PARTS * DK], [1, n]])
                    sp.dma_start(dst(hh)[QROW[L]:ROWS[L], :], src).then_inc(done, 16)

            def parts_complete(L):
                for s in range(4):
                    sp.wait_ge(parts_st[L][s], 16 * PARTS * NSPLIT[L] * NC // 4)
                    sp.wait_ge(qkf_st[L][s], 16 * 2 * NC // 4)

            def fast(L):
                def keys(g, half):
                    if g >= 2 and half == 0:
                        sp.wait_ge(av_done[L], AV0 + NGRP * (g - 1))
                    c0 = half * (S // 2)
                    for v in range(L + 1):
                        stack_loads(L, v, 1, lambda hh: kst[L][:, g % 2, v, hh, c0:c0 + S // 2], c0, S // 2, GH * g,
                                    k_late[L][g % 2] if half else k_loaded[L][g % 2])
                    if L == 0 and half == 0:
                        a = bass.AP(relrows.tensor, relrows.offset + GH * g * P * TROW + P - 1,
                                    [[TROW - 1, P], [P * TROW, GH], [1, BAND]])
                        sp.dma_start(tb0[:, g % 2, :, :], a).then_inc(k_loaded[0][g % 2], 16)

                def queries(m):
                    if m >= 2:
                        sp.wait_ge(scores_psum[L], 2 * NT * (m - 1))
                    c0 = CW * (m % NC)
                    for v in range(L + 1):
                        stack_loads(L, v, 0, lambda hh: qst[L][:, m % 2, v, hh, :], c0, CW,
                                    GH * (m // NC), q_loaded[L][m % 2])
                    if L == 0:
                        src = onehw[:, c0:c0 + CW].unsqueeze(1).to_broadcast([BIAS_ROWS, GH, CW])
                        sp.dma_start(qst0[0:BIAS_ROWS, m % 2, 0, :, :], src).then_inc(q_loaded[0][m % 2], 16)

                keys(0, 0)
                queries(0)
                keys(0, 1)
                queries(1)
                keys(1, 0)
                keys(1, 1)
                for m in range(2, NC * NG):
                    queries(m)
                    if m % NC == 0 and m // NC + 1 < NG:
                        keys(m // NC + 1, 0)
                        keys(m // NC + 1, 1)

            def general(L, k_, q_):
                with sp.Fori(0, H) as h:
                    for u, dst in ((1, k_), (0, q_)):
                        if u == 1:
                            sp.wait_ge(g_fin[L], h * NT + 1)
                        a = bass.AP(qkf[L].tensor, qkf[L].offset + u * D * S + h * (DK * S), [[S, DK], [1, S]])
                        sp.dma_start(dst[:], a).then_inc(g_load[L], 16)
                    if L == 0:
                        a = bass.AP(relrows.tensor, relrows.offset + P - 1 + h * (P * TROW), [[TROW - 1, P], [1, BAND]])
                        sp.dma_start(g_tb[:], a).then_inc(g_load[L], 16)

            for c in range(NC):
                stores(0, c)
            parts_complete(0)
            sp.wait_ge(onehw_ready, 1)
            sp.wait_ge(relrows_stored, 16 * NG)
            sp.wait_ge(flag_ready, 1)
            fv = sp.value_load(flag[0:1, 0:1])
            with sp.If(fv > 0):
                fast(0)
            with sp.Else():
                general(0, g_k, g_q)
            for c in range(NC - 1):
                stores(1, c)
            sp.wait_ge(y0_read, NC * (E0 + 1))
            load(wenc[:], t["L1_ffn_W_enc"], ld_ffn1)
            load(benc[:], t["L1_ffn_b_enc"].rearrange("(a p) -> p a", p=P), ld_ffn1)
            load(ws2c[:], t["L1_ffn_W_s2c"].rearrange("(a p) m -> p a m", p=P), ld_ffn1)
            load(bs2c[:], t["L1_ffn_b_s2c"].rearrange("(p a) -> p a", a=1), ld_ffn1)
            load(wr1[0:M1, :], t["L1_ffn_Wr"], ld_ffn1)
            load(wr1[M1:, :], row("L1_ffn_br", E1, 1), ld_ffn1)
            load(w11[0:M1, :].rearrange("m (e h) -> m e h", e=E1), t["L1_ffn_W1"].rearrange("e m h -> m e h"), ld_ffn1)
            load(w11[M1:, :], row("L1_ffn_b1", E1 * HID1, 1), ld_ffn1)
            load(w21[:], t["L1_ffn_W2"].rearrange("e h m -> h e m"), ld_ffn1)
            for a in range(PARTS):
                load(b21[E1 * a:E1 * (a + 1), :], t["L1_ffn_b2"], ld_ffn1)
            for a in range(2):
                load(wc2s[M1 * a:M1 * (a + 1), :], t["L1_ffn_W_c2s"], ld_ffn1)
            load(bc2s[:], t["L1_ffn_b_c2s"].rearrange("(a p) -> p a", p=P), ld_ffn1)
            load(wdec[:], t["L1_ffn_W_dec"].rearrange("(a p) d -> p a d", p=P), ld_ffn1)
            load(bdec[:], row("L1_ffn_b_dec", D), ld_ffn1)
            load(lngr[:], row("L1_ffn_ln_g", D), ld_ffn1)
            load(lnbr[:], row("L1_ffn_ln_b", D), ld_ffn1)
            stores(1, NC - 1)
            parts_complete(1)
            sp.wait_ge(flag_ready, 1 + 1)
            fv = sp.value_load(flag[0:1, 1:2])
            with sp.If(fv > 0):
                fast(1)
            with sp.Else():
                general(1, h_k, h_q)
            xout = out.rearrange("b (t p) d -> p (b t) d", p=P)
            for c in range(NC):
                sp.wait_ge(fo_ready, c + 1)
                sp.dma_start(xout[:, TC * c:TC * (c + 1), :], fo[:, c, :, :]).then_inc(stored, 16)
            sp.wait_ge(stored, 16 * NC)

        order0 = [E0, E0 + 1] + list(range(E0))

        def y_index(n):
            c, j = divmod(n, len(order0))
            return (E0 + 1) * c + max(j - 1, 0)

        def ln_pass(L, second):
            return 2 * L + second

        @block.gpsimd
        def _(pool):
            self_n = [0]

            def link(ins):
                self_n[0] += 1
                ins.then_inc(pool_self, 1)
                pool.wait_ge(pool_self, self_n[0])

            def iota(dst, pattern, base, mult):
                return nc.gpsimd.iota(dst, pattern, base, mult, allow_small_or_imprecise_dtypes=True)

            link(nc.gpsimd.memset(ident[:], 0.0))
            link(nc.gpsimd.affine_select(out=ident[:], in_=ident[:], compare_op=ALU.not_equal, fill=1.0, base=0,
                                         pattern=[[-1, P]], channel_multiplier=1))
            link(nc.gpsimd.memset(headones[:], 1.0))
            hv = headones[:].rearrange("p (a b) -> p a b", b=DK)
            link(nc.gpsimd.affine_select(out=hv, in_=hv, compare_op=ALU.is_ge, fill=0.0, base=0,
                                         pattern=[[-DK, H], [0, DK]], channel_multiplier=1))
            link(nc.gpsimd.affine_select(out=hv, in_=hv, compare_op=ALU.is_ge, fill=0.0, base=DK - 1,
                                         pattern=[[DK, H], [0, DK]], channel_multiplier=-1))
            iota(iota_e[:], [[1, 8]], 0, 0)
            iota(rp[:, 0:1], [[0, 1]], 0, 1)
            iota(iota_p[:, 0:1], [[0, 1]], 0, 1)
            iota(kbi[:], [[1, NT]], 0, 0)
            iota(dup[:, 0, :], [[1, CW]], 0, 0)
            iota(dup[:, 1, :], [[1, CW]], 0, 0)
            iota(dtri[:], [[1, P]], 0, -1).then_inc(consts, 1)
            for L in Ls:
                nc.gpsimd.memset(marks[0:1, 0 + L:1 + L], 0.0).then_inc(exp_done[L], EXP0)
                nc.gpsimd.memset(marks[0:1, 2 + L:3 + L], 0.0).then_inc(av_done[L], AV0)
                nc.gpsimd.memset(marks[0:1, 4 + L:5 + L], 0.0).then_inc(acc_free[L], ACC0)
                nc.gpsimd.memset(marks[0:1, 6 + L:7 + L], 0.0).then_inc(g_fin[L], GEN0)
            def fill(L):
                link(nc.gpsimd.memset(vh[L][:].rearrange("p a k h w -> p (a k h w)"), 0.0))
                link(nc.gpsimd.memset(vh[L][:, :, :, :, DK:DK + 1].rearrange("p a k h w -> p (a k) h w"), 1.0))

            def group(L, g):
                p_ = g % 2
                if L == 0:
                    for hh in range(GH):
                        nc.gpsimd.tensor_copy(
                            kst0[0:BIAS_ROWS, p_, 0, hh, :].rearrange("p (k n) -> p k n", n=P),
                            ktab[:, g * GH + hh, :].unsqueeze(2).to_broadcast([BIAS_ROWS, NT, P]))
                if g == 0:
                    pool.wait_ge(v_ready[L], NC)
                nc.gpsimd.tensor_copy(
                    vh[L][:, p_, :, :, 0:DK],
                    vall[:, :, g * (GH * DK):(g + 1) * (GH * DK)].rearrange("p k (h d) -> p k h d", h=GH))\
                  .then_inc(group_ready[L], 1)

            def fast(L):
                for g in range(1, NG):
                    pool.wait_ge(av_done[L], g * NGRP + (AV0 - NGRP))
                    group(L, g)

            def general1():
                iota(h_strip[:], [[-1, STRIP]], (NT - 1) * P, 1).then_inc(g_strip_ready[1], 1)

            fill(0)
            pool.wait_ge(ktab_ready, 1)
            group(0, 0)
            pool.wait_ge(gates_ready, 1)
            pool.wait_ge(ld_ffn0, 16 * (2 * (E0 + SH0) + 6))
            w20v = w20[:].rearrange("p e k d -> p (e k) d")
            nk = (E0 + SH0) * KT0
            link(nc.gpsimd.tensor_tensor(w20v, w20v, gbrow[:, 0, :].unsqueeze(1).to_broadcast([P, nk, D]), ALU.mult))
            nc.gpsimd.tensor_tensor(b20[:], b20[:], gbrow[0:E0 + SH0, 0, :], ALU.mult)
            link(nc.gpsimd.tensor_scalar(w20[:, E0:, :, :].rearrange("p e k d -> p (e k d)"),
                                         w20[:, E0:, :, :].rearrange("p e k d -> p (e k d)"),
                                         1.0 / SH0, None, ALU.mult))
            nc.gpsimd.memset(marks[0:1, 8:9], 0.0).then_inc(gb_folded, 1)
            pool.wait_ge(flag_ready, 1)
            fv = pool.value_load(flag[0:1, 0:1])
            with pool.If(fv > 0):
                fast(0)
            pool.wait_ge(y0_read, NC * (E0 + 1))
            fill(1)
            group(1, 0)
            pool.wait_ge(flag_ready, 1 + 1)
            fv = pool.value_load(flag[0:1, 1:2])
            with pool.If(fv > 0):
                fast(1)
            with pool.Else():
                general1()

        @block.scalar
        def _(act):
            def modcol(L, j):
                return mod[:, L, j:j + 1]

            def ln_out(L, second, c):
                m = NC * ln_pass(L, second) + c
                act.wait_ge(ln_psum, m + 1)
                nc.scalar.activation(hT[:, CW * c:CW * (c + 1)], bank(6), ACT.Identity,
                                     bias=modcol(L, 3 * second), scale=modcol(L, 3 * second + 1)).then_inc(hT_ready, 1)

            def q32_slot(L, c, u):
                n = 2 * c + u
                if n >= 4:
                    act.wait_ge(qkf_st[L][n % 4], 16 * (n // 4))
                    act.wait_ge(split_done[L], NSPLIT[L] * (c - 1))
                    act.wait_ge(nrm_psum, 2 * NC * L + 2 * (c - 1))
                return q32[L][:, c % 2, u, :]

            def square(L, c, u):
                nc.scalar.activation(sq[L][:, c % 2, u, :], q32[L][:, c % 2, u, :], ACT.Square).then_inc(sq_ready, 1)

            def first_part(L, n, src):
                if n >= 4:
                    act.wait_ge(parts_st[L][n % 4], 16 * PARTS * (n // 4))
                nc.scalar.copy(pp[L][:, n % 4, 0, :], src).then_inc(p1_ready[L], 1)

            def second_part(L, n):
                act.wait_ge(r1_ready[L], n + 1)
                nc.scalar.copy(pp[L][:, n % 4, 1, :], r1[L][:, n % 4, :]).then_inc(p2_ready[L], 1)

            def project0(c):
                for u in range(2):
                    act.wait_ge(qk_psum, 2 * c + u + 1)
                    dst = q32_slot(0, c, u)
                    bias, scale = (bqs[:, 0:1], SCALE[0]) if u == 0 else (bqk[:, 1:2], 1.0)
                    nc.scalar.activation(dst, bank(3 * (c % 2) + u), ACT.Identity, bias=bias, scale=scale)\
                      .then_inc(q32_ready, 1)
                    act.wait_ge(q32_ready, 2 * c + u + 1)
                    first_part(0, 2 * c + u, dst)
                    square(0, c, u)
                if c + 1 < NC:
                    ln_out(0, 0, c + 1)
                for u in range(2):
                    second_part(0, 2 * c + u)

            def layer1_step(j, c):
                if j == 2:
                    ln_out(1, 0, c)
                elif j == 3:
                    act.wait_ge(qk_psum, 2 * NC + 2 * c + 1)
                    dst = q32_slot(1, c, 0)
                    nc.scalar.activation(dst, bank(5), ACT.Copy, scale=SCALE[1]).then_inc(q32_ready, 1)
                    act.wait_ge(kv_psum, c + 1)
                    nc.scalar.copy(kv32[:, c % 2, :], bank(6)).then_inc(kv_read, 1)
                elif j == 4:
                    act.wait_ge(lat_psum, c + 1)
                    nc.scalar.copy(lat[:, c % 2, :], ps[0:32, 5, :]).then_inc(lat_ready, 1)
                elif j == 5:
                    act.wait_ge(qk_psum, 2 * NC + 2 * c + 2)
                    dst = q32_slot(1, c, 1)
                    nc.scalar.copy(dst, bank(6)).then_inc(q32_ready, 1)
                    act.wait_ge(q32_ready, 2 * NC + 2 * c + 2)
                    for u in range(2):
                        square(1, c, u)
                elif j == 7:
                    for n in range(4 * c, 4 * c + 4):
                        act.wait_ge(w32_ready, n + 1)
                        first_part(1, n, w32[:, n % 4, :])
                elif j == 9:
                    for n in range(4 * c, 4 * c + 4):
                        second_part(1, n)

            def project_step(L, c, j):
                if j == 0:
                    act.wait_ge(aoT_psum, NC * L + c + 1)
                    if c:
                        act.wait_ge(y_psum, NC * L + c)
                    nc.scalar.copy(oT[:], bank(6 + c % 2)).then_inc(oT_ready, 1)

            def fast(L):
                def pair_of_groups(i, last):
                    for p_ in range(2):
                        g = 2 * i + p_
                        nfix = 0
                        for gi, (qc, kb) in enumerate(groups):
                            k = NGRP * p_ + gi
                            for pair in range(2):
                                step = 2 * gi + pair
                                b = 2 * ((NSTEP * p_ + step) % SCORE_BUFS)
                                if fix_of(L, qc, kb):
                                    nfix += 1
                                    act.wait_ge(fixed[L], g * NFIX[L] + nfix)
                                else:
                                    act.wait_ge(scores_psum[L], g * NSTEP + (step + 1))
                                if pair == 0:
                                    act.wait_ge(av_done[L], i * (2 * NGRP) + (AV0 + last_use(k, PROB_BUFS, 2 * NGRP) + 1))
                                nc.scalar.activation(pr[L][:, k % PROB_BUFS, pair, :, :], ps[:, b:b + 2, :], ACT.Exp)\
                                  .then_inc(exp_done[L], 1)
                            if last and p_ == 1 and qc and kb in PROJ_AT:
                                project_step(L, qc - 1, PROJ_AT.index(kb))

                with act.Fori(0, NG // 2 - 1) as i:
                    pair_of_groups(i, False)
                pair_of_groups(NG // 2 - 1, True)

            def general(L):
                g_row = (g_s, h_s)[L]
                st = (g_m, h_st)[L]
                if L == 1:
                    act.wait_ge(g_strip_ready[1], 1)
                    nc.scalar.activation(h_strip[:], h_strip[:], ACT.Abs).then_inc(g_strip_ready[1], 1)
                    act.wait_ge(g_strip_ready[1], 2)
                    nc.scalar.activation(h_strip[:], h_strip[:], ACT.Exp, scale=-DECAY).then_inc(g_strip_ready[1], 1)
                with act.Fori(0, H * NT) as n:
                    act.wait_ge(g_max[L], n + 1)
                    nc.scalar.activation(g_row[:], g_row[:], ACT.Exp, bias=st[:, 1:2], accum_out=st[:, 2:3])\
                      .then_inc(g_exp[L], 1)
                for c in range(EARLY):
                    project_step(L, c, 0)

            def attend(L):
                act.wait_ge(flag_ready, L + 1)
                fv = act.value_load(flag[0:1, L:L + 1])
                with act.If(fv > 0):
                    fast(L)
                with act.Else():
                    general(L)

            def projected(L):
                ln_out(L, 1, 0)
                project_step(L, NC - 1, 0)
                for c in range(1, NC):
                    ln_out(L, 1, c)

            act.wait_ge(ld_mod, 16 * 4)
            nc.scalar.activation(cexp[:], ccol[:], ACT.Exp, scale=-1.0).then_inc(silu_exp, 1)
            act.wait_ge(consts, 1)
            nc.scalar.activation(dup[:, 0, :], dup[:, 0, :], ACT.Exp, scale=-DECAY).then_inc(decays, 1)
            nc.scalar.activation(dup[:, 1, :], dup[:, 1, :], ACT.Exp, scale=DECAY).then_inc(decays, 1)
            act.wait_ge(decays, 3)
            nc.scalar.activation(dtri[:], dtri[:], ACT.Exp, scale=2 * DECAY).then_inc(decays, 1)
            act.wait_ge(mod_done, 1)
            act.wait_ge(ld_att0, 16 * 5)
            ln_out(0, 0, 0)
            for c in range(NC):
                project0(c)
            attend(0)
            projected(0)
            act.wait_ge(gate_d, 1)
            nc.scalar.activation(gsm[:, :, 1], gsm[:, :, 0], ACT.Exp).then_inc(gate_e, 1)
            act.wait_ge(ld_ffn0, 16 * (2 * (E0 + SH0) + 6))
            for n in range(NC * len(order0)):
                e = order0[n % len(order0)]
                if n >= HB:
                    act.wait_ge(y0_psum, y_index(n - HB) + 1)
                for k in range(KT0):
                    act.wait_ge(h_psum, KT0 * n + k + 1)
                    nc.scalar.activation(hbuf0[:, n % HB, k, :], bank((KT0 * n + k) % 3), ACT.Gelu,
                                         bias=b10[:, e, k:k + 1]).then_inc(h_act, 1)
                c, j = divmod(n, len(order0))
                if c:
                    layer1_step(j, c - 1)
            for j in range(len(order0)):
                layer1_step(j, NC - 1)
            attend(1)
            projected(1)
            act.wait_ge(ld_ffn1, 16 * 19)
            for c in range(NC):
                for a in range(2):
                    act.wait_ge(enc_psum, 2 * c + a + 1)
                    if c >= 2:
                        act.wait_ge(cont_psum, c - 1)
                    nc.scalar.activation(sp_e[:, c % 2, a, :], bank(2 * (c % 2) + a), ACT.Sigmoid,
                                         bias=benc[:, a:a + 1]).then_inc(enc_act, 1)
            act.wait_ge(gate_d, 1 + 1)
            nc.scalar.activation(gts[:], gts[:], ACT.Exp).then_inc(gate_e, 1)

            def expand1(c):
                act.wait_ge(yy_psum, (c + 1) * E1 // 2)
                if c >= 2:
                    act.wait_ge(exp1_psum, 2 * (c - 1))
                nc.scalar.copy(eoT[:, c % 2, :], bank(4 + c % 2)).then_inc(eoT_ready, 1)

            def squash1(c):
                for a in range(2):
                    act.wait_ge(exp1_psum, 2 * c + a + 1)
                    if c >= 2:
                        act.wait_ge(dec_psum, c - 1)
                    nc.scalar.activation(sp_e[:, c % 2, a, :], bank(6 + a), ACT.Sigmoid, bias=bc2s[:, a:a + 1])\
                      .then_inc(exp1_act, 1)

            def relu1(n):
                act.wait_ge(hh_psum, n + 1)
                if n >= E1:
                    act.wait_ge(hh_act, n - E1 + 1)
                nc.scalar.activation(rbuf1[:, n % E1, :], bank(n % 2), ACT.Relu).then_inc(relu_done, 1)

            for n in range(E1):
                relu1(n)
            for n in range(NC * E1):
                if n + E1 < NC * E1:
                    relu1(n + E1)
                c, e = divmod(n, E1)
                if c and e == 1:
                    expand1(c - 1)
                if c and e == 3:
                    squash1(c - 1)
            expand1(NC - 1)
            squash1(NC - 1)

        @block.tensor
        def _(pe):
            mm, tr = nc.tensor.matmul, nc.tensor.transpose

            def ln_transpose(L, second, c):
                m = NC * ln_pass(L, second) + c
                pe.wait_ge(xn_ready, m + 1)
                if m:
                    pe.wait_ge(hT_ready, m)
                for k in range(TC):
                    last = tr(ps[:, 6, P * k:P * (k + 1)], xn[:, m % 2, k, :], ident[:])
                last.then_inc(ln_psum, 1)

            def norms(L, c, us=range(2)):
                for u in us:
                    i = 2 * c + u
                    pe.wait_ge(sq_ready, 2 * NC * L + i + 1)
                    if i:
                        pe.wait_ge(nrm_read, 2 * NC * L + i)
                    mm(bank(7), headones[:], sq[L][:, c % 2, u, :], start=True, stop=True).then_inc(nrm_psum, 1)

            def project0(c):
                b = 3 * (c % 2)
                cols = slice(CW * c, CW * (c + 1))
                pe.wait_ge(hT_ready, c + 1)
                if c >= 2:
                    pe.wait_ge(q32_ready, 2 * (c - 1))
                    pe.wait_ge(v_ready[0], c - 1)
                for u in range(2):
                    mm(bank(b + u), wqkv[:, D * u:D * (u + 1)], hT[:, cols], start=True, stop=True)\
                      .then_inc(qk_psum, 1)
                for k in range(TC):
                    last = mm(ps[:, b + 2, P * k:P * (k + 1)], hT[:, CW * c + P * k:CW * c + P * (k + 1)],
                              wqkv[:, 2 * D:3 * D], start=True, stop=True)
                last.then_inc(v_psum[0], 1)

            def layer1_step(j, c):
                if j == 2:
                    if c:
                        pe.wait_ge(q32_ready, 2 * NC + 2 * c)
                    ln_transpose(1, 0, c)
                elif j == 3:
                    cols = slice(CW * c, CW * (c + 1))
                    pe.wait_ge(hT_ready, 2 * NC + c + 1)
                    if c:
                        pe.wait_ge(v_ready[1], c)
                    mm(bank(5), wq1[:], hT[:, cols], start=True, stop=True).then_inc(qk_psum, 1)
                    mm(bank(6), wk1[:], hT[:, cols], start=True, stop=False)
                    mm(bank(6), wv1[:], hT[:, cols], start=False, stop=True).then_inc(kv_psum, 1)
                elif j == 4:
                    pe.wait_ge(kv_read, c + 1)
                    pe.wait_ge(q32_ready, 2 * NC + 2 * c + 1)
                    mm(ps[0:32, 5, :], wdn1[:], kv32[:, c % 2, :], start=True, stop=True).then_inc(lat_psum, 1)
                elif j == 5:
                    pe.wait_ge(lat_ready, c + 1)
                    mm(bank(6), wup1[:, 0, :], lat[:, c % 2, :], start=True, stop=True).then_inc(qk_psum, 1)
                    for k in range(TC):
                        last = mm(ps[:, 5, P * k:P * (k + 1)], lat[:, c % 2, P * k:P * (k + 1)],
                                  wup1[:, 1, :], start=True, stop=True)
                    last.then_inc(v_psum[1], 1)
                elif j in (7, 9):
                    norms(1, c, [(j - 7) // 2])

            def decide(L):
                pe.wait_ge(pm_ready, L + 1)
                tr(ps[0:1, 7, 0:P], pm[:, 0:1], ident[:]).then_inc(pmT_psum, 1)

            def project_step(L, c, j):
                b = 6 + c % 2
                if j == 0:
                    if c >= 2:
                        pe.wait_ge(x_added, NC * L + c - 1)
                    for k in range(TC):
                        last = tr(ps[:, b, P * k:P * (k + 1)], ao[:, TC * c + k, :], ident[:])
                    last.then_inc(aoT_psum, 1)
                elif j == 1:
                    pe.wait_ge(oT_ready, NC * L + c + 1)
                    mm(bank(b), (wout0, wo1)[L][:], oT[:], start=True, stop=True).then_inc(y_psum, 1)
                else:
                    pe.wait_ge(yT_ready, NC * L + c + 1)
                    for k in range(TC):
                        last = tr(ps[:, b, P * k:P * (k + 1)], yT[:, P * k:P * (k + 1)], ident[:])
                    last.then_inc(yback_psum, 1)

            def fast(L):
                def scores(g, p_, i, gi):
                    qc, kb = groups[gi]
                    if gi == 0:
                        pe.wait_ge(k_loaded[L][p_], i * KLOADS[L] + KLOADS[L])
                        pe.wait_ge(group_ready[L], g + 1)
                    if gi == NT // 2:
                        pe.wait_ge(k_late[L][p_], i * KLATE[L] + KLATE[L])
                    if gi % NT == 0:
                        pe.wait_ge(q_loaded[L][qc % 2], g * (2 * QLOADS[L]) + QLOADS[L] * (qc // 2 + 1))
                    for pair in range(2):
                        step = 2 * gi + pair
                        b = 2 * ((NSTEP * p_ + step) % SCORE_BUFS)
                        last_exp = last_use(NSTEP * p_ + step, SCORE_BUFS, 2 * NSTEP)
                        pe.wait_ge(exp_done[L], i * (2 * NSTEP) + (EXP0 + last_exp + 1))
                        nlo = min(max(kb - TC * qc, 0), TC) * P if L == 1 else 0
                        for hh in range(2):
                            head = 2 * pair + hh
                            for v, lo, hi in ((1, 0, nlo), (0, nlo, CW)):
                                if lo < hi:
                                    last = mm(ps[:, b + hh, lo:hi],
                                              kst[L][0:ROWS[L], p_, v, head, P * kb:P * (kb + 1)],
                                              qst[L][0:ROWS[L], qc % 2, v, head, lo:hi], start=True, stop=True)
                        last.then_inc(scores_psum[L], 1)

                def values(g, p_, gi):
                    qc, kb = groups[gi]
                    pe.wait_ge(exp_done[L], g * NSTEP + (EXP0 + 2 * gi + 2))
                    if gi % NT == 0:
                        pe.wait_ge(acc_free[L], g * NC + (qc + ACC0 - 1))
                    for h in range(GH):
                        last = mm(ps[VW * h:VW * (h + 1), 6 + qc % 2, :], vh[L][:, p_, kb, h, :],
                                  pr[L][:, (NGRP * p_ + gi) % PROB_BUFS, h // 2, h % 2, :],
                                  start=(gi % NT == 0), stop=(gi % NT == NT - 1))
                    last.then_inc(av_done[L], 1)

                def turn(g, qc):
                    pe.wait_ge(acc_copied[L], g * NC + (qc + 1))
                    for k in range(TC):
                        last = tr(ps[:, 6 + qc % 2, P * k:P * (k + 1)], ot[L][:, P * k:P * (k + 1)], ident[:])
                    last.then_inc(accT_psum[L], 1)

                def pair_of_groups(i, final):
                    for k in range(2 * NGRP):
                        scores(2 * i + k // NGRP, k // NGRP, i, k % NGRP)
                        if k >= LAG:
                            p_, gi = divmod(k - LAG, NGRP)
                            if final and p_ == 1 and gi >= 2 * NT and gi % NT == 0:
                                pe.wait_ge(x_added, NC * L + gi // NT - 1)
                            values(2 * i + p_, p_, gi)
                        if k > NT and k % NT == TURN_AT:
                            p_, qc = divmod(k // NT - 1, NC)
                            turn(2 * i + p_, qc)
                        if final and k >= NGRP + NT and k % NT in PROJ_AT:
                            qc = (k - NGRP) // NT - 1
                            if k % NT == PROJ_AT[0]:
                                pe.wait_ge(acc_free[L], (NG - 1) * NC + ACC0 + qc + 1)
                            project_step(L, qc, PROJ_AT.index(k % NT))
                    for gi in range(NGRP - LAG, NGRP):
                        values(2 * i + 1, 1, gi)
                    turn(2 * i + 1, NC - 1)

                with pe.Fori(0, NG // 2 - 1) as i:
                    pair_of_groups(i, False)
                pair_of_groups(NG // 2 - 1, True)

            def general(L):
                k_, qt_, row_, pt_ = ((g_k, g_qt, g_s, g_pt), (h_k, h_qt, h_s, h_pt))[L]
                nload = 48 if L == 0 else 32
                with pe.Fori(0, H) as h:
                    if L == 0:
                        pe.wait_ge(g_load[L], h * nload + nload)
                        for b in range(3):
                            last = tr(ps[:, 4, P * b:P * (b + 1)], g_tb[:, P * (2 - b):P * (3 - b)], ident[:])
                        last.then_inc(g_tbT, 1)
                    with pe.Fori(0, NT) as q:
                        n = h * NT + q
                        pe.wait_ge(g_load[L], h * nload + nload)
                        pe.wait_ge(g_q_ready[L], n + 1)
                        pe.wait_ge(g_fin[L], n + GEN0)
                        for c in range(NC):
                            last = mm(bank(c), qt_[:], k_[:, CW * c:CW * (c + 1)], start=True, stop=True)
                        last.then_inc(g_sc[L], 1)
                        pe.wait_ge(g_exp[L], n + 1)
                        for kb in range(NT):
                            last = tr(ps[:, 4 + kb // TC, P * (kb % TC):P * (kb % TC + 1)],
                                      row_[:, P * kb:P * (kb + 1)], ident[:])
                        last.then_inc(g_tp[L], 1)
                        pe.wait_ge(g_tc[L], n + 1)
                        for kb in range(NT):
                            last = mm(ps[:, 0, 0:DK], pt_[:, P * kb:P * (kb + 1)],
                                      vall[:, kb, bass.ds(h * DK, DK)], start=(kb == 0), stop=(kb == NT - 1))
                        last.then_inc(g_av[L], 1)
                pe.wait_ge(g_fin[L], GEN0 + H * NT)
                for c in range(EARLY):
                    for j in range(3):
                        project_step(L, c, j)

            def attend(L):
                pe.wait_ge(flag_ready, L + 1)
                fv = pe.value_load(flag[0:1, L:L + 1])
                with pe.If(fv > 0):
                    fast(L)
                with pe.Else():
                    general(L)

            def projected(L):
                pe.wait_ge(x_added, NC * L + NC - 1)
                ln_transpose(L, 1, 0)
                pe.wait_ge(ao_ready, L + 1)
                project_step(L, NC - 1, 0)
                ln_transpose(L, 1, 1)
                project_step(L, NC - 1, 1)
                project_step(L, NC - 1, 2)
                for c in range(2, NC):
                    ln_transpose(L, 1, c)

            def turn_weights(L, n, src):
                pe.wait_ge(w_ready, L + 1)
                for c in range(NC):
                    if c >= 2:
                        pe.wait_ge(wT_ready, NC * L + c - 1)
                    for k in range(TC):
                        last = tr(ps[0:n, 6 + c % 2, P * k:P * (k + 1)], src[:, TC * c + k, 0:n], ident[:])
                    last.then_inc(wT_psum, 1)

            pe.wait_ge(consts, 1)
            pe.wait_ge(silu_done, 1)
            for L in Ls:
                for j in range(6):
                    mm(ps[:, 7, 6 * L + j:6 * L + j + 1], wmod_sb[L][:, D * j:D * (j + 1)], silu[:, L:L + 1],
                       start=True, stop=True)
            for L in Ls:
                last = mm(ps[:, 6, D * L:D * (L + 1)], silub[:, L, :], wmod_sb[L][:, 5 * D:6 * D], start=True, stop=True)
            last.then_inc(mod_psum, 1)
            pe.wait_ge(ld_rel, 16 * 6)
            tr(ps[0:H, 5, 0:P], relt[:, 0, :], ident[:])
            tr(ps[0:H, 5, P:2 * P], relt[:, 1, :], ident[:])
            tr(ps[0:H, 5, 2 * P:2 * P + 1], relt[0:1, 2, :], ident[0:1, 0:1]).then_inc(relT_psum, 1)
            pe.wait_ge(mod_done, 1)
            pe.wait_ge(ld_att0, 16 * 5)
            ln_transpose(0, 0, 0)
            for c in range(NC):
                if c == 1:
                    pe.wait_ge(relv_ready, 1)
                project0(c)
                if c:
                    norms(0, c - 1)
                if c + 1 < NC:
                    ln_transpose(0, 0, c + 1)
            norms(0, NC - 1)
            decide(0)
            attend(0)
            projected(0)

            pe.wait_ge(ld_ffn0, 16 * (2 * (E0 + SH0) + 6))
            for c in range(NC):
                pe.wait_ge(hT_ready, NC + c + 1)
                for k in range(TC):
                    last = mm(ps[:, 7, E0 * (TC * c + k):E0 * (TC * c + k + 1)],
                              hT[:, CW * c + P * k:CW * c + P * (k + 1)], rw0[:], start=True, stop=True)
                last.then_inc(gate_psum, 1)

            def hidden0(n):
                c, j = divmod(n, len(order0))
                for k in range(KT0):
                    i = KT0 * n + k
                    if i >= 3:
                        pe.wait_ge(h_act, i - 2)
                    mm(bank(i % 3), w10[:, order0[j], P * k:P * (k + 1)], hT[:, CW * c:CW * (c + 1)],
                       start=True, stop=True).then_inc(h_psum, 1)

            def output0(n):
                c, j = divmod(n, len(order0))
                if j == 0:
                    return
                y = y_index(n)
                pe.wait_ge(h_act, KT0 * (n + 1))
                if y >= 2:
                    pe.wait_ge(y0_read, y - 1)
                for k in range(TC):
                    dst = ps[:, 3 + y % 2, P * k:P * (k + 1)]
                    toks = slice(P * k, P * (k + 1))
                    if j == 1:
                        mm(dst, wT0[:, CW * c + P * k:CW * c + P * (k + 1)], b20[:], start=True, stop=False)
                        terms = [(n - 1, order0[0]), (n, order0[1])]
                    else:
                        terms = [(n, order0[j])]
                    every = [(m, e, q) for m, e in terms for q in range(KT0)]
                    for a, (m, e, q) in enumerate(every):
                        last = mm(dst, hbuf0[:, m % HB, q, toks], w20[:, e, q, :],
                                  start=(j > 1 and a == 0), stop=(a == len(every) - 1))
                last.then_inc(y0_psum, 1)

            hidden0(0)
            hidden0(1)
            turn_weights(0, E0 + SH0, wgt)
            pe.wait_ge(wT_ready, NC)
            pe.wait_ge(gb_folded, 1)
            pe.wait_ge(ld_att1, 16 * 7)
            for n in range(2, NC * len(order0)):
                hidden0(n)
                output0(n - 1)
                c, j = divmod(n, len(order0))
                if c:
                    layer1_step(j, c - 1)
            output0(NC * len(order0) - 1)
            for j in range(len(order0)):
                layer1_step(j, NC - 1)
            decide(1)
            attend(1)
            projected(1)

            pe.wait_ge(ld_ffn1, 16 * 19)

            def encode(c):
                pe.wait_ge(hT_ready, 3 * NC + c + 1)
                for a in range(2):
                    if c >= 2:
                        pe.wait_ge(enc_act, 2 * (c - 2) + a + 1)
                    mm(bank(2 * (c % 2) + a), wenc[:, P * a:P * (a + 1)], hT[:, CW * c:CW * (c + 1)],
                       start=True, stop=True).then_inc(enc_psum, 1)

            def contract(c):
                pe.wait_ge(enc_act, 2 * (c + 1))
                if c >= 2:
                    pe.wait_ge(cont_ready, c - 1)
                for a in range(2):
                    last = mm(ps[0:M1, 4 + c % 2, :], ws2c[:, a, :], sp_e[:, c % 2, a, :], start=(a == 0), stop=(a == 1))
                last.then_inc(cont_psum, 1)

            def route(c):
                pe.wait_ge(cont_ready, c + 1)
                for k in range(TC):
                    last = mm(ps[:, 7, E1 * (TC * c + k):E1 * (TC * c + k + 1)],
                              contT[:, CW * c + P * k:CW * c + P * (k + 1)], wr1[:], start=True, stop=True)
                last.then_inc(gate_psum, 1)

            encode(0)
            for c in range(NC):
                if c + 1 < NC:
                    encode(c + 1)
                contract(c)
                if c:
                    route(c - 1)
            route(NC - 1)

            def hidden1(n):
                c, e = divmod(n, E1)
                if n >= 2:
                    pe.wait_ge(relu_done, n - 1)
                mm(bank(n % 2), w11[:, HID1 * e:HID1 * (e + 1)], contT[:, CW * c:CW * (c + 1)],
                   start=True, stop=True).then_inc(hh_psum, 1)

            def weights1(n):
                c, e = divmod(n, E1)
                if n >= 2:
                    pe.wait_ge(hh_act, n - 1)
                mm(bank(2 + n % 2), sel1[:, e, :], wTb[:, CW * c:CW * (c + 1)], start=True, stop=True)\
                  .then_inc(wb_psum, 1)

            def output1(n):
                c, e = divmod(n, E1)
                out_ = 4 + c % 2
                pe.wait_ge(hh_act, n + 1)
                if e == 1:
                    if c >= 2:
                        pe.wait_ge(eoT_ready, c - 1)
                    mm(ps[0:M1, out_, :], b21[:], wT1[:, CW * c:CW * (c + 1)], start=True, stop=False)
                for h in range(2):
                    last = mm(ps[M1 * h:M1 * (h + 1), out_, :], w21[:, e - 1 + h, :], hbuf1[:, (n - 1 + h) % 4, :],
                              start=(h == 1 and e == 1), stop=(e == E1 - 1))
                last.then_inc(yy_psum, 1)

            def expand1(c):
                pe.wait_ge(eoT_ready, c + 1)
                if c:
                    pe.wait_ge(dec_ready, c)
                for a in range(2):
                    mm(bank(6 + a), wc2s[:, P * a:P * (a + 1)], eoT[:, c % 2, :], start=True, stop=True)\
                      .then_inc(exp1_psum, 1)

            def decode1(c):
                pe.wait_ge(exp1_act, 2 * (c + 1))
                for k in range(TC):
                    for a in range(2):
                        last = mm(ps[:, 6, P * k:P * (k + 1)], sp_e[:, c % 2, a, P * k:P * (k + 1)], wdec[:, a, :],
                                  start=(a == 0), stop=(a == 1))
                last.then_inc(dec_psum, 1)

            for n in range(E1):
                hidden1(n)
            turn_weights(1, PARTS * E1, wpart)
            pe.wait_ge(wT_ready, NC + NC)
            pe.wait_ge(sel_ready, 1)
            for n in range(NC * E1):
                weights1(n)
                if n + E1 < NC * E1:
                    hidden1(n + E1)
                if n % 2 and n >= 3:
                    output1(n - 2)
                c, e = divmod(n, E1)
                if c and e == 3:
                    expand1(c - 1)
                if c and e == 6:
                    decode1(c - 1)
            output1(NC * E1 - 1)
            expand1(NC - 1)
            decode1(NC - 1)

        @block.vector
        def _(dve):
            v = nc.vector
            self_n = [0]

            def link(ins):
                self_n[0] += 1
                ins.then_inc(dve_self, 1)
                dve.wait_ge(dve_self, self_n[0])

            def rsqrt_guess(var):
                link(v.tensor_scalar(rs_v[:], var, EPS, None, ALU.add))
                link(v.tensor_single_scalar(rs_i[:], rs_v[:].bitcast(I32), 1, op=ALU.logical_shift_right))
                link(v.tensor_scalar(rs_y[:].bitcast(I32), rs_i[:], -1.0, MAGIC, ALU.mult, ALU.add))

            def rsqrt_newton():
                link(v.scalar_tensor_tensor(rs_t[:], rs_y[:], -0.5, rs_y[:], ALU.mult, ALU.mult))
                link(v.tensor_tensor(rs_t[:], rs_t[:], rs_v[:], ALU.mult))
                link(v.scalar_tensor_tensor(rs_y[:], rs_t[:], 1.5, rs_y[:], ALU.add, ALU.mult))

            def moments(src, c):
                for k in range(TC):
                    last = v.bn_stats(stats[:, TC * c + k, :], src(k))
                link(last)
                for k in range(TC):
                    last = v.bn_aggr(meanvar[:, TC * c + k, :], stats[:, TC * c + k, :])
                link(last)

            def ln(L, second, c):
                m = NC * ln_pass(L, second) + c
                moments(lambda k: x[:, TC * c + k, :], c)
                rsqrt_guess(meanvar[:, TC * c:TC * (c + 1), 1])
                for _ in range(3):
                    rsqrt_newton()
                if m >= 2:
                    dve.wait_ge(ln_psum, m - 1)
                for k in range(TC):
                    last = v.tensor_scalar(xn[:, m % 2, k, :], x[:, TC * c + k, :], meanvar[:, TC * c + k, 0:1],
                                           rs_y[:, k:k + 1], ALU.subtract, ALU.mult)
                last.then_inc(xn_ready, 1)

            def remainder(L, n, src):
                dve.wait_ge(p1_ready[L], n + 1)
                v.tensor_tensor(r1[L][:, n % 4, :], src, pp[L][:, n % 4, 0, :], ALU.subtract).then_inc(r1_ready[L], 1)

            def third_part(L, n):
                dve.wait_ge(p2_ready[L], n + 1)
                v.tensor_tensor(pp[L][:, n % 4, 2, :], r1[L][:, n % 4, :], pp[L][:, n % 4, 1, :], ALU.subtract)\
                 .then_inc(split_done[L], 1)

            def norm_max(L, c, us=range(2)):
                for u in us:
                    dve.wait_ge(nrm_psum, 2 * NC * L + 2 * c + u + 1)
                    v.tensor_reduce(nmx[:, L, u, c:c + 1], bank(7), AX, ALU.max).then_inc(nrm_read, 1)

            def project0(c, also=None):
                for u in range(2):
                    remainder(0, 2 * c + u, q32[0][:, c % 2, u, :])
                dve.wait_ge(v_psum[0], c + 1)
                v.tensor_tensor(vall[:, TC * c:TC * (c + 1), :], tile4(3 * (c % 2) + 2),
                                bvrow[:].unsqueeze(1).to_broadcast([P, TC, D]), ALU.add).then_inc(v_ready[0], 1)
                if c == 0:
                    also()
                if c + 2 < NC:
                    dve.wait_ge(ld_x[c + 2], 16)
                    ln(0, 0, c + 2)
                for u in range(2):
                    third_part(0, 2 * c + u)
                norm_max(0, c)

            def layer1_step(j, c):
                four = range(4 * c, 4 * c + 4)
                if j == -1:
                    ln(1, 0, c)
                elif j == 4:
                    far = DECAY * (CW * c - S // 2)
                    for n in four:
                        u, d = n % 2, (n // 2) % 2
                        if d == 0:
                            dve.wait_ge(q32_ready, 2 * NC + 2 * c + u + 1)
                        sign = d ^ u
                        v.scalar_tensor_tensor(w32[:, n % 4, :], q32[1][:, c % 2, u, :],
                                               float(np.exp(far if sign else -far)), dup[:, sign, :],
                                               ALU.mult, ALU.mult).then_inc(w32_ready, 1)
                    dve.wait_ge(v_psum[1], c + 1)
                    v.tensor_copy(vall[:, TC * c:TC * (c + 1), :], tile4(5)).then_inc(v_ready[1], 1)
                elif j == 6:
                    dve.wait_ge(w32_ready, 4 * c + 4)
                    for n in four:
                        remainder(1, n, w32[:, n % 4, :])
                    norm_max(1, c, [0])
                elif j == 8:
                    for n in four:
                        third_part(1, n)
                    norm_max(1, c, [1])

            def decide(L):
                dve.wait_ge(nrm_read, 2 * NC * L + 2 * NC)
                link(v.tensor_reduce(pm[:, 2:4], nmx[:, L, :, :], AX, ALU.max))
                if L == 1:
                    link(v.memset(pm[:, 1:2], 0.0))
                link(v.scalar_tensor_tensor(pm[:, 0:1], pm[:, 2:3], 1.0 / SCORE_LIMIT ** 2, pm[:, 3:4], ALU.mult, ALU.mult))
                v.tensor_tensor(pm[:, 0:1], pm[:, 0:1], pm[:, 1:2], ALU.max).then_inc(pm_ready, 1)
                dve.wait_ge(pmT_psum, L + 1)
                link(v.tensor_reduce(flagf[0:1, L:L + 1], ps[0:1, 7, 0:P], AX, ALU.max))
                dve.wait_ge(group_ready[L], 1)
                v.tensor_single_scalar(flag[0:1, L:L + 1], flagf[0:1, L:L + 1], 1.0, op=ALU.is_le)\
                 .then_inc(flag_ready, 1)

            def project_step(L, c, j):
                if j == 1:
                    dve.wait_ge(y_psum, NC * L + c + 1)
                    if c:
                        dve.wait_ge(yback_psum, NC * L + c)
                    if L == 0:
                        ins = v.tensor_scalar(yT[:], bank(6 + c % 2), bqk[:, 2:3], mod[:, 0, 2:3], ALU.add, ALU.mult)
                    else:
                        ins = v.tensor_scalar(yT[:], bank(6 + c % 2), mod[:, 1, 2:3], None, ALU.mult)
                    ins.then_inc(yT_ready, 1)
                elif j == 2:
                    dve.wait_ge(yback_psum, NC * L + c + 1)
                    xc = x[:, TC * c:TC * (c + 1), :]
                    v.tensor_tensor(xc, xc, tile4(6 + c % 2), ALU.add).then_inc(x_added, 1)
                    dve.wait_ge(x_added, NC * L + c + 1)

            def fast(L):
                def fix(g, p_, gi):
                    qc, kb = groups[gi]
                    f = fix_of(L, qc, kb)
                    if not f:
                        return
                    for pair in range(2):
                        step = 2 * gi + pair
                        b = 2 * ((NSTEP * p_ + step) % SCORE_BUFS)
                        dve.wait_ge(scores_psum[L], g * NSTEP + (step + 1))
                        s_ = ps[:, b:b + 2, P * f[0]:P * f[1]]
                        if L == 0:
                            a = TC * qc + f[0] - kb + 1
                            other = tb0[:, p_, 2 * pair:2 * pair + 2, P * a:P * (a + f[1] - f[0])]
                        else:
                            other = dtri[:].unsqueeze(1).to_broadcast([P, 2, P])
                        v.tensor_tensor(s_, s_, other, (ALU.add, ALU.mult)[L]).then_inc(fixed[L], 1)

                def copy_out(g, qc):
                    dve.wait_ge(av_done[L], g * NGRP + (AV0 + NT * (qc + 1)))
                    v.tensor_copy(ot[L][:], bank(6 + qc % 2)).then_inc(acc_copied[L], 1)

                def normalise(g, qc):
                    acc = ps[:, 6 + qc % 2, :].rearrange("p (t h w) -> p t h w", t=TC, h=GH)
                    o_ = onorm[:, qc % 2, :, :]
                    dve.wait_ge(accT_psum[L], g * NC + (qc + 1))
                    v.reciprocal(o_, acc[:, :, :, DK]).then_inc(den_ready[L], 1)
                    dve.wait_ge(den_ready[L], g * NC + (qc + 1))
                    dst = ao[:, TC * qc:TC * (qc + 1), bass.ds(g * (GH * DK), GH * DK)]
                    v.tensor_tensor(dst.rearrange("p t (h d) -> p t h d", h=GH), acc[:, :, :, 0:DK],
                                    o_.unsqueeze(3).to_broadcast([P, TC, GH, DK]), ALU.mult).then_inc(acc_free[L], 1)

                def pair_of_groups(i, final):
                    for k in range(2 * NGRP):
                        p_, gi = divmod(k, NGRP)
                        if L == 0 and gi == 0:
                            dve.wait_ge(k_loaded[0][p_], i * KLOADS[0] + KLOADS[0])
                        fix(2 * i + p_, p_, gi)
                        if k > NT and k % NT in (COPY_AT, NORM_AT):
                            p_, qc = divmod(k // NT - 1, NC)
                            (copy_out if k % NT == COPY_AT else normalise)(2 * i + p_, qc)
                        if final and k >= NGRP + NT and k % NT in PROJ_AT:
                            qc = (k - NGRP) // NT - 1
                            project_step(L, qc, PROJ_AT.index(k % NT))
                            if k % NT == PROJ_AT[-1] and qc < NC - 2:
                                ln(L, 1, qc)
                    copy_out(2 * i + 1, NC - 1)
                    normalise(2 * i + 1, NC - 1)

                with dve.Fori(0, NG // 2 - 1) as i:
                    pair_of_groups(i, False)
                pair_of_groups(NG // 2 - 1, True)
                dve.wait_ge(acc_free[L], ACC0 + NC * NG)

            def general(L):
                q_, qt_, row_, pt_, st = ((g_q, g_qt, g_s, g_pt, g_m), (h_q, h_qt, h_s, h_pt, h_st))[L]
                nload = 48 if L == 0 else 32
                ops = 2 if L == 0 else 8
                if L == 1:
                    dve.wait_ge(g_strip_ready[1], 3)
                with dve.Fori(0, H) as h:
                    if L == 0:
                        lo = P * (NT - 2)
                        dve.wait_ge(g_tbT, h + 1)
                        v.tensor_copy(g_strip[:, lo:lo + BAND], ps[:, 4, 0:BAND])
                        v.tensor_copy(g_strip[:, 0:lo], crow[:, 1, bass.ds(h, 1)].to_broadcast([P, lo]))
                        v.tensor_copy(g_strip[:, lo + BAND:], crow[:, 0, bass.ds(h, 1)].to_broadcast([P, lo]))\
                         .then_inc(g_strip_ready[0], 1)
                    with dve.Fori(0, NT) as q:
                        n = h * NT + q
                        done = [0]

                        def then(ins):
                            done[0] += 1
                            ins.then_inc(g_dv[L], 1)
                            dve.wait_ge(g_dv[L], n * ops + done[0])

                        strip = (g_strip, h_strip)[L][:, bass.ds(q * -P + (NT - 1) * P, S)]
                        dve.wait_ge(g_load[L], h * nload + nload)
                        v.tensor_copy(qt_[:], q_[:, bass.ds(q * P, P)]).then_inc(g_q_ready[L], 1)
                        dve.wait_ge(g_sc[L], n + 1)
                        scored = ps[:, 0:4, :].rearrange("p a b -> p (a b)")
                        if L == 0:
                            dve.wait_ge(g_strip_ready[0], h + 1)
                            then(v.tensor_tensor(row_[:], scored, strip, ALU.add))
                        else:
                            then(v.tensor_copy(row_[:], scored))
                            then(v.tensor_tensor(h_m[:], row_[:], row_[:], ALU.is_equal))
                            then(v.tensor_scalar(row_[:], row_[:], CLAMP, -CLAMP, ALU.min, ALU.max))
                            then(v.memset(h_r[:], -CLAMP))
                            v.memset(marks[0:1, 11:12], 0.0)
                            then(v.copy_predicated(h_r[:], h_m[:].bitcast(I32), row_[:]))
                            then(v.tensor_tensor(row_[:], h_r[:], strip, ALU.mult))
                            then(v.tensor_scalar(row_[:], row_[:], CLAMP, -CLAMP, ALU.min, ALU.max))
                        then(v.tensor_reduce(st[:, 0:1], row_[:], AX, ALU.max))
                        v.tensor_scalar(st[:, 1:2], st[:, 0:1], -1.0, None, ALU.mult).then_inc(g_max[L], 1)
                        dve.wait_ge(g_tp[L], n + 1)
                        v.tensor_copy(pt_[:], ps[:, 4:8, :].rearrange("p a b -> p (a b)")).then_inc(g_tc[L], 1)
                        dve.wait_ge(g_av[L], n + 1)
                        v.reciprocal(st[:, 3:4], st[:, 2:3]).then_inc(den_ready[L], 1)
                        dve.wait_ge(den_ready[L], n + 1)
                        v.tensor_scalar(ao[:, bass.ds(q, 1), bass.ds(h * DK, DK)].rearrange("p a d -> p (a d)"),
                                        ps[:, 0, 0:DK], st[:, 3:4], None, ALU.mult).then_inc(g_fin[L], 1)
                dve.wait_ge(g_fin[L], GEN0 + H * NT)
                for c in range(EARLY):
                    for j in range(3):
                        project_step(L, c, j)
                    if c < NC - 2:
                        ln(L, 1, c)

            def attend(L):
                dve.wait_ge(flag_ready, L + 1)
                fv = dve.value_load(flag[0:1, L:L + 1])
                before = self_n[0]
                with dve.If(fv > 0):
                    fast(L)
                after, self_n[0] = self_n[0], before
                with dve.Else():
                    general(L)
                assert self_n[0] == after
                v.memset(marks[0:1, 9 + L:10 + L], 0.0).then_inc(ao_ready, 1)

            def projected(L):
                project_step(L, NC - 1, 1)
                ln(L, 1, NC - 2)
                project_step(L, NC - 1, 2)
                ln(L, 1, NC - 1)

            def top2(L):
                for k in range(NT):
                    v.max(mx8[:, k, :], gts[:, k, :])
                link(v.memset(wgt[:, :, 8:10], 1.0 if L else 1.0 / SH0))
                for k in range(NT):
                    last = v.max_index(ix8[:, k, :], mx8[:, k, :], gts[:, k, :])
                link(last)
                link(v.tensor_copy(ixf[:], ix8[:, :, 0:2]))

            def place(L):
                def wide(a):
                    return a.unsqueeze(2).to_broadcast([P, NT, 8])

                io = iota_e[:].unsqueeze(1).to_broadcast([P, NT, 8])
                v.tensor_tensor(eq1[:], io, wide(ixf[:, :, 0]), ALU.is_equal)
                link(v.tensor_tensor(eq2[:], io, wide(ixf[:, :, 1]), ALU.is_equal))
                v.tensor_tensor(eq1[:], eq1[:], wide(gsm[:, :, 2]), ALU.mult)
                link(v.tensor_tensor(eq2[:], eq2[:], wide(gsm[:, :, 3]), ALU.mult))
                if L == 0:
                    v.tensor_tensor(wgt[:, :, 0:8], eq1[:], eq2[:], ALU.add).then_inc(w_ready, 1)
                    return
                link(v.tensor_tensor(wgt[:, :, 0:8], eq1[:], eq2[:], ALU.add))
                link(v.tensor_copy(wpb[:], wgt[:, :, 0:8]))
                v.tensor_copy(wpart[:, :, 0:8], wpb[:])
                link(v.tensor_tensor(eq1[:], wgt[:, :, 0:8], wpb[:], ALU.subtract))
                link(v.tensor_copy(wpb[:], eq1[:]))
                v.tensor_copy(wpart[:, :, 8:16], wpb[:])
                v.tensor_tensor(wpart[:, :, 16:24], eq1[:], wpb[:], ALU.subtract).then_inc(w_ready, 1)

            def copy_weights(L, n, dst):
                for c in range(NC):
                    dve.wait_ge(wT_psum, NC * L + c + 1)
                    if L == 1:
                        v.tensor_copy(wTb[:, CW * c:CW * (c + 1)], ps[0:n, 6 + c % 2, :])
                    v.tensor_copy(dst[:, CW * c:CW * (c + 1)], ps[0:n, 6 + c % 2, :]).then_inc(wT_ready, 1)

            link(v.memset(pm[:], 0.0))
            dve.wait_ge(silu_exp, 1)
            link(v.tensor_scalar(silu[:], cexp[:], 1.0, None, ALU.add))
            link(v.reciprocal(cexp[:], silu[:]))
            link(v.tensor_tensor(silu[:], cexp[:], ccol[:], ALU.mult))
            v.tensor_copy(silub[:], silu[:].unsqueeze(2).to_broadcast([P, 2, P])).then_inc(silu_done, 1)
            dve.wait_ge(consts, 1)
            dve.wait_ge(decays, 2)
            v.tensor_scalar(dtri[:], dtri[:], 0.0, None, ALU.min).then_inc(decays, 1)
            dve.wait_ge(ld_x[0], 16)
            ln(0, 0, 0)
            dve.wait_ge(mod_psum, 1)
            link(v.tensor_copy(mod[:], ps[:, 7, 0:12].rearrange("p (a b) -> p a b", a=2)))
            link(v.tensor_scalar(mod[:, :, 1:5:3], mod[:, :, 1:5:3], 1.0, None, ALU.add))
            link(v.tensor_copy(gbrow[:], ps[:, 6, 0:2 * D].rearrange("p (a b) -> p a b", a=2)))
            dve.wait_ge(ld_att0, 16 * 5)
            v.tensor_scalar(bqs[:], bqk[:, 0:1], SCALE[0], None, ALU.mult).then_inc(mod_done, 1)
            dve.wait_ge(ld_x[1], 16)
            ln(0, 0, 1)
            def bias_rows():
                link(v.tensor_scalar(rp[:, 1:2], rp[:, 0:1], float(NT), None, ALU.is_ge))
                link(v.tensor_scalar(rp[:, 2:3], rp[:, 0:1], 2.0 * NT, None, ALU.is_ge))
                link(v.scalar_tensor_tensor(rp[:, 3:4], rp[:, 1:2], -float(NT), rp[:, 0:1], ALU.mult, ALU.add))
                link(v.scalar_tensor_tensor(rp[:, 3:4], rp[:, 2:3], -float(NT), rp[:, 3:4], ALU.mult, ALU.add))
                link(v.tensor_scalar(rp[:, 4:6], rp[:, 1:3], -1.0, None, ALU.mult))
                v.tensor_scalar(mhi[:], kbi[:], rp[:, 3:4], -2.0, ALU.subtract, ALU.is_le)
                v.tensor_scalar(mlo[:], kbi[:], rp[:, 3:4], 2.0, ALU.subtract, ALU.is_ge)
                link(v.tensor_scalar(oneh[:], kbi[:], rp[:, 3:4], 0.0, ALU.subtract, ALU.is_equal))
                v.tensor_copy(onehw[:].rearrange("p (k n) -> p k n", n=P),
                              oneh[:].unsqueeze(2).to_broadcast([BIAS_ROWS, NT, P])).then_inc(onehw_ready, 1)
                cr = crow[0:BIAS_ROWS]
                link(v.tensor_copy(cpa[:], cr))
                link(v.scalar_tensor_tensor(cpb[:], cpa[:], rp[:, 4:5], cr, ALU.mult, ALU.add))
                link(v.tensor_copy(cpc[:], cpb[:]))
                link(v.scalar_tensor_tensor(cpd[:], cpc[:], rp[:, 5:6], cpb[:], ALU.mult, ALU.add))

                def over_heads(a):
                    return a.unsqueeze(1).to_broadcast([BIAS_ROWS, H, NT])

                def over_tiles(a):
                    return a.unsqueeze(2).to_broadcast([BIAS_ROWS, H, NT])

                v.tensor_tensor(ktab[:], over_heads(mhi[:]), over_tiles(cpd[:, 1, :]), ALU.mult)
                link(v.tensor_tensor(ktab2[:], over_heads(mlo[:]), over_tiles(cpd[:, 0, :]), ALU.mult))
                v.tensor_tensor(ktab[:], ktab[:], ktab2[:], ALU.add).then_inc(ktab_ready, 1)

            def gates_and_bias():
                v.tensor_scalar(gatesgn[:], mod[:, :, 2], 0.0, 2.0, ALU.is_ge, ALU.mult)
                link(v.scalar_tensor_tensor(gateabs[:], mod[:, :, 2], -1.0, mod[:, :, 2], ALU.mult, ALU.max))
                link(v.tensor_scalar(gateabs[:], gateabs[:], 0.25, None, ALU.max))
                link(v.scalar_tensor_tensor(mod[:, :, 2], gatesgn[:], -1.0, gateabs[:], ALU.add, ALU.mult))
                link(v.tensor_scalar(gbsgn[:], gbrow[:], 0.0, 2.0, ALU.is_ge, ALU.mult))
                link(v.scalar_tensor_tensor(gbrow[:], gbrow[:], -1.0, gbrow[:], ALU.mult, ALU.max))
                link(v.tensor_scalar(gbrow[:], gbrow[:], 0.25, None, ALU.max))
                v.scalar_tensor_tensor(gbrow[:], gbsgn[:], -1.0, gbrow[:], ALU.add, ALU.mult).then_inc(gates_ready, 1)
                dve.wait_ge(relT_psum, 1)
                link(v.tensor_copy(relv[:, P - 1:P + 2 * REL], ps[0:H, 5, 0:2 * REL + 1]))
                v.tensor_copy(relv[:, 0:P - 1], relv[:, P - 1:P].to_broadcast([H, P - 1]))
                v.tensor_copy(relv[:, P + 2 * REL:], relv[:, P + 2 * REL - 1:P + 2 * REL].to_broadcast([H, TROW - P - 2 * REL]))\
                 .then_inc(relv_ready, 1)
                link(v.tensor_tensor(relsq[:], relf[:], relf[:], ALU.mult))
                link(v.tensor_reduce(flagr[:], relsq[:], AX, ALU.max))
                link(v.tensor_scalar(pm[0:H, 1:2], flagr[:], 1.0 / BIAS_LIMIT ** 2, None, ALU.mult))
                bias_rows()

            for c in range(NC):
                project0(c, gates_and_bias)
            decide(0)
            attend(0)
            projected(0)

            link(v.tensor_scalar(iota_p[:, 1:2], iota_p[:, 0:1], float(E1), -float(E1), ALU.is_ge, ALU.mult))
            link(v.tensor_scalar(iota_p[:, 2:3], iota_p[:, 0:1], 2.0 * E1, -float(E1), ALU.is_ge, ALU.mult))
            link(v.tensor_tensor(iota_p[:, 1:2], iota_p[:, 1:2], iota_p[:, 2:3], ALU.add))
            link(v.tensor_tensor(iota_p[:, 3:4], iota_p[:, 0:1], iota_p[:, 1:2], ALU.add))
            link(v.tensor_scalar(sel8[:], iota_e[0:PARTS * E1, :], iota_p[:, 3:4], None, ALU.is_equal))
            v.tensor_copy(sel1[:], sel8[:].unsqueeze(2).to_broadcast([PARTS * E1, E1, P])).then_inc(sel_ready, 1)

            dve.wait_ge(gate_psum, NC)
            link(v.tensor_tensor(gts[:], ps[:, 7, 0:NT * E0].rearrange("p (a b) -> p a b", b=E0),
                                 rb0[:].unsqueeze(1).to_broadcast([P, NT, E0]), ALU.add))
            top2(0)
            v.tensor_tensor(gsm[:, :, 0], mx8[:, :, 1], mx8[:, :, 0], ALU.subtract).then_inc(gate_d, 1)
            dve.wait_ge(gate_e, 1)
            link(v.tensor_scalar(gsm[:, :, 0], gsm[:, :, 1], 1.0, None, ALU.add))
            link(v.reciprocal(gsm[:, :, 2], gsm[:, :, 0]))
            link(v.tensor_tensor(gsm[:, :, 3], gsm[:, :, 1], gsm[:, :, 2], ALU.mult))
            place(0)
            copy_weights(0, E0 + SH0, wT0)
            for c in range(NC):
                for j in range(1, len(order0)):
                    n = len(order0) * c + j
                    y = y_index(n)
                    dve.wait_ge(y0_psum, y + 1)
                    if y:
                        dve.wait_ge(y0_read, y)
                    if j == 1:
                        xc = x[:, TC * c:TC * (c + 1), :]
                        last = v.tensor_tensor(xc, xc, tile4(3 + y % 2), ALU.add)
                    else:
                        e = order0[j]
                        for k in range(TC):
                            xt = x[:, TC * c + k, :]
                            last = v.scalar_tensor_tensor(xt, ps[:, 3 + y % 2, P * k:P * (k + 1)],
                                                          wgt[:, TC * c + k, e:e + 1], xt, ALU.mult, ALU.add)
                    last.then_inc(y0_read, 1)
                    if c:
                        layer1_step(j, c - 1)
                dve.wait_ge(y0_read, (E0 + 1) * (c + 1))
                layer1_step(-1, c)
            for j in range(len(order0)):
                layer1_step(j, NC - 1)
            decide(1)
            attend(1)
            projected(1)

            link(v.memset(contT[M1:, :], 1.0))
            dve.wait_ge(ld_ffn1, 16 * 19)
            for c in range(NC):
                dve.wait_ge(cont_psum, c + 1)
                v.tensor_scalar(contT[0:M1, CW * c:CW * (c + 1)], ps[0:M1, 4 + c % 2, :], bs2c[:, 0:1], None, ALU.add)\
                 .then_inc(cont_ready, 1)
            dve.wait_ge(gate_psum, NC + NC)
            logits = ps[:, 7, 0:NT * E1].rearrange("p (a b) -> p a b", b=E1)

            def over(a):
                return a.unsqueeze(2).to_broadcast([P, NT, E1])

            link(v.tensor_reduce(gsm[:, :, 0], logits, AX, ALU.max))
            v.tensor_tensor(gts[:], logits, over(gsm[:, :, 0]), ALU.subtract).then_inc(gate_d, 1)
            dve.wait_ge(gate_e, 1 + 1)
            link(v.tensor_reduce(gsm[:, :, 1], gts[:], AX, ALU.add))
            link(v.reciprocal(gsm[:, :, 0], gsm[:, :, 1]))
            link(v.tensor_tensor(gts[:], gts[:], over(gsm[:, :, 0]), ALU.mult))
            top2(1)
            link(v.tensor_tensor(gsm[:, :, 0], mx8[:, :, 0], mx8[:, :, 1], ALU.add))
            link(v.reciprocal(gsm[:, :, 1], gsm[:, :, 0]))
            v.tensor_tensor(gsm[:, :, 2], mx8[:, :, 0], gsm[:, :, 1], ALU.mult)
            link(v.tensor_tensor(gsm[:, :, 3], mx8[:, :, 1], gsm[:, :, 1], ALU.mult))
            place(1)
            copy_weights(1, PARTS * E1, wT1)

            v.tensor_tensor(lngr[:], lngr[:], gbrow[:, 1, :], ALU.mult)
            link(v.tensor_tensor(lnbr[:], lnbr[:], gbrow[:, 1, :], ALU.mult))
            link(v.tensor_tensor(x[:], x[:], lnbr[:].unsqueeze(1).to_broadcast([P, NT, D]), ALU.add))

            def weigh1(n):
                dve.wait_ge(relu_done, n + 1)
                dve.wait_ge(wb_psum, n + 1)
                if n >= 4:
                    dve.wait_ge(yy_psum, (n - 4) // 2 + 1)
                v.tensor_tensor(hbuf1[:, n % 4, :], rbuf1[:, n % E1, :], bank(2 + n % 2), ALU.mult)\
                 .then_inc(hh_act, 1)

            def finish1(c, step):
                d_ = dec[:, c % 2, :, :]
                if step == 0:
                    dve.wait_ge(dec_psum, c + 1)
                    v.tensor_tensor(d_, tile4(6), bdec[:].unsqueeze(1).to_broadcast([P, TC, D]), ALU.add)\
                     .then_inc(dec_ready, 1)
                elif step == 1:
                    dve.wait_ge(dec_ready, c + 1)
                    moments(lambda k: dec[:, c % 2, k, :], c)
                    rsqrt_guess(meanvar[:, TC * c:TC * (c + 1), 1])
                elif step in (2, 3, 4):
                    rsqrt_newton()
                elif step == 5:
                    for k in range(TC):
                        last = v.tensor_scalar(dec[:, c % 2, k, :], dec[:, c % 2, k, :], meanvar[:, TC * c + k, 0:1],
                                               rs_y[:, k:k + 1], ALU.subtract, ALU.mult)
                    link(last)
                elif step == 6:
                    link(v.tensor_tensor(d_, d_, lngr[:].unsqueeze(1).to_broadcast([P, TC, D]), ALU.mult))
                    v.tensor_tensor(fo[:, c, :, :], d_, x[:, TC * c:TC * (c + 1), :], ALU.add).then_inc(fo_ready, 1)

            for n in range(NC * E1):
                weigh1(n)
                c, e = divmod(n + 1, E1)
                if c >= 2:
                    finish1(c - 2, e)
            for step in range(1, 7):
                finish1(NC - 2, step)
            for step in range(7):
                finish1(NC - 1, step)


def kernel(**inputs):
    import concourse.bacc as bacc
    from concourse.bass_utils import run_bass_kernel_spmd

    nc = bacc.Bacc("TRN2", target_bir_lowering=False, num_devices=1)
    arrays, args = {}, {}
    for name, a in inputs.items():
        a = np.ascontiguousarray(a)
        arrays[f"in_{name}_dram"] = a
        args[name] = nc.dram_tensor(f"in_{name}_dram", a.shape, mybir.dt.from_np(a.dtype), kind="ExternalInput").ap()
    out = nc.dram_tensor("out_0_dram", (1, S, D), F32, kind="ExternalOutput").ap()
    adaln_two_layers(nc, args, out)
    r = run_bass_kernel_spmd(nc, [arrays], core_ids=[0])
    return r.results[0]["out_0_dram"]
```
